# Optimizing a Trainium2 kernel written in Bass

```python
import numpy as np
import jax
import jax.numpy as jnp

def _softmax(x, axis=-1):
    return jax.nn.softmax(x, axis=axis)

def _gelu(x):
    return jax.nn.gelu(x, approximate=True)

def _silu(x):
    return jax.nn.silu(x)

def _sigmoid(x):
    return jax.nn.sigmoid(x)

def _layernorm(x, axis=-1, eps=1e-05):
    m = jnp.mean(x, axis=axis, keepdims=True)
    v = jnp.var(x, axis=axis, keepdims=True)
    return (x - m) / jnp.sqrt(v + eps)

def _scatter_add(tgt, idx, src, axis=0):
    return tgt.at[idx].add(src)

def _segment_sum(src, seg, n):
    return jax.ops.segment_sum(src, seg, n)
kernel_name = 'mk_adj_preln_d4_adj_r2_151433'

def setup_inputs(seed: int=0):
    np.random.seed(seed)
    _w = jnp.asarray

    def _rec_inputs():
        import jax
        import jax.numpy as jnp
        _gk = jax.random.key(seed)
        x = -0.0004039 + 1 * jax.random.normal(jax.random.fold_in(_gk, 1), (128, 64, 384), jnp.float32)
        _w = (1.0 + jnp.arange(64, dtype=jnp.float32)) ** (-0.5)
        _w = _w / _w.mean()
        _pij = jnp.clip(0.125 * _w[:, None] * _w[None, :], 0.0, 1.0)
        _a = jax.random.uniform(jax.random.fold_in(_gk, 2), (128, 64, 64)) < _pij
        _af = _a.astype(jnp.float32)
        adj = _af
        return (x, adj)
    x, adj = _rec_inputs()

    def _L0_gnn_setup():
        import jax, jax.numpy as jnp
        import numpy as np
        B, S, H, L = (32, 256, 384, 2)

        def _layer_norm(z, a, b, eps=0.001):
            mu = jnp.mean(z, axis=-1, keepdims=True)
            sigma = jnp.std(z, axis=-1, keepdims=True, ddof=1)
            return (z - mu) / (sigma + eps) * a + b
        key = jax.random.key(seed)
        ks = jax.random.split(key, 6)
        hidden_state = jax.random.normal(ks[0], (B, S, H), dtype=jnp.float32)
        adjacency_matrix = (jax.random.uniform(ks[1], (B, S, S)) < 0.2).astype(jnp.float32)
        W_left = 0.05 * jax.random.normal(ks[2], (L, H, H), dtype=jnp.float32)
        W_right = 0.05 * jax.random.normal(ks[3], (L, H, H), dtype=jnp.float32)
        W_lin = 0.05 * jax.random.normal(ks[4], (L, H, H), dtype=jnp.float32)
        b_lin = jnp.zeros((L, H), dtype=jnp.float32)
        ln_a = jnp.ones((L, H), dtype=jnp.float32)
        ln_b = jnp.zeros((L, H), dtype=jnp.float32)
        return {'hidden_state': hidden_state, 'adjacency_matrix': adjacency_matrix, 'W_left': W_left, 'W_right': W_right, 'W_lin': W_lin, 'b_lin': b_lin, 'ln_a': ln_a, 'ln_b': ln_b}
    _L0_gnn_all = _L0_gnn_setup()
    _L0_gnn_in = {k: v for k, v in _L0_gnn_all.items() if k in ('W_left', 'W_right', 'W_lin', 'b_lin', 'ln_a', 'ln_b')}
    del _L0_gnn_all

    def _L1_gnn_setup():
        import jax, jax.numpy as jnp
        import numpy as np
        NUM_HEADS = 12
        HIDDEN = 384
        HEAD = HIDDEN // NUM_HEADS
        B, N = (16, 256)
        key = jax.random.key(seed)
        ks = jax.random.split(key, 9)
        s = 0.02
        return {'x': jax.random.normal(ks[0], (B, N, HIDDEN), jnp.float32), 'spatial_encoding': jax.random.normal(ks[1], (B, N, N), jnp.float32), 'edge_encoding': jax.random.normal(ks[2], (B, N, N), jnp.float32), 'Wq': jax.random.normal(ks[3], (HIDDEN, HIDDEN), jnp.float32) * s, 'Wk': jax.random.normal(ks[4], (HIDDEN, HIDDEN), jnp.float32) * s, 'Wv': jax.random.normal(ks[5], (HIDDEN, HIDDEN), jnp.float32) * s, 'bv': jax.random.normal(ks[6], (HIDDEN,), jnp.float32) * s, 'Wo': jax.random.normal(ks[7], (HIDDEN, HIDDEN), jnp.float32) * s, 'bo': jax.random.normal(ks[8], (HIDDEN,), jnp.float32) * s}
    _L1_gnn_all = _L1_gnn_setup()
    _L1_gnn_in = {k: v for k, v in _L1_gnn_all.items() if k in ('Wq', 'Wk', 'Wv', 'bv', 'Wo', 'bo')}
    del _L1_gnn_all

    def _L2_gnn_setup():
        import jax, jax.numpy as jnp
        import numpy as np
        NUM_HEADS = 12
        HIDDEN = 384
        HEAD = HIDDEN // NUM_HEADS
        SCALE = HIDDEN ** (-0.5)
        key = jax.random.key(seed)
        ks = jax.random.split(key, 8)
        B, N = (16, 256)
        std = HIDDEN ** (-0.5)
        return {'x': jax.random.normal(ks[0], (B, N, HIDDEN), dtype=jnp.float32), 'encoding_bias': jax.random.normal(ks[1], (B, N, N), dtype=jnp.float32), 'Wq': jax.random.normal(ks[2], (HIDDEN, HIDDEN), dtype=jnp.float32) * std, 'Wk': jax.random.normal(ks[3], (HIDDEN, HIDDEN), dtype=jnp.float32) * std, 'Wv': jax.random.normal(ks[4], (HIDDEN, HIDDEN), dtype=jnp.float32) * std, 'bv': jax.random.normal(ks[5], (HIDDEN,), dtype=jnp.float32) * 0.01, 'Wo': jax.random.normal(ks[6], (HIDDEN, HIDDEN), dtype=jnp.float32) * std, 'bo': jax.random.normal(ks[7], (HIDDEN,), dtype=jnp.float32) * 0.01}
    _L2_gnn_all = _L2_gnn_setup()
    _L2_gnn_in = {k: v for k, v in _L2_gnn_all.items() if k in ('Wq', 'Wk', 'Wv', 'bv', 'Wo', 'bo')}
    del _L2_gnn_all

    def _L3_gnn_setup():
        import jax, jax.numpy as jnp
        import numpy as np
        LN_EPS = 1e-12

        def _digcn_forward(hidden_state, adjacency_matrix, Wl, bl, Ws, bs, Wr, br, ln_w, ln_b):
            B, S, D = hidden_state.shape
            temper = jnp.asarray(D, jnp.float32) ** 0.5
            i = jnp.arange(S)
            upper = (i[None, :] > i[:, None]).astype(hidden_state.dtype)
            lower = (i[None, :] < i[:, None]).astype(hidden_state.dtype)

            def layer(h, params):
                wl, b_l, ws, b_s, wr, b_r, g, beta = params
                u = jnp.einsum('bid,bjd->bij', h, h) / temper
                a = jax.nn.softmax(u, axis=-1)
                delta = a * adjacency_matrix
                attn = delta / (jnp.sum(delta, axis=-1, keepdims=True) + 1e-10)
                hl = h @ wl.T + b_l
                hs = h @ ws.T + b_s
                hr = h @ wr.T + b_r
                diag_a = jnp.diagonal(attn, axis1=1, axis2=2)
                ctx = jnp.einsum('bij,bjd->bid', attn * upper, hl) + diag_a[..., None] * hs + jnp.einsum('bij,bjd->bid', attn * lower, hr)
                mean = ctx.mean(-1, keepdims=True)
                var = ctx.var(-1, keepdims=True)
                o = (ctx - mean) / jnp.sqrt(var + LN_EPS) * g + beta
                return (jax.nn.relu(o), None)
            out, _ = jax.lax.scan(layer, hidden_state, (Wl, bl, Ws, bs, Wr, br, ln_w, ln_b))
            return out
        key = jax.random.key(seed)
        ks = jax.random.split(key, 6)
        B, S, D, L = (8, 512, 384, 2)
        scale = (1.0 / D) ** 0.5
        hidden_state = jax.random.normal(ks[0], (B, S, D), jnp.float32)
        adjacency_matrix = (jax.random.uniform(ks[1], (B, S, S)) < 0.05).astype(jnp.float32)
        Wl = jax.random.normal(ks[2], (L, D, D), jnp.float32) * scale
        Ws = jax.random.normal(ks[3], (L, D, D), jnp.float32) * scale
        Wr = jax.random.normal(ks[4], (L, D, D), jnp.float32) * scale
        bl = jnp.zeros((L, D), jnp.float32)
        bs = jnp.zeros((L, D), jnp.float32)
        br = jnp.zeros((L, D), jnp.float32)
        ln_w = jnp.ones((L, D), jnp.float32)
        ln_b = jnp.zeros((L, D), jnp.float32)
        return dict(hidden_state=hidden_state, adjacency_matrix=adjacency_matrix, Wl=Wl, bl=bl, Ws=Ws, bs=bs, Wr=Wr, br=br, ln_w=ln_w, ln_b=ln_b)
    _L3_gnn_all = _L3_gnn_setup()
    _L3_gnn_in = {k: v for k, v in _L3_gnn_all.items() if k in ('Wl', 'bl', 'Ws', 'bs', 'Wr', 'br', 'ln_w', 'ln_b')}
    del _L3_gnn_all
    return {'x': x, 'adj': adj, 'L0_gnn_W_left': _L0_gnn_in['W_left'], 'L0_gnn_W_right': _L0_gnn_in['W_right'], 'L0_gnn_W_lin': _L0_gnn_in['W_lin'], 'L0_gnn_b_lin': _L0_gnn_in['b_lin'], 'L0_gnn_ln_a': _L0_gnn_in['ln_a'], 'L0_gnn_ln_b': _L0_gnn_in['ln_b'], 'L1_gnn_Wq': _L1_gnn_in['Wq'], 'L1_gnn_Wk': _L1_gnn_in['Wk'], 'L1_gnn_Wv': _L1_gnn_in['Wv'], 'L1_gnn_bv': _L1_gnn_in['bv'], 'L1_gnn_Wo': _L1_gnn_in['Wo'], 'L1_gnn_bo': _L1_gnn_in['bo'], 'L2_gnn_Wq': _L2_gnn_in['Wq'], 'L2_gnn_Wk': _L2_gnn_in['Wk'], 'L2_gnn_Wv': _L2_gnn_in['Wv'], 'L2_gnn_bv': _L2_gnn_in['bv'], 'L2_gnn_Wo': _L2_gnn_in['Wo'], 'L2_gnn_bo': _L2_gnn_in['bo'], 'L3_gnn_Wl': _L3_gnn_in['Wl'], 'L3_gnn_bl': _L3_gnn_in['bl'], 'L3_gnn_Ws': _L3_gnn_in['Ws'], 'L3_gnn_bs': _L3_gnn_in['bs'], 'L3_gnn_Wr': _L3_gnn_in['Wr'], 'L3_gnn_br': _L3_gnn_in['br'], 'L3_gnn_ln_w': _L3_gnn_in['ln_w'], 'L3_gnn_ln_b': _L3_gnn_in['ln_b']}

def reference(x, adj, L0_gnn_W_left, L0_gnn_W_right, L0_gnn_W_lin, L0_gnn_b_lin, L0_gnn_ln_a, L0_gnn_ln_b, L1_gnn_Wq, L1_gnn_Wk, L1_gnn_Wv, L1_gnn_bv, L1_gnn_Wo, L1_gnn_bo, L2_gnn_Wq, L2_gnn_Wk, L2_gnn_Wv, L2_gnn_bv, L2_gnn_Wo, L2_gnn_bo, L3_gnn_Wl, L3_gnn_bl, L3_gnn_Ws, L3_gnn_bs, L3_gnn_Wr, L3_gnn_br, L3_gnn_ln_w, L3_gnn_ln_b):
    import jax
    import jax.numpy as jnp

    def _L0_gnn_ref(hidden_state, adjacency_matrix, W_left, W_right, W_lin, b_lin, ln_a, ln_b):
        import jax, jax.numpy as jnp
        import numpy as np
        B, S, H, L = (32, 256, 384, 2)

        def _layer_norm(z, a, b, eps=0.001):
            mu = jnp.mean(z, axis=-1, keepdims=True)
            sigma = jnp.std(z, axis=-1, keepdims=True, ddof=1)
            return (z - mu) / (sigma + eps) * a + b
        temper = float(np.sqrt(H))
        adj = adjacency_matrix
        adj_tri = jnp.triu(adj, k=1)
        diag_mask = jnp.triu(adj, k=0) - adj_tri
        h = hidden_state
        for l in range(L):
            m_left = jnp.einsum('bsh,oh->bso', h, W_left[l])
            m_right = jnp.einsum('bsh,oh->bso', h, W_right[l])
            u_left = jnp.einsum('bih,bjh->bij', h, m_left) / temper
            u_right = jnp.einsum('bih,bjh->bij', h, m_right) / temper
            u = u_left * adj_tri + u_left * diag_mask + u_right * jnp.swapaxes(adj_tri, 1, 2)
            delta_exp_u = jnp.exp(u) * adj
            attention = delta_exp_u / (jnp.sum(delta_exp_u, axis=2, keepdims=True) + 1e-10)
            h_lin = jnp.einsum('bsh,oh->bso', h, W_lin[l]) + b_lin[l]
            ctx = jnp.matmul(attention, h_lin)
            h = jax.nn.relu(_layer_norm(ctx, ln_a[l], ln_b[l]))
        return h

    def _L1_gnn_ref(x, spatial_encoding, edge_encoding, Wq, Wk, Wv, bv, Wo, bo):
        import jax, jax.numpy as jnp
        import numpy as np
        NUM_HEADS = 12
        HIDDEN = 384
        HEAD = HIDDEN // NUM_HEADS
        B, N = (16, 256)
        b, n, h = x.shape
        scale = jnp.asarray(HIDDEN, x.dtype) ** (-0.5)
        q = (x @ Wq.T).reshape(b, n, NUM_HEADS, HEAD)
        k = (x @ Wk.T).reshape(b, n, NUM_HEADS, HEAD)
        v = (x @ Wv.T + bv).reshape(b, n, NUM_HEADS, HEAD)
        bias = (spatial_encoding + edge_encoding)[:, None]
        scores = jnp.einsum('bqhd,bkhd->bhqk', q, k) * scale + bias
        row_nonzero = jnp.any(scores != 0, axis=-1, keepdims=True)
        scores = jnp.where(row_nonzero, scores, -jnp.inf)
        p = jax.nn.softmax(scores, axis=-1)
        p = jnp.nan_to_num(p)
        out = jnp.einsum('bhqk,bkhd->bqhd', p, v).reshape(b, n, h)
        return out @ Wo.T + bo

    def _L2_gnn_ref(x, encoding_bias, Wq, Wk, Wv, bv, Wo, bo):
        import jax, jax.numpy as jnp
        import numpy as np
        NUM_HEADS = 12
        HIDDEN = 384
        HEAD = HIDDEN // NUM_HEADS
        SCALE = HIDDEN ** (-0.5)
        B, N, _ = x.shape
        q = (x @ Wq.T).reshape(B, N, NUM_HEADS, HEAD)
        k = (x @ Wk.T).reshape(B, N, NUM_HEADS, HEAD)
        v = (x @ Wv.T + bv).reshape(B, N, NUM_HEADS, HEAD)
        a = jnp.einsum('bnhd,bmhd->bhnm', q, k) * SCALE + encoding_bias[:, None, :, :]
        pad_mask = jnp.all(a == 0, axis=-1)
        a = jnp.where(pad_mask[..., None], -jnp.inf, a)
        a = jax.nn.softmax(a, axis=-1)
        a = jnp.nan_to_num(a)
        o = jnp.einsum('bhnm,bmhd->bnhd', a, v).reshape(B, N, HIDDEN)
        return o @ Wo.T + bo

    def _L3_gnn_ref(hidden_state, adjacency_matrix, Wl, bl, Ws, bs, Wr, br, ln_w, ln_b):
        import jax, jax.numpy as jnp
        import numpy as np
        LN_EPS = 1e-12

        def _digcn_forward(hidden_state, adjacency_matrix, Wl, bl, Ws, bs, Wr, br, ln_w, ln_b):
            B, S, D = hidden_state.shape
            temper = jnp.asarray(D, jnp.float32) ** 0.5
            i = jnp.arange(S)
            upper = (i[None, :] > i[:, None]).astype(hidden_state.dtype)
            lower = (i[None, :] < i[:, None]).astype(hidden_state.dtype)

            def layer(h, params):
                wl, b_l, ws, b_s, wr, b_r, g, beta = params
                u = jnp.einsum('bid,bjd->bij', h, h) / temper
                a = jax.nn.softmax(u, axis=-1)
                delta = a * adjacency_matrix
                attn = delta / (jnp.sum(delta, axis=-1, keepdims=True) + 1e-10)
                hl = h @ wl.T + b_l
                hs = h @ ws.T + b_s
                hr = h @ wr.T + b_r
                diag_a = jnp.diagonal(attn, axis1=1, axis2=2)
                ctx = jnp.einsum('bij,bjd->bid', attn * upper, hl) + diag_a[..., None] * hs + jnp.einsum('bij,bjd->bid', attn * lower, hr)
                mean = ctx.mean(-1, keepdims=True)
                var = ctx.var(-1, keepdims=True)
                o = (ctx - mean) / jnp.sqrt(var + LN_EPS) * g + beta
                return (jax.nn.relu(o), None)
            out, _ = jax.lax.scan(layer, hidden_state, (Wl, bl, Ws, bs, Wr, br, ln_w, ln_b))
            return out
        return _digcn_forward(hidden_state, adjacency_matrix, Wl, bl, Ws, bs, Wr, br, ln_w, ln_b)
    h = jnp.maximum(_layernorm(x, axis=-1), 0.0)
    x = x + _L0_gnn_ref(h, adj, L0_gnn_W_left, L0_gnn_W_right, L0_gnn_W_lin, L0_gnn_b_lin, L0_gnn_ln_a, L0_gnn_ln_b)
    h = jnp.maximum(_layernorm(x, axis=-1), 0.0)
    x = x + _L1_gnn_ref(h, adj, adj, L1_gnn_Wq, L1_gnn_Wk, L1_gnn_Wv, L1_gnn_bv, L1_gnn_Wo, L1_gnn_bo)
    h = jnp.maximum(_layernorm(x, axis=-1), 0.0)
    x = x + _L2_gnn_ref(h, adj, L2_gnn_Wq, L2_gnn_Wk, L2_gnn_Wv, L2_gnn_bv, L2_gnn_Wo, L2_gnn_bo)
    h = jnp.maximum(_layernorm(x, axis=-1), 0.0)
    x = x + _L3_gnn_ref(h, adj, L3_gnn_Wl, L3_gnn_bl, L3_gnn_Ws, L3_gnn_bs, L3_gnn_Wr, L3_gnn_br, L3_gnn_ln_w, L3_gnn_ln_b)
    return x

_drawn_inputs = setup_inputs


def setup_inputs(seed=0):
    import zlib

    import numpy as np

    out = dict(_drawn_inputs(seed))
    spreads = {'L0_gnn_b_lin': (0.0, 0.1),
     'L0_gnn_ln_a': (1.0, 0.2),
     'L0_gnn_ln_b': (0.0, 0.1),
     'L3_gnn_bl': (0.0, 0.1),
     'L3_gnn_bs': (0.0, 0.275),
     'L3_gnn_br': (0.0, 0.1),
     'L3_gnn_ln_w': (1.0, 0.2),
     'L3_gnn_ln_b': (0.0, 0.1)}
    factors = {'L0_gnn_W_right': 3.428,
     'L1_gnn_Wq': 28.985,
     'L1_gnn_Wk': 29.193,
     'L1_gnn_bv': 8.0,
     'L1_gnn_bo': 4.215,
     'L2_gnn_Wq': 8.0,
     'L2_gnn_Wk': 8.0,
     'L2_gnn_bv': 7.921,
     'L2_gnn_bo': 8.0}
    for name, (base, spread) in spreads.items():
        noise = np.random.default_rng([zlib.crc32(name.encode()), seed]).standard_normal(out[name].shape)
        drawn = base * np.exp(spread * noise) if base else spread * noise
        out[name] = jnp.asarray(drawn.astype(out[name].dtype))
    for name, factor in factors.items():
        out[name] = (out[name] * factor).astype(out[name].dtype)
    return out
```

```python
from contextlib import ExitStack

import numpy as np

import concourse.bass as bass
from concourse import mybir

GRAPHS, NODES, FEAT = 128, 64, 384
P = 128
C = FEAT // P
T = 2
TOK = T * P
STREAMS = 2
GROUPS = GRAPHS * NODES // TOK
ITER = GROUPS // STREAMS
HEADS = 12
HD = FEAT // HEADS
HT = HEADS * T
HPC = P // HD
BANK = 512
MATS = 6
LN_EPS = 1e-5
LAG_GCN0, LAG_ATT, LAG_GCN3 = 12, 7, 12

ALU = mybir.AluOpType
ACT = mybir.ActivationFunctionType
F32 = mybir.dt.float32
F32R = mybir.dt.float32r
AX = mybir.AxisListType


class Count:

    def __init__(self, names):
        self.names = names
        self.place = {name: k + 1 for k, name in enumerate(names)}

    def __call__(self, name, i):
        return i * len(self.names) + self.place[name]

    def all_before(self, i):
        return i * len(self.names)


def stage_order(stages, lag):
    n = len(stages)
    for j in range(n):
        yield stages[j], 0, False
        yield stages[(j - lag) % n], 1, j < lag


def run_stages(eng, order, todo):
    order = [(todo[stage], s, late) for stage, s, late in order if stage in todo]
    for stage, s, late in order:
        if not late:
            stage(s, 0)
    with eng.Fori(1, ITER) as i:
        for stage, s, late in order:
            stage(s, i - 1 if late else i)
    for stage, s, late in order:
        if late:
            stage(s, ITER - 1)


def head_tile(t, h):
    return (h % HPC) * T * C + t * C + h // HPC


def exact_product(nc, out, terms):
    for k, (lhs_hi, lhs_lo, rhs_hi, rhs_lo) in enumerate(terms):
        nc.tensor.matmul(out, lhs_hi, rhs_hi, start=(k == 0), stop=False)
        nc.tensor.matmul(out, lhs_hi, rhs_lo, start=False, stop=False)
        last = nc.tensor.matmul(out, lhs_lo, rhs_hi, start=False, stop=(k == len(terms) - 1))
    return last


class Shared:
    pass


def weight_split(nc, g, phase, n_mats, act, dve):
    if act is not None:
        act.wait_ge(g.weights_in[phase], 16)
        for m in range(n_mats):
            nc.scalar.activation(g.w_hi[:, m], g.w_raw[:, m], ACT.Copy).then_inc(g.hi_split[phase], 1)
    if dve is not None:
        dve.wait_ge(g.weights_in[phase], 16)
        for m in range(n_mats):
            dve.wait_ge(g.hi_split[phase], m + 1)
            nc.vector.tensor_tensor(g.w_lo[:, m], g.w_raw[:, m], g.w_hi[:, m].bitcast(F32),
                                    ALU.subtract).then_inc(g.lo_split[phase], 1)


def move_program(nc, sp, g, phase, n_mats, rows, x_in, x_out, adj_list, bufs, sems, x_free, adj_free, x_new):
    for dst, src in rows:
        sp.dma_start(dst, src.partition_broadcast(P)).then_inc(sems.params_in, 16)

    def load(s, i):
        group = i * STREAMS + s
        sp.dma_start(bufs[s].xin[:], x_in[group]).then_inc(sems.x_in[s], 16)
        for k, a in enumerate(adj_list):
            sp.dma_start(bufs[s].adjin[:, k], a[group]).then_inc(sems.adj_in[s], 16)

    def store(s, i):
        x_new(s, i)
        sp.dma_start(x_out[i * STREAMS + s], bufs[s].xout[:]).then_inc(sems.stored[s], 16)

    for s in range(STREAMS):
        load(s, 0)
    if phase + 1 < len(g.weights):
        sp.wait_ge(g.hi_split[phase], n_mats)
        sp.wait_ge(g.lo_split[phase], n_mats)
        nxt = g.weights[phase + 1]
        sp.dma_start(g.w_raw[:, :nxt.shape[1]], nxt).then_inc(g.weights_in[phase + 1], 16)
    with sp.Fori(1, ITER) as i:
        for s in range(STREAMS):
            x_free(s, i - 1)
            adj_free(s, i - 1)
            load(s, i)
        for s in range(STREAMS):
            store(s, i - 1)
    for s in range(STREAMS):
        store(s, ITER - 1)
    for s in range(STREAMS):
        sp.wait_ge(sems.stored[s], 16 * ITER + 1)


class Sems:
    pass


class Buf:
    pass


def phase_sems(nc, ctx, phase):
    m = Sems()

    def sem(name):
        return ctx.enter_context(nc.semaphore(f"{name}_{phase}"))
    m.params_in = sem("params_in")
    m.start_zero = sem("start_zero")
    m.factor_set = sem("factor_set")
    m.x_in, m.adj_in, m.stored, m.pe_done, m.act_done, m.dve_done, m.pool_done = (
        [sem(f"{name}{s}") for s in range(STREAMS)]
        for name in ("x_in", "adj_in", "stored", "pe_done", "act_done", "dve_done", "pool_done"))
    return m


def attention_phase(nc, g, phase, bias_times, x_in, x_out, adj, bv, bo):
    SCALE = float(FEAT) ** -0.5
    WQ, WK, WV, WO = range(4)
    stages = ["norm", "hT", "q", "k", "v", "scores", "soft_a", "soft_b", "soft_c",
              "pt0", "pt1", "pt2", "pt3", "pt4", "pt5", "pv", "out"]
    order = list(stage_order(stages, LAG_ATT))
    PE = Count(["hT", "q", "k", "v", "scores", "pt0", "pt1", "pt2", "pt3", "pt4", "pt5", "pv", "out"])
    AC = Count(["h", "hT_hi", "q", "e", "pt0", "pt2", "pt4", "oT_hi"])
    DV = Count(["stats", "aggr", "var", "shift", "hT_lo", "k", "v", "s", "max", "absmax", "diff", "sum", "rsum",
                "factor", "p", "pt1", "pt3", "pt5", "oT_lo", "xout"])
    PO = Count(["bias", "xb", "rstd", "p"])

    with ExitStack() as ctx:
        def sb(name, shape, dt=F32):
            return ctx.enter_context(nc.sbuf_tensor(f"{name}_{phase}", shape, dt))
        sems = phase_sems(nc, ctx, phase)
        pe_done, act_done, dve_done, pool_done = sems.pe_done, sems.act_done, sems.dve_done, sems.pool_done
        bv_row = sb("bv_row", [P, FEAT])
        bo_row = sb("bo_row", [P, FEAT])
        bias_factor = sb("bias_factor", [P, T, NODES])
        bufs = []
        for s in range(STREAMS):
            b = Buf()
            b.xin = sb(f"xin{s}", [P, T, FEAT])
            b.adjin = sb(f"adjin{s}", [P, 1, T, NODES])
            b.xb = sb(f"xb{s}", [P, T, FEAT])
            b.bias = sb(f"bias{s}", [P, T, NODES])
            b.st = sb(f"st{s}", [P, T, 6])
            b.mv = sb(f"mv{s}", [P, T, 2])
            b.rstd = sb(f"rstd{s}", [P, T])
            b.shift = sb(f"shift{s}", [P, T])
            b.h = sb(f"h{s}", [P, T, FEAT])
            b.t_hi = sb(f"t_hi{s}", [P, C, TOK], F32R)
            b.t_lo = sb(f"t_lo{s}", [P, C, TOK], F32R)
            b.q = sb(f"q{s}", [P, C, TOK])
            b.k = sb(f"k{s}", [P, C, TOK])
            b.v = sb(f"v{s}", [P, T, FEAT])
            b.s = sb(f"s{s}", [P, HT, NODES])
            b.max = sb(f"max{s}", [P, HT])
            b.absmax = sb(f"absmax{s}", [P, HT])
            b.sum = sb(f"sum{s}", [P, HT])
            b.rsum = sb(f"rsum{s}", [P, HT])
            b.factor = sb(f"factor{s}", [P, HT])
            b.p = sb(f"p{s}", [P, HT, P])
            b.pT = sb(f"pT{s}", [P, HT, P])
            b.xout = sb(f"xout{s}", [P, T, FEAT])
            b.ps = g.ps[s]
            b.ps_row = b.ps[:, 0:2, :].rearrange("p a b -> p (a b)")[:, 0:C * TOK].rearrange(
                "p (c t) -> p c t", c=C)
            b.ps_row2 = b.ps[:, 2:4, :].rearrange("p a b -> p (a b)")[:, 0:C * TOK].rearrange(
                "p (c t) -> p c t", c=C)
            b.ps_s = b.ps[:, :, 0:T * C * NODES].rearrange("p r (t c k) -> p r t c k", t=T, c=C)
            bufs.append(b)

        block = ctx.enter_context(nc.Block())

        @block.sync
        def _(sp):
            def x_free(s, i):
                sp.wait_ge(act_done[s], AC("h", i))
                sp.wait_ge(pool_done[s], PO("xb", i))

            def x_new(s, i):
                sp.wait_ge(dve_done[s], DV("xout", i))
            move_program(nc, sp, g, phase, 4, [(bv_row[:], bv), (bo_row[:], bo)], x_in, x_out, [adj], bufs,
                         sems, x_free, lambda s, i: None, x_new)

        @block.gpsimd
        def _(pool):
            pool.wait_ge(sems.params_in, 32)
            nc.gpsimd.memset(bias_factor[:], bias_times / SCALE).then_inc(sems.factor_set, 1)
            pool.wait_ge(sems.factor_set, 1)

            def norm(s, i):
                b = bufs[s]
                pool.wait_ge(dve_done[s], DV.all_before(i))
                pool.wait_ge(sems.adj_in[s], 16 * (i + 1))
                pool.wait_ge(sems.x_in[s], 16 * (i + 1))
                nc.gpsimd.tensor_tensor(b.bias[:], b.adjin[:, 0], bias_factor[:], ALU.mult)\
                    .then_inc(pool_done[s], 1)
                nc.gpsimd.tensor_tensor(b.xb[:], b.xin[:], bo_row[:].unsqueeze(1).broadcast_to([P, T, FEAT]),
                                        ALU.add).then_inc(pool_done[s], 1)
                pool.wait_ge(dve_done[s], DV("var", i))
                nc.gpsimd.tensor_tensor(b.rstd[:], b.rstd[:], g.neg_half[:, 0:T],
                                        ALU.pow).then_inc(pool_done[s], 1)
                pool.wait_ge(pool_done[s], PO("rstd", i))

            def soft_c(s, i):
                b = bufs[s]
                pool.wait_ge(dve_done[s], DV("factor", i))
                nc.gpsimd.tensor_tensor(b.p[NODES:P, :, NODES:P], b.s[NODES:P],
                                        b.factor[NODES:P].unsqueeze(2).broadcast_to([NODES, HT, NODES]),
                                        ALU.mult).then_inc(pool_done[s], 1)
                pool.wait_ge(pool_done[s], PO("p", i))

            run_stages(pool, order, {"norm": norm, "soft_c": soft_c})

        @block.scalar
        def _(act):
            weight_split(nc, g, phase, 4, act, None)

            def norm(s, i):
                b = bufs[s]
                act.wait_ge(dve_done[s], DV("shift", i))
                for t in range(T):
                    ins = nc.scalar.activation(b.h[:, t], b.xin[:, t], ACT.Relu, bias=b.shift[:, t:t + 1],
                                               scale=b.rstd[:, t:t + 1])
                ins.then_inc(act_done[s], 1)

            def hT(s, i):
                b = bufs[s]
                act.wait_ge(pe_done[s], PE("hT", i))
                nc.scalar.activation(b.t_hi[:], b.ps_row, ACT.Copy).then_inc(act_done[s], 1)

            def q(s, i):
                b = bufs[s]
                act.wait_ge(pe_done[s], PE("q", i))
                nc.scalar.activation(b.q[:], b.ps_row2, ACT.Copy).then_inc(act_done[s], 1)

            def soft_b(s, i):
                b = bufs[s]
                act.wait_ge(dve_done[s], DV("diff", i))
                nc.scalar.activation(b.s[:], b.s[:], ACT.Exp, scale=SCALE).then_inc(act_done[s], 1)

            def pt(u):
                def stage(s, i):
                    b = bufs[s]
                    act.wait_ge(pe_done[s], PE(f"pt{u}", i))
                    nc.scalar.activation(b.pT[:, 4 * u:4 * u + 4], b.ps[:, u % 4, :], ACT.Copy)\
                        .then_inc(act_done[s], 1)
                return stage

            def pv(s, i):
                b = bufs[s]
                act.wait_ge(pe_done[s], PE("pv", i))
                nc.scalar.activation(b.t_hi[:], b.ps_row2, ACT.Copy).then_inc(act_done[s], 1)

            run_stages(act, order, {"norm": norm, "hT": hT, "q": q, "soft_b": soft_b, "pt0": pt(0),
                                    "pt2": pt(2), "pt4": pt(4), "pv": pv})

        @block.vector
        def _(dve):
            weight_split(nc, g, phase, 4, None, dve)
            for s in range(STREAMS):
                nc.vector.memset(bufs[s].p[:], 0.0).then_inc(sems.start_zero, 1)
                nc.vector.memset(g.mark[:, s:s + 1], 0.0).then_inc(sems.stored[s], 1)
            dve.wait_ge(sems.params_in, 32)
            dve.wait_ge(sems.start_zero, STREAMS)

            def norm(s, i):
                b = bufs[s]
                dve.wait_ge(sems.x_in[s], 16 * (i + 1))
                for t in range(T):
                    ins = nc.vector.bn_stats(b.st[:, t], b.xin[:, t])
                ins.then_inc(dve_done[s], 1)
                dve.wait_ge(dve_done[s], DV("stats", i))
                nc.vector.memset(g.pad[:], 0.0)
                for t in range(T):
                    ins = nc.vector.bn_aggr(b.mv[:, t], b.st[:, t])
                ins.then_inc(dve_done[s], 1)
                dve.wait_ge(dve_done[s], DV("aggr", i))
                nc.vector.tensor_scalar(b.rstd[:], b.mv[:, :, 1], LN_EPS, None, ALU.add)\
                    .then_inc(dve_done[s], 1)
                dve.wait_ge(pool_done[s], PO("rstd", i))
                nc.vector.scalar_tensor_tensor(b.shift[:], b.mv[:, :, 0], -1.0, b.rstd[:], ALU.mult,
                                               ALU.mult).then_inc(dve_done[s], 1)

            def hT(s, i):
                b = bufs[s]
                dve.wait_ge(act_done[s], AC("hT_hi", i))
                nc.vector.tensor_tensor(b.t_lo[:], b.ps_row, b.t_hi[:].bitcast(F32), ALU.subtract)\
                    .then_inc(dve_done[s], 1)

            def k(s, i):
                b = bufs[s]
                dve.wait_ge(pe_done[s], PE("k", i))
                nc.vector.tensor_copy(b.k[:], b.ps_row).then_inc(dve_done[s], 1)

            def v(s, i):
                b = bufs[s]
                dve.wait_ge(pe_done[s], PE("v", i))
                nc.vector.tensor_tensor(b.v[:], b.ps[:, 2:4, 0:FEAT],
                                        bv_row[:].unsqueeze(1).broadcast_to([P, T, FEAT]),
                                        ALU.add).then_inc(dve_done[s], 1)

            def soft_a(s, i):
                b = bufs[s]
                dve.wait_ge(pe_done[s], PE("scores", i))
                dve.wait_ge(pool_done[s], PO("bias", i))
                for t in range(T):
                    ins = nc.vector.tensor_tensor(
                        b.s[:].rearrange("p (r t c) k -> p r t c k", r=HPC, t=T)[:, :, t], b.ps_s[:, :, t],
                        b.bias[:, t:t + 1].unsqueeze(1).broadcast_to([P, HPC, C, NODES]), ALU.add)
                ins.then_inc(dve_done[s], 1)
                dve.wait_ge(dve_done[s], DV("s", i))
                nc.vector.tensor_reduce(b.max[:], b.s[:], AX.X, ALU.max).then_inc(dve_done[s], 1)

            def soft_b(s, i):
                b = bufs[s]
                nc.vector.tensor_reduce(b.absmax[:], b.s[:], AX.X, ALU.max, apply_absolute_value=True)\
                    .then_inc(dve_done[s], 1)
                dve.wait_ge(dve_done[s], DV("absmax", i))
                nc.vector.tensor_tensor(b.s[:], b.s[:], b.max[:].unsqueeze(2).broadcast_to([P, HT, NODES]),
                                        ALU.subtract).then_inc(dve_done[s], 1)

            def soft_c(s, i):
                b = bufs[s]
                dve.wait_ge(act_done[s], AC("e", i))
                nc.vector.tensor_reduce(b.sum[:], b.s[:], AX.X, ALU.add).then_inc(dve_done[s], 1)
                dve.wait_ge(dve_done[s], DV("sum", i))
                nc.vector.reciprocal(b.rsum[:], b.sum[:]).then_inc(dve_done[s], 1)
                dve.wait_ge(dve_done[s], DV("rsum", i))
                nc.vector.scalar_tensor_tensor(b.factor[:], b.absmax[:], 0.0, b.rsum[:], ALU.not_equal,
                                               ALU.mult).then_inc(dve_done[s], 1)
                dve.wait_ge(dve_done[s], DV("factor", i))
                nc.vector.tensor_tensor(b.p[0:NODES, :, 0:NODES], b.s[0:NODES],
                                        b.factor[0:NODES].unsqueeze(2).broadcast_to([NODES, HT, NODES]),
                                        ALU.mult).then_inc(dve_done[s], 1)

            def pt(u):
                def stage(s, i):
                    b = bufs[s]
                    dve.wait_ge(pe_done[s], PE(f"pt{u}", i))
                    nc.vector.tensor_copy(b.pT[:, 4 * u:4 * u + 4],
                                          b.ps[:, u % 4, :].rearrange("p (h k) -> p h k", k=P))\
                        .then_inc(dve_done[s], 1)
                return stage

            def pv(s, i):
                b = bufs[s]
                dve.wait_ge(act_done[s], AC("oT_hi", i))
                nc.vector.tensor_tensor(b.t_lo[:], b.ps_row2, b.t_hi[:].bitcast(F32), ALU.subtract)\
                    .then_inc(dve_done[s], 1)

            def out(s, i):
                b = bufs[s]
                dve.wait_ge(pe_done[s], PE("out", i))
                dve.wait_ge(pool_done[s], PO("xb", i))
                dve.wait_ge(sems.stored[s], 16 * i + 1)
                nc.vector.tensor_tensor(b.xout[:], b.ps[:, 0:2, 0:FEAT], b.xb[:], ALU.add)\
                    .then_inc(dve_done[s], 1)

            run_stages(dve, order, {"norm": norm, "hT": hT, "k": k, "v": v, "soft_a": soft_a,
                                    "soft_b": soft_b, "soft_c": soft_c, "pt1": pt(1), "pt3": pt(3),
                                    "pt5": pt(5), "pv": pv, "out": out})

        @block.tensor
        def _(pe):
            pe.wait_ge(g.hi_split[phase], 4)
            pe.wait_ge(g.lo_split[phase], 4)
            pe.wait_ge(g.const_in, g.const_count)

            def hT(s, i):
                b = bufs[s]
                pe.wait_ge(act_done[s], AC("h", i))
                pe.wait_ge(dve_done[s], DV.all_before(i))
                for c in range(C):
                    for t in range(T):
                        mm = nc.tensor.transpose(b.ps_row[:, c, t * P:(t + 1) * P],
                                                 b.h[:, t, c * P:(c + 1) * P], g.ident[:])
                mm.then_inc(pe_done[s], 1)

            def project_T(b, out, m):
                for o in range(C):
                    mm = exact_product(nc, out[:, o], [
                        (g.w_hi[:, m, c, o * P:(o + 1) * P], g.w_lo[:, m, c, o * P:(o + 1) * P],
                         b.t_hi[:, c], b.t_lo[:, c]) for c in range(C)])
                return mm

            def project(b, banks, m):
                for t in range(T):
                    mm = exact_product(nc, b.ps[:, banks + t, 0:FEAT], [
                        (b.t_hi[:, c, t * P:(t + 1) * P], b.t_lo[:, c, t * P:(t + 1) * P],
                         g.w_hi[:, m, c], g.w_lo[:, m, c]) for c in range(C)])
                return mm

            def q(s, i):
                pe.wait_ge(act_done[s], AC("hT_hi", i))
                pe.wait_ge(dve_done[s], DV("hT_lo", i))
                project_T(bufs[s], bufs[s].ps_row2, WQ).then_inc(pe_done[s], 1)

            def k(s, i):
                project_T(bufs[s], bufs[s].ps_row, WK).then_inc(pe_done[s], 1)

            def v(s, i):
                pe.wait_ge(act_done[s], AC("q", i))
                project(bufs[s], 2, WV).then_inc(pe_done[s], 1)

            def scores(s, i):
                b = bufs[s]
                pe.wait_ge(dve_done[s], DV("v", i))
                for t in range(T):
                    for h in range(HEADS):
                        r = HD * (h % HPC)
                        for gr in range(2):
                            at = t * P + gr * NODES
                            mm = nc.tensor.matmul(b.ps_s[gr * NODES:(gr + 1) * NODES, h % HPC, t, h // HPC],
                                                  b.q[r:r + HD, h // HPC, at:at + NODES],
                                                  b.k[r:r + HD, h // HPC, at:at + NODES],
                                                  start=True, stop=True)
                mm.then_inc(pe_done[s], 1)

            def pt(u):
                def stage(s, i):
                    b = bufs[s]
                    if u == 0:
                        pe.wait_ge(dve_done[s], DV("p", i))
                        pe.wait_ge(pool_done[s], PO("p", i))
                    if u >= 4:
                        if u % 2 == 0:
                            pe.wait_ge(act_done[s], AC(f"pt{u - 4}", i))
                        else:
                            pe.wait_ge(dve_done[s], DV(f"pt{u - 4}", i))
                    for j in range(4):
                        mm = nc.tensor.transpose(b.ps[:, u % 4, j * P:(j + 1) * P], b.p[:, 4 * u + j],
                                                 g.ident[:])
                    mm.then_inc(pe_done[s], 1)
                return stage

            def pv(s, i):
                b = bufs[s]
                pe.wait_ge(act_done[s], AC("pt4", i))
                pe.wait_ge(dve_done[s], DV("pt5", i))
                for t in range(T):
                    for h in range(HEADS):
                        r = HD * (h % HPC)
                        mm = nc.tensor.matmul(b.ps_row2[r:r + HD, h // HPC, t * P:(t + 1) * P],
                                              b.v[:, t, h * HD:(h + 1) * HD], b.pT[:, head_tile(t, h)],
                                              start=True, stop=True, tile_position=(0, r))
                mm.then_inc(pe_done[s], 1)

            def out(s, i):
                pe.wait_ge(act_done[s], AC("oT_hi", i))
                pe.wait_ge(dve_done[s], DV("oT_lo", i))
                project(bufs[s], 0, WO).then_inc(pe_done[s], 1)

            todo = {"hT": hT, "q": q, "k": k, "v": v, "scores": scores, "pv": pv, "out": out}
            todo.update({f"pt{u}": pt(u) for u in range(6)})
            run_stages(pe, order, todo)


def gcn_phase(nc, g, phase, directed, x_in, x_out, adjs, params):
    TEMPER = float(np.sqrt(FEAT))
    n_adj = len(adjs)
    per_layer = ["hT", "ml", "mr", "u", "soft", "att", "aT", "agg", "lin", "ln"] if not directed else \
        ["hT", "u", "soft", "att", "aT", "agg0", "agg1", "lin", "ln"]
    stages = ["norm"] + [f"{st}_{l}" for l in range(2) for st in per_layer]
    order = list(stage_order(stages, LAG_GCN3 if directed else LAG_GCN0))

    def both(names):
        return [f"{name}_{l}" for l in range(2) for name in names]

    if directed:
        PE = Count(both(["hT", "u", "aT", "agg0", "agg1", "lin"]))
        AC = Count(["h"] + both(["hT", "e", "bd", "agg0_hi", "agg1_hi", "z", "h_next"])[:-1])
        DV = Count(["stats", "aggr", "var", "shift"] + both(
            ["max", "diff", "sum", "rsum", "ea", "a", "asum", "asum_eps", "rasum", "att", "parts", "psum",
             "aT", "agg0_lo", "agg1_lo", "c0", "c1", "c2", "lstats", "laggr", "lvar", "lshift", "zb"])
            + ["xout"])
        PO = Count(["adj", "x", "rstd"] + both(["lstd", "za"]))
        LN_LAST_EPS = 1e-12
    else:
        PE = Count(both(["hT", "ml", "mr", "u", "aT", "agg", "lin"]))
        AC = Count(["h"] + both(["hT_hi", "hT", "ml", "e", "agg_hi", "z", "h_next"])[:-1])
        DV = Count(["stats", "aggr", "var", "shift"] + both(
            ["hT_lo", "mr", "w", "u", "ea", "asum", "asum_eps", "rasum", "share", "att", "aT",
             "agg_lo", "ctx", "lstats", "laggr", "lvar", "lsig", "lrstd", "lshift", "zb"]) + ["xout"])
        PO = Count(["adj", "clr", "x", "rstd"] + both(["lstd", "za"]))

    with ExitStack() as ctx:
        def sb(name, shape, dt=F32):
            return ctx.enter_context(nc.sbuf_tensor(f"{name}_{phase}", shape, dt))
        sems = phase_sems(nc, ctx, phase)
        pe_done, act_done, dve_done, pool_done = sems.pe_done, sems.act_done, sems.dve_done, sems.pool_done
        rows = [[sb(f"row{l}_{k}", [P, FEAT]) for k in range(len(params[l]))] for l in range(2)]
        bufs = []
        for s in range(STREAMS):
            b = Buf()
            b.xin = sb(f"xin{s}", [P, T, FEAT])
            b.adjin = sb(f"adjin{s}", [P, n_adj, T, NODES])
            b.x = sb(f"x{s}", [P, T, FEAT])
            b.adj = sb(f"adj{s}", [P, T, NODES])
            b.st = sb(f"st{s}", [P, T, 6])
            b.mv = sb(f"mv{s}", [P, T, 2])
            b.rstd = sb(f"rstd{s}", [P, T])
            b.shift = sb(f"shift{s}", [P, T])
            b.h = sb(f"h{s}", [P, T, FEAT])
            b.hT = sb(f"hT{s}", [P, C, TOK])
            b.e = sb(f"e{s}", [P, T, NODES])
            b.asum = sb(f"asum{s}", [P, T])
            b.rasum = sb(f"rasum{s}", [P, T])
            b.a_bd = sb(f"a_bd{s}", [P, T, P])
            b.ctx = sb(f"ctx{s}", [P, T, FEAT])
            b.z = sb(f"z{s}", [P, T, FEAT])
            b.xout = sb(f"xout{s}", [P, T, FEAT])
            if directed:
                b.max = sb(f"max{s}", [P, T])
                b.sum = sb(f"sum{s}", [P, T])
                b.rsum = sb(f"rsum{s}", [P, T])
                b.att = sb(f"att{s}", [P, T, NODES])
                b.parts = sb(f"parts{s}", [P, T, 3, NODES])
                b.psum = sb(f"psum{s}", [P, T, 3])
                b.aT = sb(f"aT{s}", [P, T, 3, P])
                b.agg_hi = sb(f"agg_hi{s}", [P, T, C, 3 * P], F32R)
                b.agg_lo = sb(f"agg_lo{s}", [P, T, C, 3 * P], F32R)
            else:
                b.clr = sb(f"clr{s}", [P, T, 2, NODES])
                b.t_hi = sb(f"t_hi{s}", [P, C, TOK], F32R)
                b.t_lo = sb(f"t_lo{s}", [P, C, TOK], F32R)
                b.mlr = sb(f"mlr{s}", [P, C, 2, TOK])
                b.w = sb(f"w{s}", [P, T, 2, NODES])
                b.share = sb(f"share{s}", [P, T])
                b.aT = sb(f"aT{s}", [P, T, P])
            b.ps = g.ps[s]
            b.ps_row = b.ps[:, 0:2, :].rearrange("p a b -> p (a b)")[:, 0:C * TOK].rearrange(
                "p (c t) -> p c t", c=C)
            b.ps_row2 = b.ps[:, 2:4, :].rearrange("p a b -> p (a b)")[:, 0:C * TOK].rearrange(
                "p (c t) -> p c t", c=C)
            bufs.append(b)

        block = ctx.enter_context(nc.Block())

        @block.sync
        def _(sp):
            def x_free(s, i):
                sp.wait_ge(act_done[s], AC("h", i))
                sp.wait_ge(pool_done[s], PO("x", i))

            def x_new(s, i):
                sp.wait_ge(dve_done[s], DV("xout", i))
            if phase == 0:
                sp.dma_start(g.w_raw[:, :g.weights[0].shape[1]], g.weights[0]).then_inc(g.weights_in[0], 16)
                for dst, src in g.const_loads:
                    sp.dma_start(dst, src).then_inc(g.const_in, 16)
            pairs = [(rows[l][k][:], params[l][k]) for l in range(2) for k in range(len(params[l]))]
            move_program(nc, sp, g, phase, 6, pairs, x_in, x_out, adjs, bufs, sems, x_free,
                         lambda s, i: None, x_new)

        n_rows = sum(len(p) for p in params)

        @block.gpsimd
        def _(pool):
            if phase == 0:
                nc.gpsimd.memset(g.neg_half[:], -0.5).then_inc(g.powers, 1)
                nc.gpsimd.memset(g.ones[:], 1.0).then_inc(g.powers, 1)
                nc.gpsimd.memset(g.pos_half[:], 0.5).then_inc(g.powers, 1)
            pool.wait_ge(g.powers, 3)
            pool.wait_ge(g.const_in, g.const_count)
            pool.wait_ge(sems.params_in, 16 * n_rows)

            def norm(s, i):
                b = bufs[s]
                pool.wait_ge(dve_done[s], DV.all_before(i))
                pool.wait_ge(sems.adj_in[s], 16 * n_adj * (i + 1))
                pool.wait_ge(sems.x_in[s], 16 * (i + 1))
                nc.gpsimd.tensor_tensor(b.adj[:], b.adjin[:, 0], g.ones[:], ALU.mult)\
                    .then_inc(pool_done[s], 1)
                if not directed:
                    for k in range(2):
                        ins = nc.gpsimd.tensor_tensor(b.clr[:, :, k], b.adjin[:, k],
                                                      g.tri[:, k:k + 1].broadcast_to([P, T, NODES]), ALU.mult)
                    ins.then_inc(pool_done[s], 1)
                nc.gpsimd.tensor_scalar(b.x[:], b.xin[:], 1.0, 0.0, ALU.mult, ALU.add)\
                    .then_inc(pool_done[s], 1)
                pool.wait_ge(dve_done[s], DV("var", i))
                nc.gpsimd.tensor_tensor(b.rstd[:], b.rstd[:], g.neg_half[:, 0:T],
                                        ALU.pow).then_inc(pool_done[s], 1)

            def ln(l):
                def stage(s, i):
                    b = bufs[s]
                    pool.wait_ge(dve_done[s], DV(f"lvar_{l}", i))
                    nc.gpsimd.tensor_tensor(b.rstd[:], b.rstd[:], (g.neg_half if directed else g.pos_half)[:, 0:T],
                                            ALU.pow).then_inc(pool_done[s], 1)
                    pool.wait_ge(act_done[s], AC(f"z_{l}", i))
                    nc.gpsimd.tensor_tensor(b.z[:], b.z[:], rows[l][-2][:].unsqueeze(1).broadcast_to([P, T, FEAT]),
                                            ALU.mult).then_inc(pool_done[s], 1)
                return stage

            run_stages(pool, order, {"norm": norm, "ln_0": ln(0), "ln_1": ln(1)})

        @block.scalar
        def _(act):
            weight_split(nc, g, phase, 6, act, None)

            def norm(s, i):
                b = bufs[s]
                act.wait_ge(dve_done[s], DV("shift", i))
                for t in range(T):
                    ins = nc.scalar.activation(b.h[:, t], b.xin[:, t], ACT.Relu, bias=b.shift[:, t:t + 1],
                                               scale=b.rstd[:, t:t + 1])
                ins.then_inc(act_done[s], 1)

            def layer(l):
                def hT(s, i):
                    b = bufs[s]
                    act.wait_ge(pe_done[s], PE(f"hT_{l}", i))
                    if not directed:
                        nc.scalar.activation(b.t_hi[:], b.ps_row, ACT.Copy).then_inc(act_done[s], 1)
                        act.wait_ge(dve_done[s], DV(f"hT_lo_{l}", i))
                    nc.scalar.activation(b.hT[:], b.ps_row, ACT.Copy).then_inc(act_done[s], 1)

                def ml(s, i):
                    b = bufs[s]
                    act.wait_ge(pe_done[s], PE(f"ml_{l}", i))
                    nc.scalar.activation(b.mlr[:, :, 0], b.ps_row2, ACT.Copy).then_inc(act_done[s], 1)

                def soft(s, i):
                    b = bufs[s]
                    act.wait_ge(dve_done[s], DV(f"diff_{l}" if directed else f"u_{l}", i))
                    nc.scalar.activation(b.e[:], b.e[:], ACT.Exp, scale=1.0 / TEMPER if directed else 1.0)\
                        .then_inc(act_done[s], 1)

                def att(s, i):
                    b = bufs[s]
                    act.wait_ge(dve_done[s], DV(f"att_{l}", i))
                    nc.scalar.activation(b.a_bd[0:NODES, :, 0:NODES], b.att[0:NODES], ACT.Copy)
                    nc.scalar.activation(b.a_bd[NODES:P, :, NODES:P], b.att[NODES:P], ACT.Copy)\
                        .then_inc(act_done[s], 1)

                def agg(s, i):
                    b = bufs[s]
                    act.wait_ge(pe_done[s], PE(f"agg_{l}", i))
                    nc.scalar.activation(b.t_hi[:], b.ps_row2, ACT.Copy).then_inc(act_done[s], 1)

                def agg_t(t):
                    def stage(s, i):
                        b = bufs[s]
                        act.wait_ge(pe_done[s], PE(f"agg{t}_{l}", i))
                        nc.scalar.activation(b.agg_hi[:, t], b.ps[:, 0:C, 0:3 * P], ACT.Copy)\
                            .then_inc(act_done[s], 1)
                    return stage

                def ln(s, i):
                    b = bufs[s]
                    act.wait_ge(dve_done[s], DV(f"lshift_{l}", i))
                    for t in range(T):
                        ins = nc.scalar.activation(b.z[:, t], b.ctx[:, t], ACT.Identity,
                                                   bias=b.shift[:, t:t + 1], scale=b.rstd[:, t:t + 1])
                    ins.then_inc(act_done[s], 1)
                    if l == 0:
                        act.wait_ge(dve_done[s], DV("zb_0", i))
                        nc.scalar.activation(b.h[:], b.z[:], ACT.Relu).then_inc(act_done[s], 1)

                if directed:
                    return {f"hT_{l}": hT, f"soft_{l}": soft, f"att_{l}": att, f"agg0_{l}": agg_t(0),
                            f"agg1_{l}": agg_t(1), f"ln_{l}": ln}
                return {f"hT_{l}": hT, f"ml_{l}": ml, f"soft_{l}": soft, f"agg_{l}": agg, f"ln_{l}": ln}

            run_stages(act, order, {"norm": norm, **layer(0), **layer(1)})

        @block.vector
        def _(dve):
            weight_split(nc, g, phase, 6, None, dve)
            for s in range(STREAMS):
                nc.vector.memset(bufs[s].a_bd[:], 0.0).then_inc(sems.start_zero, 1)
                nc.vector.memset(g.mark[:, s:s + 1], 0.0).then_inc(sems.stored[s], 1)
            dve.wait_ge(g.const_in, g.const_count)
            dve.wait_ge(sems.params_in, 16 * n_rows)
            dve.wait_ge(sems.start_zero, STREAMS)

            def wait_own(s, name, i):
                dve.wait_ge(dve_done[s], DV(name, i))

            def norm(s, i):
                b = bufs[s]
                dve.wait_ge(sems.x_in[s], 16 * (i + 1))
                for t in range(T):
                    ins = nc.vector.bn_stats(b.st[:, t], b.xin[:, t])
                ins.then_inc(dve_done[s], 1)
                wait_own(s, "stats", i)
                nc.vector.memset(g.pad[:], 0.0)
                for t in range(T):
                    ins = nc.vector.bn_aggr(b.mv[:, t], b.st[:, t])
                ins.then_inc(dve_done[s], 1)
                wait_own(s, "aggr", i)
                nc.vector.tensor_scalar(b.rstd[:], b.mv[:, :, 1], LN_EPS, None, ALU.add)\
                    .then_inc(dve_done[s], 1)
                dve.wait_ge(pool_done[s], PO("rstd", i))
                nc.vector.scalar_tensor_tensor(b.shift[:], b.mv[:, :, 0], -1.0, b.rstd[:], ALU.mult,
                                               ALU.mult).then_inc(dve_done[s], 1)

            def layer(l):
                def hT(s, i):
                    b = bufs[s]
                    dve.wait_ge(act_done[s], AC(f"hT_hi_{l}", i))
                    nc.vector.tensor_tensor(b.t_lo[:], b.ps_row, b.t_hi[:].bitcast(F32), ALU.subtract)\
                        .then_inc(dve_done[s], 1)

                def mr(s, i):
                    b = bufs[s]
                    dve.wait_ge(pe_done[s], PE(f"mr_{l}", i))
                    nc.vector.tensor_copy(b.mlr[:, :, 1], b.ps_row).then_inc(dve_done[s], 1)

                def normalise_start(s, i):
                    b = bufs[s]
                    wait_own(s, f"asum_{l}", i)
                    nc.vector.tensor_scalar(b.rasum[:], b.asum[:], 1e-10, None, ALU.add)\
                        .then_inc(dve_done[s], 1)
                    wait_own(s, f"asum_eps_{l}", i)
                    nc.vector.reciprocal(b.rasum[:], b.rasum[:]).then_inc(dve_done[s], 1)
                    wait_own(s, f"rasum_{l}", i)

                def soft(s, i):
                    b = bufs[s]
                    dve.wait_ge(pe_done[s], PE(f"u_{l}", i))
                    dve.wait_ge(pool_done[s], PO("x", i))
                    if directed:
                        scores = b.ps[:, 3, 0:T * NODES].rearrange("p (t j) -> p t j", t=T)
                        nc.vector.tensor_reduce(b.max[:], scores, AX.X, ALU.max).then_inc(dve_done[s], 1)
                        wait_own(s, f"max_{l}", i)
                        nc.vector.tensor_tensor(b.e[:], scores,
                                                b.max[:].unsqueeze(2).broadcast_to([P, T, NODES]),
                                                ALU.subtract).then_inc(dve_done[s], 1)
                    else:
                        nc.vector.tensor_tensor(
                            b.w[:], b.ps[:, 2, 0:T * P].rearrange("p (t k j) -> p t k j", t=T, k=2),
                            b.clr[:], ALU.mult).then_inc(dve_done[s], 1)
                        wait_own(s, f"w_{l}", i)
                        nc.vector.tensor_tensor(b.e[:], b.w[:, :, 0], b.w[:, :, 1], ALU.add)\
                            .then_inc(dve_done[s], 1)

                def att(s, i):
                    b = bufs[s]
                    dve.wait_ge(act_done[s], AC(f"e_{l}", i))
                    if directed:
                        nc.vector.tensor_reduce(b.sum[:], b.e[:], AX.X, ALU.add).then_inc(dve_done[s], 1)
                        wait_own(s, f"sum_{l}", i)
                        nc.vector.reciprocal(b.rsum[:], b.sum[:]).then_inc(dve_done[s], 1)
                        nc.vector.tensor_tensor(b.e[:], b.e[:], b.adj[:], ALU.mult).then_inc(dve_done[s], 1)
                        wait_own(s, f"ea_{l}", i)
                        nc.vector.tensor_tensor(b.e[:], b.e[:],
                                                b.rsum[:].unsqueeze(2).broadcast_to([P, T, NODES]),
                                                ALU.mult).then_inc(dve_done[s], 1)
                        wait_own(s, f"a_{l}", i)
                    else:
                        nc.vector.tensor_tensor(b.e[:], b.e[:], b.adj[:], ALU.mult).then_inc(dve_done[s], 1)
                        wait_own(s, f"ea_{l}", i)
                    nc.vector.tensor_reduce(b.asum[:], b.e[:], AX.X, ALU.add).then_inc(dve_done[s], 1)
                    normalise_start(s, i)
                    if directed:
                        nc.vector.tensor_tensor(b.att[:], b.e[:],
                                                b.rasum[:].unsqueeze(2).broadcast_to([P, T, NODES]),
                                                ALU.mult).then_inc(dve_done[s], 1)
                        wait_own(s, f"att_{l}", i)
                        nc.vector.tensor_tensor(
                            b.parts[:], b.att[:].unsqueeze(2).broadcast_to([P, T, 3, NODES]),
                            g.part_rows[:].unsqueeze(1).broadcast_to([P, T, 3, NODES]),
                            ALU.mult).then_inc(dve_done[s], 1)
                        wait_own(s, f"parts_{l}", i)
                        nc.vector.tensor_reduce(b.psum[:], b.parts[:], AX.X, ALU.add)\
                            .then_inc(dve_done[s], 1)
                    else:
                        nc.vector.tensor_tensor(b.share[:], b.asum[:], b.rasum[:], ALU.mult)\
                            .then_inc(dve_done[s], 1)
                        for q in (0, NODES):
                            ins = nc.vector.tensor_tensor(
                                b.a_bd[q:q + NODES, :, q:q + NODES], b.e[q:q + NODES],
                                b.rasum[q:q + NODES].unsqueeze(2).broadcast_to([NODES, T, NODES]), ALU.mult)
                        ins.then_inc(dve_done[s], 1)

                def aT(s, i):
                    b = bufs[s]
                    dve.wait_ge(pe_done[s], PE(f"aT_{l}", i))
                    got = b.ps[:, 3, 0:T * P].rearrange("p (t i) -> p t i", t=T)
                    if directed:
                        nc.vector.tensor_tensor(
                            b.aT[:], got.unsqueeze(2).broadcast_to([P, T, 3, P]),
                            g.part_cols[:].unsqueeze(1).broadcast_to([P, T, 3, P]),
                            ALU.mult).then_inc(dve_done[s], 1)
                    else:
                        nc.vector.tensor_copy(b.aT[:], got).then_inc(dve_done[s], 1)

                def agg(s, i):
                    b = bufs[s]
                    dve.wait_ge(act_done[s], AC(f"agg_hi_{l}", i))
                    nc.vector.tensor_tensor(b.t_lo[:], b.ps_row2, b.t_hi[:].bitcast(F32), ALU.subtract)\
                        .then_inc(dve_done[s], 1)

                def agg_t(t):
                    def stage(s, i):
                        b = bufs[s]
                        dve.wait_ge(act_done[s], AC(f"agg{t}_hi_{l}", i))
                        nc.vector.tensor_tensor(b.agg_lo[:, t], b.ps[:, 0:C, 0:3 * P],
                                                b.agg_hi[:, t].bitcast(F32), ALU.subtract)\
                            .then_inc(dve_done[s], 1)
                    return stage

                def lin(s, i):
                    b = bufs[s]
                    dve.wait_ge(pe_done[s], PE(f"lin_{l}", i))
                    if directed:
                        for m in range(3):
                            for t in range(T):
                                ins = nc.vector.scalar_tensor_tensor(
                                    b.ctx[:, t], rows[l][m][:], b.psum[:, t, m:m + 1],
                                    b.ps[:, t, 0:FEAT] if m == 0 else b.ctx[:, t], ALU.mult, ALU.add)
                            ins.then_inc(dve_done[s], 1)
                            wait_own(s, f"c{m}_{l}", i)
                    else:
                        for t in range(T):
                            ins = nc.vector.scalar_tensor_tensor(
                                b.ctx[:, t], rows[l][0][:], b.share[:, t:t + 1], b.ps[:, t, 0:FEAT],
                                ALU.mult, ALU.add)
                        ins.then_inc(dve_done[s], 1)
                        wait_own(s, f"ctx_{l}", i)
                    for t in range(T):
                        ins = nc.vector.bn_stats(b.st[:, t], b.ctx[:, t])
                    ins.then_inc(dve_done[s], 1)
                    wait_own(s, f"lstats_{l}", i)
                    nc.vector.memset(g.pad[:], 0.0)
                    for t in range(T):
                        ins = nc.vector.bn_aggr(b.mv[:, t], b.st[:, t])
                    ins.then_inc(dve_done[s], 1)
                    wait_own(s, f"laggr_{l}", i)
                    if directed:
                        nc.vector.tensor_scalar(b.rstd[:], b.mv[:, :, 1], 1e-12, None, ALU.add)\
                            .then_inc(dve_done[s], 1)
                    else:
                        nc.vector.tensor_scalar(b.rstd[:], b.mv[:, :, 1], FEAT / (FEAT - 1.0), None, ALU.mult)\
                            .then_inc(dve_done[s], 1)

                def ln(s, i):
                    b = bufs[s]
                    dve.wait_ge(pool_done[s], PO(f"lstd_{l}", i))
                    if not directed:
                        nc.vector.tensor_scalar(b.rstd[:], b.rstd[:], 1e-3, None, ALU.add)\
                            .then_inc(dve_done[s], 1)
                        wait_own(s, f"lsig_{l}", i)
                        nc.vector.reciprocal(b.rstd[:], b.rstd[:]).then_inc(dve_done[s], 1)
                        wait_own(s, f"lrstd_{l}", i)
                    nc.vector.scalar_tensor_tensor(b.shift[:], b.mv[:, :, 0], -1.0, b.rstd[:], ALU.mult,
                                                   ALU.mult).then_inc(dve_done[s], 1)
                    dve.wait_ge(pool_done[s], PO(f"za_{l}", i))
                    nc.vector.tensor_tensor(b.z[:], b.z[:], rows[l][-1][:].unsqueeze(1).broadcast_to([P, T, FEAT]),
                                            ALU.add).then_inc(dve_done[s], 1)
                    if l == 1:
                        wait_own(s, "zb_1", i)
                        dve.wait_ge(sems.stored[s], 16 * i + 1)
                        nc.vector.scalar_tensor_tensor(b.xout[:], b.z[:], 0.0, b.x[:], ALU.max, ALU.add)\
                            .then_inc(dve_done[s], 1)

                both = {f"soft_{l}": soft, f"att_{l}": att, f"aT_{l}": aT, f"lin_{l}": lin, f"ln_{l}": ln}
                if directed:
                    return {**both, f"agg0_{l}": agg_t(0), f"agg1_{l}": agg_t(1)}
                return {**both, f"hT_{l}": hT, f"mr_{l}": mr, f"agg_{l}": agg}

            run_stages(dve, order, {"norm": norm, **layer(0), **layer(1)})

        @block.tensor
        def _(pe):
            pe.wait_ge(g.hi_split[phase], 6)
            pe.wait_ge(g.lo_split[phase], 6)
            pe.wait_ge(g.const_in, g.const_count)

            def layer(l):
                def hT(s, i):
                    b = bufs[s]
                    pe.wait_ge(act_done[s], AC("h", i) if l == 0 else AC("h_next_0", i))
                    for c in range(C):
                        for t in range(T):
                            mm = nc.tensor.transpose(b.ps_row[:, c, t * P:(t + 1) * P],
                                                     b.h[:, t, c * P:(c + 1) * P], g.ident[:])
                    mm.then_inc(pe_done[s], 1)

                def project_T(b, out, m):
                    for o in range(C):
                        mm = exact_product(nc, out[:, o], [
                            (g.w_hi[:, m, c, o * P:(o + 1) * P], g.w_lo[:, m, c, o * P:(o + 1) * P],
                             b.t_hi[:, c], b.t_lo[:, c]) for c in range(C)])
                    return mm

                def ml(s, i):
                    pe.wait_ge(dve_done[s], DV(f"hT_lo_{l}", i))
                    project_T(bufs[s], bufs[s].ps_row2, 3 * l).then_inc(pe_done[s], 1)

                def mr(s, i):
                    pe.wait_ge(act_done[s], AC(f"hT_{l}", i))
                    project_T(bufs[s], bufs[s].ps_row, 3 * l + 1).then_inc(pe_done[s], 1)

                def u(s, i):
                    b = bufs[s]
                    if directed:
                        pe.wait_ge(act_done[s], AC(f"hT_{l}", i))
                    else:
                        pe.wait_ge(act_done[s], AC(f"ml_{l}", i))
                        pe.wait_ge(dve_done[s], DV(f"mr_{l}", i))
                    for t in range(T):
                        for gr in range(2):
                            at = t * P + gr * NODES
                            rows_ = slice(gr * NODES, (gr + 1) * NODES)
                            for c in range(C):
                                if directed:
                                    out = b.ps[rows_, 3, t * NODES:(t + 1) * NODES]
                                    rhs = b.hT[:, c, at:at + NODES]
                                else:
                                    out = b.ps[rows_, 2, t * P:(t + 1) * P]
                                    rhs = b.mlr[:, c, :, at:at + NODES]
                                mm = nc.tensor.matmul(out, b.hT[:, c, at:at + NODES], rhs,
                                                      start=(c == 0), stop=(c == C - 1))
                    mm.then_inc(pe_done[s], 1)

                def aT(s, i):
                    b = bufs[s]
                    if directed:
                        pe.wait_ge(act_done[s], AC(f"bd_{l}", i))
                    else:
                        pe.wait_ge(dve_done[s], DV(f"att_{l}", i))
                    for t in range(T):
                        mm = nc.tensor.transpose(b.ps[:, 3, t * P:(t + 1) * P], b.a_bd[:, t], g.ident[:])
                    mm.then_inc(pe_done[s], 1)

                def agg(s, i):
                    b = bufs[s]
                    pe.wait_ge(dve_done[s], DV(f"aT_{l}", i))
                    for c in range(C):
                        for t in range(T):
                            mm = nc.tensor.matmul(b.ps_row2[:, c, t * P:(t + 1) * P],
                                                  b.h[:, t, c * P:(c + 1) * P], b.aT[:, t],
                                                  start=True, stop=True)
                    mm.then_inc(pe_done[s], 1)

                def agg_t(t):
                    def stage(s, i):
                        b = bufs[s]
                        if t == 0:
                            pe.wait_ge(dve_done[s], DV(f"aT_{l}", i))
                        else:
                            pe.wait_ge(dve_done[s], DV(f"agg0_lo_{l}", i))
                        for c in range(C):
                            mm = nc.tensor.matmul(b.ps[:, c, 0:3 * P], b.h[:, t, c * P:(c + 1) * P],
                                                  b.aT[:, t].rearrange("p m i -> p (m i)"),
                                                  start=True, stop=True)
                        mm.then_inc(pe_done[s], 1)
                    return stage

                def lin(s, i):
                    b = bufs[s]
                    pe.wait_ge(dve_done[s], DV(f"agg1_lo_{l}" if directed else f"agg_lo_{l}", i))
                    for t in range(T):
                        if directed:
                            terms = [(b.agg_hi[:, t, c, m * P:(m + 1) * P], b.agg_lo[:, t, c, m * P:(m + 1) * P],
                                      g.w_hi[:, 3 * l + m, c], g.w_lo[:, 3 * l + m, c])
                                     for m in range(3) for c in range(C)]
                        else:
                            terms = [(b.t_hi[:, c, t * P:(t + 1) * P], b.t_lo[:, c, t * P:(t + 1) * P],
                                      g.w_hi[:, 3 * l + 2, c], g.w_lo[:, 3 * l + 2, c]) for c in range(C)]
                        mm = exact_product(nc, b.ps[:, t, 0:FEAT], terms)
                    mm.then_inc(pe_done[s], 1)

                both = {f"hT_{l}": hT, f"u_{l}": u, f"aT_{l}": aT, f"lin_{l}": lin}
                if directed:
                    return {**both, f"agg0_{l}": agg_t(0), f"agg1_{l}": agg_t(1)}
                return {**both, f"ml_{l}": ml, f"mr_{l}": mr, f"agg_{l}": agg}

            run_stages(pe, order, {**layer(0), **layer(1)})


def graph_stack(nc, x, adj, adj_t, w0, w1, w2, w3, rows0, rows1, rows2, rows3, ident, tri, part_rows,
                part_cols, out):
    with ExitStack() as ctx:
        def sb(name, shape, dt=F32):
            return ctx.enter_context(nc.sbuf_tensor(name, shape, dt))

        def sem(name):
            return ctx.enter_context(nc.semaphore(name))
        g = Shared()
        g.ident = sb("ident", [P, P])
        g.tri = sb("tri", [P, 2, NODES])
        g.part_rows = sb("part_rows", [P, 3, NODES])
        g.part_cols = sb("part_cols", [P, 3, P])
        g.neg_half = sb("neg_half", [P, T])
        g.pos_half = sb("pos_half", [P, T])
        g.ones = sb("ones", [P, T, NODES])
        g.mark = sb("mark", [P, STREAMS])
        g.pad = sb("pad", [P, 1])
        g.w_hi = sb("w_hi", [P, MATS, C, FEAT], F32R)
        g.w_lo = sb("w_lo", [P, MATS, C, FEAT], F32R)
        g.w_raw = sb("w_raw", [P, MATS, C, FEAT])
        g.ps = [ctx.enter_context(nc.psum_tensor(f"ps{s}", [P, 4, BANK], F32)) for s in range(STREAMS)]
        g.weights = [w.rearrange("m (c p) o -> p m c o", p=P) for w in (w0, w1, w2, w3)]
        g.weights_in = [sem(f"weights_in{k}") for k in range(4)]
        g.hi_split = [sem(f"hi_split{k}") for k in range(4)]
        g.lo_split = [sem(f"lo_split{k}") for k in range(4)]
        g.powers = sem("powers")
        g.const_in = sem("const_in")
        g.const_loads = [(g.ident[:], ident), (g.tri[:], tri), (g.part_rows[:], part_rows),
                         (g.part_cols[:], part_cols)]
        g.const_count = 16 * len(g.const_loads)

        def groups(a):
            return a.rearrange("b s f -> (b s) f").rearrange("(n t p) f -> n p t f", t=T, p=P)
        between = [nc.dram_tensor(f"x_after_{k}", (GRAPHS, NODES, FEAT), F32, kind="Internal").ap()
                   for k in range(3)]
        xs = [groups(a) for a in [x] + between + [out]]
        a_n, a_t = groups(adj), groups(adj_t)
        gcn_phase(nc, g, 0, False, xs[0], xs[1], [a_n, a_t], [[r[l] for r in rows0] for l in range(2)])
        attention_phase(nc, g, 1, 2, xs[1], xs[2], a_n, *rows1)
        attention_phase(nc, g, 2, 1, xs[2], xs[3], a_n, *rows2)
        gcn_phase(nc, g, 3, True, xs[3], xs[4], [a_n], [[r[l] for r in rows3] for l in range(2)])


def kernel(**inputs):
    import concourse.bacc as bacc
    from concourse.bass_utils import run_bass_kernel_spmd

    def f(name):
        return np.asarray(inputs[name])

    def transposed(names, layers=None):
        if layers is None:
            return np.ascontiguousarray(np.stack([f(n).T for n in names]))
        return np.ascontiguousarray(np.stack([f(n)[l].T for l in range(layers) for n in names]))

    i, j = np.arange(NODES)[:, None], np.arange(NODES)[None, :]
    above, on, below = (j > i), (j == i), (j < i)
    tri = np.stack([above | on, below]).astype(np.float32) / np.float32(np.sqrt(FEAT))
    part_rows = np.stack([above, on, below]).astype(np.float32)
    blocks = np.zeros((P, 3, P), np.float32)
    for k in range(P // NODES):
        at = slice(k * NODES, (k + 1) * NODES)
        blocks[at, :, at] = part_rows.transpose(2, 0, 1)
    arrays = {
        "x": np.ascontiguousarray(f("x")),
        "adj": np.ascontiguousarray(f("adj")),
        "adj_t": np.ascontiguousarray(f("adj").transpose(0, 2, 1)),
        "w0": transposed(["L0_gnn_W_left", "L0_gnn_W_right", "L0_gnn_W_lin"], 2),
        "w1": transposed([f"L1_gnn_W{c}" for c in "qkvo"]),
        "w2": transposed([f"L2_gnn_W{c}" for c in "qkvo"]),
        "w3": transposed(["L3_gnn_Wl", "L3_gnn_Ws", "L3_gnn_Wr"], 2),
        "ident": np.eye(P, dtype=np.float32),
        "tri": np.ascontiguousarray(np.tile(tri.transpose(1, 0, 2), (P // NODES, 1, 1))),
        "part_rows": np.ascontiguousarray(np.tile(part_rows.transpose(1, 0, 2), (P // NODES, 1, 1))),
        "part_cols": blocks,
    }
    rows = [["L0_gnn_b_lin", "L0_gnn_ln_a", "L0_gnn_ln_b"], ["L1_gnn_bv", "L1_gnn_bo"],
            ["L2_gnn_bv", "L2_gnn_bo"], ["L3_gnn_bl", "L3_gnn_bs", "L3_gnn_br", "L3_gnn_ln_w", "L3_gnn_ln_b"]]
    for names in rows:
        for name in names:
            arrays[name] = np.ascontiguousarray(f(name))

    nc = bacc.Bacc("TRN2", target_bir_lowering=False, num_devices=1)
    at = {name: nc.dram_tensor(f"in_{name}", a.shape, mybir.dt.from_np(a.dtype), kind="ExternalInput").ap()
          for name, a in arrays.items()}
    out = nc.dram_tensor("out", (GRAPHS, NODES, FEAT), F32, kind="ExternalOutput").ap()
    graph_stack(nc, at["x"], at["adj"], at["adj_t"], at["w0"], at["w1"], at["w2"], at["w3"],
                *[[at[name] for name in names] for names in rows],
                at["ident"], at["tri"], at["part_rows"], at["part_cols"], out)
    got = run_bass_kernel_spmd(nc, [{f"in_{name}": a for name, a in arrays.items()}], core_ids=[0])
    return got.results[0]["out"]
```

```python
from contextlib import ExitStack

import numpy as np

import concourse.bass as bass
from concourse import mybir

GRAPHS, NODES, FEAT = 128, 64, 384
P = 128
C = FEAT // P
T = 2
TOK = T * P
STREAMS = 2
GROUPS = GRAPHS * NODES // TOK
ITER = GROUPS // STREAMS
HEADS = 12
HD = FEAT // HEADS
HT = HEADS * T
HPC = P // HD
BANK = 512
MATS = 6
LN_EPS = 1e-5
BEHIND_GCN0, BEHIND_ATT, BEHIND_GCN3 = 0.245, 0.494, 0.717

ATT_STAGES = [
    ("stat", None, None, 0.2909, 0.1352), ("bias", None, None, None, 0.4833),
    ("norm", None, 0.3372, None, None), ("hT", 0.4899, 0.4810, 0.3621, None),
    ("q", 0.5068, 0.6152, None, None), ("k", 0.5091, None, 0.6249, None), ("v", 0.6110, None, 0.7804, None),
    ("scores", 0.9019, None, None, None), ("soft_a", None, None, 0.8494, None),
    ("soft_b", None, 1.0656, 0.9224, None), ("soft_c", None, None, 1.0536, 1.0966),
    ("pt0", 1.1250, 1.1496, None, None), ("pt1", 1.1364, None, 1.0755, None),
    ("pt2", 1.1758, 1.1746, None, None), ("pt3", 1.2121, None, 1.1563, None),
    ("pt4", 1.2149, 1.1766, None, None), ("pt5", 1.3312, None, 1.2231, None),
    ("pv", 1.3954, 1.1879, 1.3164, None), ("out", 1.4074, None, 1.4285, None),
    ("xb", None, None, None, 0.6009),
]
GCN0_STAGES = [
    ("stat", None, None, 0.2442, 0.1339), ("adj", None, None, None, 0.8520),
    ("norm", None, 0.5055, None, None), ("hT_0", 0.5764, 0.5727, 0.6205, None),
    ("ml_0", 0.7062, 0.7476, None, None), ("mr_0", 0.7667, None, 0.8063, None),
    ("lin_0", 0.8542, None, 0.9453, None), ("u_0", 0.9437, None, None, None),
    ("soft_0", None, 0.8709, 0.9375, None), ("att_0", None, None, 0.9439, None),
    ("aT_0", 0.9856, None, 0.9512, None), ("agg_0", 0.9909, None, 1.0278, 1.0632),
    ("ln_0", None, 1.0378, 1.0308, None), ("hT_1", 1.1405, 1.1150, 1.1651, None),
    ("ml_1", 1.1973, 1.1792, None, None), ("mr_1", 1.2512, None, 1.3425, None),
    ("lin_1", 1.3653, None, 1.3813, None), ("u_1", 1.4115, None, None, None),
    ("soft_1", None, 1.4160, 1.4802, None), ("att_1", None, None, 1.4837, None),
    ("aT_1", 1.4960, None, 1.5039, None), ("agg_1", 1.5258, None, 1.5933, 1.6737),
    ("ln_1", None, None, 1.7338, None), ("x", None, None, None, 1.0354),
]
GCN3_STAGES = [
    ("stat", None, None, 0.0455, 0.0189), ("adj", None, None, None, 0.0734),
    ("norm", None, 0.1339, None, None), ("hT_0", 0.1753, 0.1451, 0.1160, None),
    ("w0_0", 0.2706, None, 0.2336, None), ("u_0", 0.2737, None, None, None),
    ("w1_0", 0.3194, 0.3893, None, 0.4572), ("w2_0", 0.4227, None, 0.3840, None),
    ("soft_0", None, 0.4082, 0.3050, None), ("att_0", None, None, 0.3385, None),
    ("aT_0", 0.4360, None, 0.3910, None), ("agg_0", 0.4899, None, 0.4787, 0.4661),
    ("ln_0", None, 0.7767, 0.5986, None), ("hT_1", 0.7390, 0.7770, 0.7451, None),
    ("w0_1", 0.8509, None, 0.8238, None), ("u_1", 0.9738, None, None, None),
    ("w1_1", 1.0030, 1.0602, None, 1.0236), ("w2_1", 1.0957, None, 1.0944, None),
    ("soft_1", None, 1.0083, 0.8564, None), ("att_1", None, None, 1.0192, None),
    ("aT_1", 1.1183, None, 1.0713, None), ("agg_1", 1.1923, None, 1.1190, 1.1855),
    ("ln_1", None, None, 1.2528, None), ("x", None, None, None, 0.7494),
]

ALU = mybir.AluOpType
ACT = mybir.ActivationFunctionType
F32 = mybir.dt.float32
F32R = mybir.dt.float32r
AX = mybir.AxisListType


class Count:

    def __init__(self, order, s, stages):
        self.late = {}
        self.place = {}
        for stage, stream, late in order:
            if stream == s:
                for name in stages.get(stage, []):
                    self.place[name] = len(self.place) + 1
                    self.late[name] = late
        self.missing = sum(self.late.values())

    def all(self, i, *events):
        there = [(name, back) for name, back in events if not isinstance(i, int) or i >= back]
        name, back = max(there, key=lambda event: (self.late[event[0]] - event[1], self.place[event[0]]))
        return self(name, i - back)

    def __call__(self, name, i):
        turn = i + self.late[name]
        if isinstance(turn, int) and turn in (0, ITER):
            here = sum(self.late[n] == (turn > 0) for n in self.place if self.place[n] <= self.place[name])
            return here + (ITER * len(self.place) - self.missing if turn else 0)
        return turn * len(self.place) + (self.place[name] - self.missing)


def stage_orders(stages, behind):
    orders = []
    for engine in range(1, 5):
        order = []
        for s in range(STREAMS):
            for k, stage in enumerate(stages):
                if stage[engine] is not None:
                    at = stage[engine] + s * behind
                    assert 0 <= at < 2
                    order.append((at % 1, s, k, stage[0], int(at)))
        orders.append([(name, s, late) for _, s, _, name, late in sorted(order)])
    return orders


def counts(order, stages):
    return [Count(order, s, stages) for s in range(STREAMS)]


def run_stages(eng, order, todo):
    order = [(todo[stage], s, late) for stage, s, late in order if stage in todo]

    def round_of(r):
        for stage, s, late in order:
            if not isinstance(r, int) or 0 <= r - late < ITER:
                stage(s, r - late)
    round_of(0)
    round_of(1)
    with eng.Fori(2, ITER) as r:
        round_of(r)
    round_of(ITER)


def later(i):
    return not isinstance(i, int) or i > 0


def head_tile(t, h):
    return (h % HPC) * T * C + t * C + h // HPC


def exact_product(nc, out, terms):
    for k, (lhs_hi, lhs_lo, rhs_hi, rhs_lo) in enumerate(terms):
        nc.tensor.matmul(out, lhs_hi, rhs_hi, start=(k == 0), stop=False)
        nc.tensor.matmul(out, lhs_hi, rhs_lo, start=False, stop=False)
        last = nc.tensor.matmul(out, lhs_lo, rhs_hi, start=False, stop=(k == len(terms) - 1))
    return last


class Shared:
    pass


def weight_split(nc, g, phase, n_mats, act, dve):
    if act is not None:
        act.wait_ge(g.weights_in[phase], 16)
        for m in range(n_mats):
            nc.scalar.activation(g.w_hi[:, m], g.w_raw[:, m], ACT.Copy).then_inc(g.hi_split[phase], 1)
    if dve is not None:
        dve.wait_ge(g.weights_in[phase], 16)
        for m in range(n_mats):
            dve.wait_ge(g.hi_split[phase], m + 1)
            nc.vector.tensor_tensor(g.w_lo[:, m], g.w_raw[:, m], g.w_hi[:, m].bitcast(F32),
                                    ALU.subtract).then_inc(g.lo_split[phase], 1)


def move_program(nc, sp, g, phase, n_mats, rows, x_in, x_out, adj_list, bufs, sems, x_free, x_new):
    for dst, src in rows:
        sp.dma_start(dst, src.partition_broadcast(P)).then_inc(sems.params_in, 16)

    def load(s, i):
        group = i * STREAMS + s
        sp.dma_start(bufs[s].xin[:], x_in[group]).then_inc(sems.x_in[s], 16)
        for k, a in enumerate(adj_list):
            sp.dma_start(bufs[s].adjin[:, k], a[group]).then_inc(sems.adj_in[s], 16)

    def store(s, i):
        x_new(s, i)
        sp.dma_start(x_out[i * STREAMS + s], bufs[s].xout[:]).then_inc(sems.stored[s], 16)

    for s in range(STREAMS):
        load(s, 0)
    if phase + 1 < len(g.weights):
        sp.wait_ge(g.hi_split[phase], n_mats)
        sp.wait_ge(g.lo_split[phase], n_mats)
        nxt = g.weights[phase + 1]
        sp.dma_start(g.w_raw[:, :nxt.shape[1]], nxt).then_inc(g.weights_in[phase + 1], 16)

    def turn(i):
        for s in range(STREAMS):
            x_free(s, i - 1)
            load(s, i)
        for s in range(STREAMS):
            store(s, i - 1)
    turn(1)
    with sp.Fori(2, ITER) as i:
        turn(i)
    for s in range(STREAMS):
        store(s, ITER - 1)
    for s in range(STREAMS):
        sp.wait_ge(sems.stored[s], 16 * ITER + 1)


class Sems:
    pass


class Buf:
    pass


def phase_sems(nc, ctx, phase):
    m = Sems()

    def sem(name):
        return ctx.enter_context(nc.semaphore(f"{name}_{phase}"))
    m.params_in = sem("params_in")
    m.start_zero = sem("start_zero")
    m.factor_set = sem("factor_set")
    m.x_in, m.adj_in, m.stored, m.pe_done, m.act_done, m.dve_done, m.pool_done = (
        [sem(f"{name}{s}") for s in range(STREAMS)]
        for name in ("x_in", "adj_in", "stored", "pe_done", "act_done", "dve_done", "pool_done"))
    return m


def attention_phase(nc, g, phase, bias_times, x_in, x_out, adj, bv, bo):
    SCALE = float(FEAT) ** -0.5
    WQ, WK, WV, WO = range(4)
    pe_order, act_order, dve_order, pool_order = stage_orders(ATT_STAGES, BEHIND_ATT)
    PE = counts(pe_order, {n: [n] for n in ["hT", "q", "k", "v", "scores", "pt0", "pt1", "pt2", "pt3", "pt4",
                                         "pt5", "pv", "out"]})
    AC = counts(act_order, {"norm": ["h"], "hT": ["hT_hi"], "q": ["q"], "soft_b": ["e"], "pt0": ["pt0"],
                        "pt2": ["pt2"], "pt4": ["pt4"], "pv": ["oT_hi"]})
    DV = counts(dve_order, {"stat": ["stats", "aggr", "var", "shift"], "hT": ["hT_lo"], "k": ["k"], "v": ["v"],
                        "soft_a": ["s", "max"], "soft_b": ["absmax", "diff"],
                        "soft_c": ["sum", "rsum", "factor", "p"], "pt1": ["pt1"], "pt3": ["pt3"],
                        "pt5": ["pt5"], "pv": ["oT_lo"], "out": ["xout"]})
    PO = counts(pool_order, {"stat": ["rstd"], "bias": ["bias"], "xb": ["xb"], "soft_c": ["p"]})

    with ExitStack() as ctx:
        def sb(name, shape, dt=F32):
            return ctx.enter_context(nc.sbuf_tensor(f"{name}_{phase}", shape, dt))
        sems = phase_sems(nc, ctx, phase)
        pe_done, act_done, dve_done, pool_done = sems.pe_done, sems.act_done, sems.dve_done, sems.pool_done
        bv_row = sb("bv_row", [P, FEAT])
        bo_row = sb("bo_row", [P, FEAT])
        bias_factor = sb("bias_factor", [P, T, NODES])
        bufs = []
        for s in range(STREAMS):
            b = Buf()
            b.xin = sb(f"xin{s}", [P, T, FEAT])
            b.adjin = sb(f"adjin{s}", [P, 1, T, NODES])
            b.xb = sb(f"xb{s}", [P, T, FEAT])
            b.bias = sb(f"bias{s}", [P, T, NODES])
            b.x_st = sb(f"x_st{s}", [P, T, 6])
            b.x_mv = sb(f"x_mv{s}", [P, T, 2])
            b.x_rstd = sb(f"x_rstd{s}", [P, T])
            b.x_shift = sb(f"x_shift{s}", [P, T])
            b.h = sb(f"h{s}", [P, T, FEAT])
            b.t_hi = sb(f"t_hi{s}", [P, C, TOK], F32R)
            b.t_lo = sb(f"t_lo{s}", [P, C, TOK], F32R)
            b.q = sb(f"q{s}", [P, C, TOK])
            b.k = sb(f"k{s}", [P, C, TOK])
            b.v = sb(f"v{s}", [P, T, FEAT])
            b.s = sb(f"s{s}", [P, HT, NODES])
            b.max = sb(f"max{s}", [P, HT])
            b.absmax = sb(f"absmax{s}", [P, HT])
            b.sum = sb(f"sum{s}", [P, HT])
            b.rsum = sb(f"rsum{s}", [P, HT])
            b.factor = sb(f"factor{s}", [P, HT])
            b.p = sb(f"p{s}", [P, HT, P])
            b.pT = sb(f"pT{s}", [P, HT, P])
            b.xout = sb(f"xout{s}", [P, T, FEAT])
            b.ps = g.ps[s]
            b.ps_row = b.ps[:, 0:2, :].rearrange("p a b -> p (a b)")[:, 0:C * TOK].rearrange(
                "p (c t) -> p c t", c=C)
            b.ps_row2 = b.ps[:, 2:4, :].rearrange("p a b -> p (a b)")[:, 0:C * TOK].rearrange(
                "p (c t) -> p c t", c=C)
            b.ps_s = b.ps[:, :, 0:T * C * NODES].rearrange("p r (t c k) -> p r t c k", t=T, c=C)
            bufs.append(b)

        block = ctx.enter_context(nc.Block())

        @block.sync
        def _(sp):
            def x_free(s, i):
                sp.wait_ge(pool_done[s], PO[s].all(i, ("xb", 0), ("bias", 0)))
                sp.wait_ge(act_done[s], AC[s]("h", i))

            def x_new(s, i):
                sp.wait_ge(dve_done[s], DV[s]("xout", i))
            move_program(nc, sp, g, phase, 4, [(bv_row[:], bv), (bo_row[:], bo)], x_in, x_out, [adj], bufs,
                         sems, x_free, x_new)

        @block.gpsimd
        def _(pool):
            pool.wait_ge(sems.params_in, 32)
            nc.gpsimd.memset(bias_factor[:], bias_times / SCALE).then_inc(sems.factor_set, 1)
            pool.wait_ge(sems.factor_set, 1)

            def stat(s, i):
                b = bufs[s]
                pool.wait_ge(dve_done[s], DV[s]("var", i))
                nc.gpsimd.tensor_tensor(b.x_rstd[:], b.x_rstd[:], g.neg_half[:, 0:T],
                                        ALU.pow).then_inc(pool_done[s], 1)
                pool.wait_ge(pool_done[s], PO[s]("rstd", i))

            def bias(s, i):
                b = bufs[s]
                pool.wait_ge(sems.adj_in[s], 16 * (i + 1))
                if later(i):
                    pool.wait_ge(dve_done[s], DV[s]("s", i - 1))
                nc.gpsimd.tensor_tensor(b.bias[:], b.adjin[:, 0], bias_factor[:], ALU.mult)\
                    .then_inc(pool_done[s], 1)
                pool.wait_ge(pool_done[s], PO[s]("bias", i))

            def xb(s, i):
                b = bufs[s]
                pool.wait_ge(sems.x_in[s], 16 * (i + 1))
                if later(i):
                    pool.wait_ge(dve_done[s], DV[s]("xout", i - 1))
                nc.gpsimd.tensor_tensor(b.xb[:], b.xin[:], bo_row[:].unsqueeze(1).broadcast_to([P, T, FEAT]),
                                        ALU.add).then_inc(pool_done[s], 1)
                pool.wait_ge(pool_done[s], PO[s]("xb", i))

            def soft_c(s, i):
                b = bufs[s]
                pool.wait_ge(dve_done[s], DV[s]("factor", i))
                nc.gpsimd.tensor_tensor(b.p[NODES:P, :, NODES:P], b.s[NODES:P],
                                        b.factor[NODES:P].unsqueeze(2).broadcast_to([NODES, HT, NODES]),
                                        ALU.mult).then_inc(pool_done[s], 1)
                pool.wait_ge(pool_done[s], PO[s]("p", i))

            run_stages(pool, pool_order, {"stat": stat, "bias": bias, "xb": xb, "soft_c": soft_c})

        @block.scalar
        def _(act):
            weight_split(nc, g, phase, 4, act, None)

            def norm(s, i):
                b = bufs[s]
                act.wait_ge(dve_done[s], DV[s]("shift", i))
                if later(i):
                    act.wait_ge(pe_done[s], PE[s]("hT", i - 1))
                for t in range(T):
                    ins = nc.scalar.activation(b.h[:, t], b.xin[:, t], ACT.Relu, bias=b.x_shift[:, t:t + 1],
                                               scale=b.x_rstd[:, t:t + 1])
                ins.then_inc(act_done[s], 1)

            def hT(s, i):
                b = bufs[s]
                act.wait_ge(pe_done[s], PE[s].all(i, ("hT", 0), ("out", 1)))
                nc.scalar.activation(b.t_hi[:], b.ps_row, ACT.Copy).then_inc(act_done[s], 1)

            def q(s, i):
                b = bufs[s]
                act.wait_ge(pe_done[s], PE[s]("q", i))
                nc.scalar.activation(b.q[:], b.ps_row, ACT.Copy).then_inc(act_done[s], 1)

            def soft_b(s, i):
                b = bufs[s]
                act.wait_ge(dve_done[s], DV[s]("diff", i))
                nc.scalar.activation(b.s[:], b.s[:], ACT.Exp, scale=SCALE).then_inc(act_done[s], 1)

            def pt(u):
                def stage(s, i):
                    b = bufs[s]
                    act.wait_ge(pe_done[s], PE[s](f"pt{u}", i))
                    nc.scalar.activation(b.pT[:, 4 * u:4 * u + 4], b.ps[:, u % 4, :], ACT.Copy)\
                        .then_inc(act_done[s], 1)
                return stage

            def pv(s, i):
                b = bufs[s]
                act.wait_ge(pe_done[s], PE[s]("pv", i))
                nc.scalar.activation(b.t_hi[:], b.ps_row2, ACT.Copy).then_inc(act_done[s], 1)

            run_stages(act, act_order, {"norm": norm, "hT": hT, "q": q, "soft_b": soft_b, "pt0": pt(0),
                                    "pt2": pt(2), "pt4": pt(4), "pv": pv})

        @block.vector
        def _(dve):
            weight_split(nc, g, phase, 4, None, dve)
            for s in range(STREAMS):
                nc.vector.memset(bufs[s].p[:], 0.0).then_inc(sems.start_zero, 1)
                nc.vector.memset(g.mark[:, s:s + 1], 0.0).then_inc(sems.stored[s], 1)
            dve.wait_ge(sems.params_in, 32)
            dve.wait_ge(sems.start_zero, STREAMS)

            def stat(s, i):
                b = bufs[s]
                dve.wait_ge(sems.x_in[s], 16 * (i + 1))
                for t in range(T):
                    ins = nc.vector.bn_stats(b.x_st[:, t], b.xin[:, t])
                ins.then_inc(dve_done[s], 1)
                dve.wait_ge(dve_done[s], DV[s]("stats", i))
                nc.vector.memset(g.pad[:], 0.0)
                for t in range(T):
                    ins = nc.vector.bn_aggr(b.x_mv[:, t], b.x_st[:, t])
                ins.then_inc(dve_done[s], 1)
                dve.wait_ge(dve_done[s], DV[s]("aggr", i))
                nc.vector.tensor_scalar(b.x_rstd[:], b.x_mv[:, :, 1], LN_EPS, None, ALU.add)\
                    .then_inc(dve_done[s], 1)
                dve.wait_ge(pool_done[s], PO[s]("rstd", i))
                nc.vector.scalar_tensor_tensor(b.x_shift[:], b.x_mv[:, :, 0], -1.0, b.x_rstd[:], ALU.mult,
                                               ALU.mult).then_inc(dve_done[s], 1)

            def hT(s, i):
                b = bufs[s]
                dve.wait_ge(act_done[s], AC[s]("hT_hi", i))
                nc.vector.tensor_tensor(b.t_lo[:], b.ps_row, b.t_hi[:].bitcast(F32), ALU.subtract)\
                    .then_inc(dve_done[s], 1)

            def k(s, i):
                b = bufs[s]
                dve.wait_ge(pe_done[s], PE[s]("k", i))
                nc.vector.tensor_copy(b.k[:], b.ps_row2).then_inc(dve_done[s], 1)

            def v(s, i):
                b = bufs[s]
                dve.wait_ge(pe_done[s], PE[s]("v", i))
                nc.vector.tensor_tensor(b.v[:], b.ps[:, 0:2, 0:FEAT],
                                        bv_row[:].unsqueeze(1).broadcast_to([P, T, FEAT]),
                                        ALU.add).then_inc(dve_done[s], 1)

            def soft_a(s, i):
                b = bufs[s]
                dve.wait_ge(pe_done[s], PE[s]("scores", i))
                dve.wait_ge(pool_done[s], PO[s]("bias", i))
                for t in range(T):
                    ins = nc.vector.tensor_tensor(
                        b.s[:].rearrange("p (r t c) k -> p r t c k", r=HPC, t=T)[:, :, t], b.ps_s[:, :, t],
                        b.bias[:, t:t + 1].unsqueeze(1).broadcast_to([P, HPC, C, NODES]), ALU.add)
                ins.then_inc(dve_done[s], 1)
                dve.wait_ge(dve_done[s], DV[s]("s", i))
                nc.vector.tensor_reduce(b.max[:], b.s[:], AX.X, ALU.max).then_inc(dve_done[s], 1)

            def soft_b(s, i):
                b = bufs[s]
                nc.vector.tensor_reduce(b.absmax[:], b.s[:], AX.X, ALU.max, apply_absolute_value=True)\
                    .then_inc(dve_done[s], 1)
                dve.wait_ge(dve_done[s], DV[s]("absmax", i))
                nc.vector.tensor_tensor(b.s[:], b.s[:], b.max[:].unsqueeze(2).broadcast_to([P, HT, NODES]),
                                        ALU.subtract).then_inc(dve_done[s], 1)

            def soft_c(s, i):
                b = bufs[s]
                dve.wait_ge(act_done[s], AC[s]("e", i))
                nc.vector.tensor_reduce(b.sum[:], b.s[:], AX.X, ALU.add).then_inc(dve_done[s], 1)
                dve.wait_ge(dve_done[s], DV[s]("sum", i))
                nc.vector.reciprocal(b.rsum[:], b.sum[:]).then_inc(dve_done[s], 1)
                dve.wait_ge(dve_done[s], DV[s]("rsum", i))
                nc.vector.scalar_tensor_tensor(b.factor[:], b.absmax[:], 0.0, b.rsum[:], ALU.not_equal,
                                               ALU.mult).then_inc(dve_done[s], 1)
                dve.wait_ge(dve_done[s], DV[s]("factor", i))
                nc.vector.tensor_tensor(b.p[0:NODES, :, 0:NODES], b.s[0:NODES],
                                        b.factor[0:NODES].unsqueeze(2).broadcast_to([NODES, HT, NODES]),
                                        ALU.mult).then_inc(dve_done[s], 1)

            def pt(u):
                def stage(s, i):
                    b = bufs[s]
                    dve.wait_ge(pe_done[s], PE[s](f"pt{u}", i))
                    nc.vector.tensor_copy(b.pT[:, 4 * u:4 * u + 4],
                                          b.ps[:, u % 4, :].rearrange("p (h k) -> p h k", k=P))\
                        .then_inc(dve_done[s], 1)
                return stage

            def pv(s, i):
                b = bufs[s]
                dve.wait_ge(act_done[s], AC[s]("oT_hi", i))
                nc.vector.tensor_tensor(b.t_lo[:], b.ps_row2, b.t_hi[:].bitcast(F32), ALU.subtract)\
                    .then_inc(dve_done[s], 1)

            def out(s, i):
                b = bufs[s]
                dve.wait_ge(pe_done[s], PE[s]("out", i))
                dve.wait_ge(pool_done[s], PO[s]("xb", i))
                dve.wait_ge(sems.stored[s], 16 * i + 1)
                nc.vector.tensor_tensor(b.xout[:], b.ps[:, 2:4, 0:FEAT], b.xb[:], ALU.add)\
                    .then_inc(dve_done[s], 1)

            run_stages(dve, dve_order, {"stat": stat, "hT": hT, "k": k, "v": v, "soft_a": soft_a,
                                    "soft_b": soft_b, "soft_c": soft_c, "pt1": pt(1), "pt3": pt(3),
                                    "pt5": pt(5), "pv": pv, "out": out})

        @block.tensor
        def _(pe):
            pe.wait_ge(g.hi_split[phase], 4)
            pe.wait_ge(g.lo_split[phase], 4)
            pe.wait_ge(g.const_in, g.const_count)

            def hT(s, i):
                b = bufs[s]
                pe.wait_ge(act_done[s], AC[s].all(i, ("h", 0), ("pt4", 1)))
                if later(i):
                    pe.wait_ge(dve_done[s], DV[s]("pt5", i - 1))
                for c in range(C):
                    for t in range(T):
                        mm = nc.tensor.transpose(b.ps_row[:, c, t * P:(t + 1) * P],
                                                 b.h[:, t, c * P:(c + 1) * P], g.ident[:])
                mm.then_inc(pe_done[s], 1)

            def project_T(b, out, m):
                for o in range(C):
                    mm = exact_product(nc, out[:, o], [
                        (g.w_hi[:, m, c, o * P:(o + 1) * P], g.w_lo[:, m, c, o * P:(o + 1) * P],
                         b.t_hi[:, c], b.t_lo[:, c]) for c in range(C)])
                return mm

            def project(b, banks, m):
                for t in range(T):
                    mm = exact_product(nc, b.ps[:, banks + t, 0:FEAT], [
                        (b.t_hi[:, c, t * P:(t + 1) * P], b.t_lo[:, c, t * P:(t + 1) * P],
                         g.w_hi[:, m, c], g.w_lo[:, m, c]) for c in range(C)])
                return mm

            def q(s, i):
                pe.wait_ge(act_done[s], AC[s]("hT_hi", i))
                pe.wait_ge(dve_done[s], DV[s]("hT_lo", i))
                project_T(bufs[s], bufs[s].ps_row, WQ).then_inc(pe_done[s], 1)

            def k(s, i):
                if later(i):
                    pe.wait_ge(dve_done[s], DV[s]("xout", i - 1))
                project_T(bufs[s], bufs[s].ps_row2, WK).then_inc(pe_done[s], 1)

            def v(s, i):
                pe.wait_ge(act_done[s], AC[s]("q", i))
                project(bufs[s], 0, WV).then_inc(pe_done[s], 1)

            def scores(s, i):
                b = bufs[s]
                pe.wait_ge(dve_done[s], DV[s]("v", i))
                for t in range(T):
                    for h in range(HEADS):
                        r = HD * (h % HPC)
                        for gr in range(2):
                            at = t * P + gr * NODES
                            mm = nc.tensor.matmul(b.ps_s[gr * NODES:(gr + 1) * NODES, h % HPC, t, h // HPC],
                                                  b.q[r:r + HD, h // HPC, at:at + NODES],
                                                  b.k[r:r + HD, h // HPC, at:at + NODES],
                                                  start=True, stop=True)
                mm.then_inc(pe_done[s], 1)

            def pt(u):
                def stage(s, i):
                    b = bufs[s]
                    if u == 0:
                        pe.wait_ge(dve_done[s], DV[s]("p", i))
                        pe.wait_ge(pool_done[s], PO[s]("p", i))
                    if u >= 4:
                        if u % 2 == 0:
                            pe.wait_ge(act_done[s], AC[s](f"pt{u - 4}", i))
                        else:
                            pe.wait_ge(dve_done[s], DV[s](f"pt{u - 4}", i))
                    for j in range(4):
                        mm = nc.tensor.transpose(b.ps[:, u % 4, j * P:(j + 1) * P], b.p[:, 4 * u + j],
                                                 g.ident[:])
                    mm.then_inc(pe_done[s], 1)
                return stage

            def pv(s, i):
                b = bufs[s]
                pe.wait_ge(act_done[s], AC[s]("pt4", i))
                pe.wait_ge(dve_done[s], DV[s]("pt5", i))
                for t in range(T):
                    for h in range(HEADS):
                        r = HD * (h % HPC)
                        mm = nc.tensor.matmul(b.ps_row2[r:r + HD, h // HPC, t * P:(t + 1) * P],
                                              b.v[:, t, h * HD:(h + 1) * HD], b.pT[:, head_tile(t, h)],
                                              start=True, stop=True, tile_position=(0, r))
                mm.then_inc(pe_done[s], 1)

            def out(s, i):
                pe.wait_ge(act_done[s], AC[s]("oT_hi", i))
                pe.wait_ge(dve_done[s], DV[s]("oT_lo", i))
                project(bufs[s], 2, WO).then_inc(pe_done[s], 1)

            todo = {"hT": hT, "q": q, "k": k, "v": v, "scores": scores, "pv": pv, "out": out}
            todo.update({f"pt{u}": pt(u) for u in range(6)})
            run_stages(pe, pe_order, todo)


def gcn_phase(nc, g, phase, directed, x_in, x_out, adjs, params):
    TEMPER = float(np.sqrt(FEAT))
    n_adj = len(adjs)
    LEFT, RIGHT, LIN = range(3)
    UPPER, ON, LOWER = range(3)
    pe_order, act_order, dve_order, pool_order = stage_orders(GCN3_STAGES, BEHIND_GCN3) if directed else \
        stage_orders(GCN0_STAGES, BEHIND_GCN0)

    def both(stages_):
        return {f"{st}_{l}": [f"{name}_{l}" for name in names if (name[:6], l) != ("h_next", 1)]
                for l in range(2) for st, names in stages_.items()}

    if directed:
        PE = counts(pe_order, both({n: [n] for n in ["hT", "w0", "w1", "w2", "u", "aT", "agg"]}))
        AC = counts(act_order, {"norm": ["h"], **both({"hT": ["hT_hi", "hT"], "w1": ["w1"], "soft": ["e"],
                                                   "ln": ["h_next0", "h_next1"]})})
        events = both({"hT": ["hT_lo"], "w0": ["w0"], "w2": ["w2"], "soft": ["max", "diff"],
                       "att": ["sum", "rsum", "ea", "a", "asum", "asum_eps", "rasum", "att", "on", "on_sum",
                               "diag"],
                       "aT": ["aT"], "agg": ["ctx", "lstats", "laggr", "lvar", "cen"],
                       "ln": ["z0", "z1"]})
        PO = counts(pool_order, {"stat": ["rstd"], "adj": ["adj"], "x": ["x"],
                            **both({"w1": ["w1"], "agg": ["lstd"]})})
    else:
        PE = counts(pe_order, both({n: [n] for n in ["hT", "ml", "mr", "lin", "u", "aT", "agg"]}))
        AC = counts(act_order, {"norm": ["h"], **both({"hT": ["hT_hi", "hT"], "ml": ["ml"], "soft": ["e"],
                                                   "ln": ["h_next0", "h_next1"]})})
        events = both({"hT": ["hT_lo"], "mr": ["mr"], "lin": ["lin"], "soft": ["w", "u"],
                       "att": ["ea", "asum", "asum_eps", "rasum", "att"], "aT": ["aT"],
                       "agg": ["lstats", "laggr", "lvar", "cen"], "ln": ["lsig", "lrstd", "z0", "z1"]})
        PO = counts(pool_order, {"stat": ["rstd"], "adj": ["adj", "clr"], "x": ["x"], **both({"agg": ["lstd"]})})
    events["ln_1"].append("xout")
    DV = counts(dve_order, {"stat": ["stats", "aggr", "var", "shift"], **events})

    with ExitStack() as ctx:
        def sb(name, shape, dt=F32):
            return ctx.enter_context(nc.sbuf_tensor(f"{name}_{phase}", shape, dt))
        sems = phase_sems(nc, ctx, phase)
        pe_done, act_done, dve_done, pool_done = sems.pe_done, sems.act_done, sems.dve_done, sems.pool_done
        rows = [[sb(f"row{l}_{k}", [P, FEAT]) for k in range(len(params[l]))] for l in range(2)]
        bufs = []
        for s in range(STREAMS):
            b = Buf()
            b.xin = sb(f"xin{s}", [P, T, FEAT])
            b.adjin = sb(f"adjin{s}", [P, n_adj, T, NODES])
            b.x = sb(f"x{s}", [P, T, FEAT])
            b.adj = sb(f"adj{s}", [P, T, NODES])
            b.st = sb(f"st{s}", [P, T, 6])
            b.mv = sb(f"mv{s}", [P, T, 2])
            b.rstd = sb(f"rstd{s}", [P, T])
            b.x_st = sb(f"x_st{s}", [P, T, 6])
            b.x_mv = sb(f"x_mv{s}", [P, T, 2])
            b.x_rstd = sb(f"x_rstd{s}", [P, T])
            b.x_shift = sb(f"x_shift{s}", [P, T])
            b.h = sb(f"h{s}", [P, T, FEAT])
            b.t_hi = sb(f"t_hi{s}", [P, C, TOK], F32R)
            b.t_lo = sb(f"t_lo{s}", [P, C, TOK], F32R)
            b.hT = sb(f"hT{s}", [P, C, TOK])
            b.e = sb(f"e{s}", [P, T, NODES])
            b.asum = sb(f"asum{s}", [P, T])
            b.rasum = sb(f"rasum{s}", [P, T])
            b.a_bd = sb(f"a_bd{s}", [P, T, P])
            b.z = sb(f"z{s}", [P, T, FEAT])
            b.xout = sb(f"xout{s}", [P, T, FEAT])
            if directed:
                b.max = sb(f"max{s}", [P, T])
                b.sum = sb(f"sum{s}", [P, T])
                b.rsum = sb(f"rsum{s}", [P, T])
                b.on = sb(f"on{s}", [P, T, NODES])
                b.diag = sb(f"diag{s}", [P, T])
                b.aT = sb(f"aT{s}", [P, T, 2, P])
                b.hw = sb(f"hw{s}", [P, T, 3, FEAT])
            else:
                b.clr = sb(f"clr{s}", [P, T, 2, NODES])
                b.mlr = sb(f"mlr{s}", [P, C, 2, TOK])
                b.w = sb(f"w{s}", [P, T, 2, NODES])
                b.aT = sb(f"aT{s}", [P, T, P])
                b.hw = sb(f"hw{s}", [P, T, FEAT])
            b.ps = g.ps[s]
            b.ps_row = b.ps[:, 0:2, :].rearrange("p a b -> p (a b)")[:, 0:C * TOK].rearrange(
                "p (c t) -> p c t", c=C)
            b.ps_row2 = b.ps[:, 2:4, :].rearrange("p a b -> p (a b)")[:, 0:C * TOK].rearrange(
                "p (c t) -> p c t", c=C)
            b.ps_tiles = b.ps[:, 0, 0:T * P].rearrange("p (t i) -> p t i", t=T)
            if directed:
                b.ps_w = [b.ps[:, 2:4, 0:FEAT], b.ps[:, 1:3, 0:FEAT], b.ps[:, 1:4:2, 0:FEAT]]
            bufs.append(b)

        block = ctx.enter_context(nc.Block())

        @block.sync
        def _(sp):
            def x_free(s, i):
                sp.wait_ge(pool_done[s], PO[s].all(i, ("x", 0), ("adj" if directed else "clr", 0)))
                sp.wait_ge(act_done[s], AC[s]("h", i))

            def x_new(s, i):
                sp.wait_ge(dve_done[s], DV[s]("xout", i))
            if phase == 0:
                sp.dma_start(g.w_raw[:, :g.weights[0].shape[1]], g.weights[0]).then_inc(g.weights_in[0], 16)
                for dst, src in g.const_loads:
                    sp.dma_start(dst, src).then_inc(g.const_in, 16)
            pairs = [(rows[l][k][:], params[l][k]) for l in range(2) for k in range(len(params[l]))]
            move_program(nc, sp, g, phase, 6, pairs, x_in, x_out, adjs, bufs, sems, x_free,
                         x_new)

        n_rows = sum(len(p) for p in params)

        @block.gpsimd
        def _(pool):
            if phase == 0:
                nc.gpsimd.memset(g.neg_half[:], -0.5).then_inc(g.powers, 1)
                nc.gpsimd.memset(g.ones[:], 1.0).then_inc(g.powers, 1)
                nc.gpsimd.memset(g.pos_half[:], 0.5).then_inc(g.powers, 1)
            pool.wait_ge(g.powers, 3)
            pool.wait_ge(g.const_in, g.const_count)
            pool.wait_ge(sems.params_in, 16 * n_rows)

            def stat(s, i):
                b = bufs[s]
                pool.wait_ge(dve_done[s], DV[s]("var", i))
                nc.gpsimd.tensor_tensor(b.x_rstd[:], b.x_rstd[:], g.neg_half[:, 0:T],
                                        ALU.pow).then_inc(pool_done[s], 1)

            def adj(s, i):
                b = bufs[s]
                pool.wait_ge(sems.adj_in[s], 16 * n_adj * (i + 1))
                if later(i):
                    pool.wait_ge(dve_done[s], DV[s]("att_1", i - 1))
                nc.gpsimd.tensor_tensor(b.adj[:], b.adjin[:, 0], g.ones[:], ALU.mult)\
                    .then_inc(pool_done[s], 1)
                if not directed:
                    for k in range(2):
                        ins = nc.gpsimd.tensor_tensor(b.clr[:, :, k], b.adjin[:, k],
                                                      g.tri[:, k:k + 1].broadcast_to([P, T, NODES]), ALU.mult)
                    ins.then_inc(pool_done[s], 1)

            def x(s, i):
                b = bufs[s]
                if later(i):
                    pool.wait_ge(dve_done[s], DV[s]("xout", i - 1))
                pool.wait_ge(sems.x_in[s], 16 * (i + 1))
                nc.gpsimd.tensor_tensor(g.idle[:, s:s + 1], g.pos_half[:, 0:1], g.pos_half[:, 0:1], ALU.mult)
                nc.gpsimd.tensor_scalar(b.x[:], b.xin[:], 1.0, 0.0, ALU.mult, ALU.add)\
                    .then_inc(pool_done[s], 1)

            def layer(l):
                def w1(s, i):
                    b = bufs[s]
                    pool.wait_ge(act_done[s], AC[s](f"w1_{l}", i))
                    nc.gpsimd.tensor_tensor(b.hw[:, :, 1], b.hw[:, :, 1],
                                            rows[l][1][:].unsqueeze(1).broadcast_to([P, T, FEAT]),
                                            ALU.add).then_inc(pool_done[s], 1)

                def agg(s, i):
                    b = bufs[s]
                    pool.wait_ge(dve_done[s], DV[s](f"lvar_{l}", i))
                    nc.gpsimd.tensor_tensor(b.rstd[:], b.rstd[:], (g.neg_half if directed else g.pos_half)[:, 0:T],
                                            ALU.pow).then_inc(pool_done[s], 1)
                return {f"agg_{l}": agg, **({f"w1_{l}": w1} if directed else {})}

            run_stages(pool, pool_order, {"stat": stat, "adj": adj, "x": x, **layer(0), **layer(1)})

        @block.scalar
        def _(act):
            weight_split(nc, g, phase, 6, act, None)

            def norm(s, i):
                b = bufs[s]
                act.wait_ge(dve_done[s], DV[s]("shift", i))
                if later(i):
                    act.wait_ge(pe_done[s], PE[s]("hT_1", i - 1))
                for t in range(T):
                    ins = nc.scalar.activation(b.h[:, t], b.xin[:, t], ACT.Relu, bias=b.x_shift[:, t:t + 1],
                                               scale=b.x_rstd[:, t:t + 1])
                ins.then_inc(act_done[s], 1)

            def layer(l):
                def hT(s, i):
                    b = bufs[s]
                    used = [("u_1", 1), ("w2_1" if directed else "lin_1", 1)] if l == 0 else []
                    act.wait_ge(pe_done[s], PE[s].all(i, (f"hT_{l}", 0), *used))
                    nc.scalar.activation(b.t_hi[:], b.ps_row, ACT.Copy).then_inc(act_done[s], 1)
                    act.wait_ge(dve_done[s], DV[s](f"hT_lo_{l}", i))
                    nc.scalar.activation(b.hT[:], b.ps_row, ACT.Copy).then_inc(act_done[s], 1)

                def ml(s, i):
                    b = bufs[s]
                    act.wait_ge(pe_done[s], PE[s](f"ml_{l}", i))
                    nc.scalar.activation(b.mlr[:, :, 0], b.ps_row2, ACT.Copy).then_inc(act_done[s], 1)

                def w1(s, i):
                    b = bufs[s]
                    act.wait_ge(pe_done[s], PE[s](f"w1_{l}", i))
                    if l == 0 and later(i):
                        act.wait_ge(dve_done[s], DV[s]("ctx_1", i - 1))
                    nc.scalar.activation(b.hw[:, :, 1], b.ps_w[1], ACT.Copy).then_inc(act_done[s], 1)

                def soft(s, i):
                    b = bufs[s]
                    act.wait_ge(dve_done[s], DV[s](f"diff_{l}" if directed else f"u_{l}", i))
                    nc.scalar.activation(b.e[:], b.e[:], ACT.Exp, scale=1.0 / TEMPER if directed else 1.0)\
                        .then_inc(act_done[s], 1)

                def ln(s, i):
                    b = bufs[s]
                    for t in range(T):
                        act.wait_ge(dve_done[s], DV[s](f"z{t}_{l}", i))
                        nc.scalar.activation(b.h[:, t], b.z[:, t], ACT.Relu).then_inc(act_done[s], 1)

                todo = {f"hT_{l}": hT, f"soft_{l}": soft}
                todo.update({f"w1_{l}": w1} if directed else {f"ml_{l}": ml})
                todo.update({f"ln_{l}": ln} if l == 0 else {})
                return todo

            run_stages(act, act_order, {"norm": norm, **layer(0), **layer(1)})

        @block.vector
        def _(dve):
            weight_split(nc, g, phase, 6, None, dve)
            for s in range(STREAMS):
                nc.vector.memset(bufs[s].a_bd[:], 0.0).then_inc(sems.start_zero, 1)
                nc.vector.memset(g.mark[:, s:s + 1], 0.0).then_inc(sems.stored[s], 1)
            dve.wait_ge(g.const_in, g.const_count)
            dve.wait_ge(sems.params_in, 16 * n_rows)
            dve.wait_ge(sems.start_zero, STREAMS)

            def wait_own(s, name, i):
                dve.wait_ge(dve_done[s], DV[s](name, i))

            def stat(s, i):
                b = bufs[s]
                dve.wait_ge(sems.x_in[s], 16 * (i + 1))
                for t in range(T):
                    ins = nc.vector.bn_stats(b.x_st[:, t], b.xin[:, t])
                ins.then_inc(dve_done[s], 1)
                wait_own(s, "stats", i)
                nc.vector.memset(g.pad[:], 0.0)
                for t in range(T):
                    ins = nc.vector.bn_aggr(b.x_mv[:, t], b.x_st[:, t])
                ins.then_inc(dve_done[s], 1)
                wait_own(s, "aggr", i)
                nc.vector.tensor_scalar(b.x_rstd[:], b.x_mv[:, :, 1], LN_EPS, None, ALU.add)\
                    .then_inc(dve_done[s], 1)
                dve.wait_ge(pool_done[s], PO[s]("rstd", i))
                nc.vector.scalar_tensor_tensor(b.x_shift[:], b.x_mv[:, :, 0], -1.0, b.x_rstd[:], ALU.mult,
                                               ALU.mult).then_inc(dve_done[s], 1)

            def layer(l):
                def hT(s, i):
                    b = bufs[s]
                    dve.wait_ge(act_done[s], AC[s](f"hT_hi_{l}", i))
                    nc.vector.tensor_tensor(b.t_lo[:], b.ps_row, b.t_hi[:].bitcast(F32), ALU.subtract)\
                        .then_inc(dve_done[s], 1)

                def mr(s, i):
                    b = bufs[s]
                    dve.wait_ge(pe_done[s], PE[s](f"mr_{l}", i))
                    nc.vector.tensor_copy(b.mlr[:, :, 1], b.ps_row).then_inc(dve_done[s], 1)

                def lin(s, i):
                    b = bufs[s]
                    dve.wait_ge(pe_done[s], PE[s](f"lin_{l}", i))
                    nc.vector.tensor_tensor(b.hw[:], b.ps[:, 2:4, 0:FEAT],
                                            rows[l][0][:].unsqueeze(1).broadcast_to([P, T, FEAT]),
                                            ALU.add).then_inc(dve_done[s], 1)

                def w(m):
                    def stage(s, i):
                        b = bufs[s]
                        dve.wait_ge(pe_done[s], PE[s](f"w{m}_{l}", i))
                        nc.vector.tensor_tensor(b.hw[:, :, m], b.ps_w[m],
                                                rows[l][m][:].unsqueeze(1).broadcast_to([P, T, FEAT]),
                                                ALU.add).then_inc(dve_done[s], 1)
                    return stage

                def soft(s, i):
                    b = bufs[s]
                    dve.wait_ge(pe_done[s], PE[s](f"u_{l}", i))
                    if directed:
                        own = [(slice(q, q + NODES), b.ps_tiles[q:q + NODES, :, q:q + NODES])
                               for q in (0, NODES)]
                        for at, scores in own:
                            ins = nc.vector.tensor_reduce(b.max[at], scores, AX.X, ALU.max)
                        ins.then_inc(dve_done[s], 1)
                        wait_own(s, f"max_{l}", i)
                        for at, scores in own:
                            ins = nc.vector.tensor_tensor(b.e[at], scores,
                                                          b.max[at].unsqueeze(2).broadcast_to([NODES, T, NODES]),
                                                          ALU.subtract)
                        ins.then_inc(dve_done[s], 1)
                    else:
                        dve.wait_ge(pool_done[s], PO[s]("clr", i))
                        nc.vector.tensor_tensor(
                            b.w[:], b.ps[:, 0, 0:T * P].rearrange("p (t k j) -> p t k j", t=T, k=2),
                            b.clr[:], ALU.mult).then_inc(dve_done[s], 1)
                        wait_own(s, f"w_{l}", i)
                        nc.vector.tensor_tensor(b.e[:], b.w[:, :, 0], b.w[:, :, 1], ALU.add)\
                            .then_inc(dve_done[s], 1)

                def att(s, i):
                    b = bufs[s]
                    dve.wait_ge(act_done[s], AC[s](f"e_{l}", i))
                    if directed:
                        nc.vector.tensor_reduce(b.sum[:], b.e[:], AX.X, ALU.add).then_inc(dve_done[s], 1)
                        wait_own(s, f"sum_{l}", i)
                        nc.vector.reciprocal(b.rsum[:], b.sum[:]).then_inc(dve_done[s], 1)
                        dve.wait_ge(pool_done[s], PO[s]("adj", i))
                        nc.vector.tensor_tensor(b.e[:], b.e[:], b.adj[:], ALU.mult).then_inc(dve_done[s], 1)
                        wait_own(s, f"ea_{l}", i)
                        nc.vector.tensor_tensor(b.e[:], b.e[:],
                                                b.rsum[:].unsqueeze(2).broadcast_to([P, T, NODES]),
                                                ALU.mult).then_inc(dve_done[s], 1)
                        wait_own(s, f"a_{l}", i)
                    else:
                        nc.vector.tensor_tensor(b.e[:], b.e[:], b.adj[:], ALU.mult).then_inc(dve_done[s], 1)
                        wait_own(s, f"ea_{l}", i)
                    nc.vector.tensor_reduce(b.asum[:], b.e[:], AX.X, ALU.add).then_inc(dve_done[s], 1)
                    wait_own(s, f"asum_{l}", i)
                    nc.vector.tensor_scalar(b.asum[:], b.asum[:], 1e-10, None, ALU.add)\
                        .then_inc(dve_done[s], 1)
                    wait_own(s, f"asum_eps_{l}", i)
                    nc.vector.reciprocal(b.rasum[:], b.asum[:]).then_inc(dve_done[s], 1)
                    wait_own(s, f"rasum_{l}", i)
                    for q in (0, NODES):
                        ins = nc.vector.tensor_tensor(
                            b.a_bd[q:q + NODES, :, q:q + NODES], b.e[q:q + NODES],
                            b.rasum[q:q + NODES].unsqueeze(2).broadcast_to([NODES, T, NODES]), ALU.mult)
                    ins.then_inc(dve_done[s], 1)
                    if directed:
                        nc.vector.tensor_tensor(b.on[:], b.e[:],
                                                g.eye[:].unsqueeze(1).broadcast_to([P, T, NODES]),
                                                ALU.mult).then_inc(dve_done[s], 1)
                        wait_own(s, f"on_{l}", i)
                        nc.vector.tensor_reduce(b.diag[:], b.on[:], AX.X, ALU.add).then_inc(dve_done[s], 1)
                        wait_own(s, f"on_sum_{l}", i)
                        nc.vector.tensor_tensor(b.diag[:], b.diag[:], b.rasum[:], ALU.mult)\
                            .then_inc(dve_done[s], 1)

                def aT(s, i):
                    b = bufs[s]
                    dve.wait_ge(pe_done[s], PE[s](f"aT_{l}", i))
                    if directed:
                        nc.vector.tensor_tensor(
                            b.aT[:], b.ps_tiles.unsqueeze(2).broadcast_to([P, T, 2, P]),
                            g.part_cols[:].unsqueeze(1).broadcast_to([P, T, 2, P]),
                            ALU.mult).then_inc(dve_done[s], 1)
                    else:
                        nc.vector.tensor_copy(b.aT[:], b.ps[:, 1, 0:T * P].rearrange("p (t i) -> p t i", t=T))\
                            .then_inc(dve_done[s], 1)

                def agg(s, i):
                    b = bufs[s]
                    dve.wait_ge(pe_done[s], PE[s](f"agg_{l}", i))
                    if directed:
                        wait_own(s, f"diag_{l}", i)
                        dve.wait_ge(pool_done[s], PO[s](f"w1_{l}", i))
                        for t in range(T):
                            ins = nc.vector.scalar_tensor_tensor(
                                b.z[:, t], b.hw[:, t, ON], b.diag[:, t:t + 1], b.ps[:, 2 + t, 0:FEAT],
                                ALU.mult, ALU.add)
                        ins.then_inc(dve_done[s], 1)
                        wait_own(s, f"ctx_{l}", i)
                    got = [b.z[:, t] if directed else b.ps[:, 2 + t, 0:FEAT] for t in range(T)]
                    for t in range(T):
                        ins = nc.vector.bn_stats(b.st[:, t], got[t])
                    ins.then_inc(dve_done[s], 1)
                    wait_own(s, f"lstats_{l}", i)
                    nc.vector.memset(g.pad[:], 0.0)
                    for t in range(T):
                        ins = nc.vector.bn_aggr(b.mv[:, t], b.st[:, t])
                    ins.then_inc(dve_done[s], 1)
                    wait_own(s, f"laggr_{l}", i)
                    if directed:
                        nc.vector.tensor_scalar(b.rstd[:], b.mv[:, :, 1], 1e-12, None, ALU.add)\
                            .then_inc(dve_done[s], 1)
                    else:
                        nc.vector.tensor_scalar(b.rstd[:], b.mv[:, :, 1], FEAT / (FEAT - 1.0), None, ALU.mult)\
                            .then_inc(dve_done[s], 1)
                    for t in range(T):
                        ins = nc.vector.scalar_tensor_tensor(b.z[:, t], got[t], b.mv[:, t, 0:1], rows[l][-2][:],
                                                             ALU.subtract, ALU.mult)
                    ins.then_inc(dve_done[s], 1)

                def ln(s, i):
                    b = bufs[s]
                    dve.wait_ge(pool_done[s], PO[s](f"lstd_{l}", i))
                    if not directed:
                        nc.vector.tensor_scalar(b.rstd[:], b.rstd[:], 1e-3, None, ALU.add)\
                            .then_inc(dve_done[s], 1)
                        wait_own(s, f"lsig_{l}", i)
                        nc.vector.reciprocal(b.rstd[:], b.rstd[:]).then_inc(dve_done[s], 1)
                        wait_own(s, f"lrstd_{l}", i)
                    wait_own(s, f"cen_{l}", i)
                    for t in range(T):
                        nc.vector.scalar_tensor_tensor(b.z[:, t], b.z[:, t], b.rstd[:, t:t + 1], rows[l][-1][:],
                                                       ALU.mult, ALU.add).then_inc(dve_done[s], 1)
                    if l == 1:
                        wait_own(s, "z1_1", i)
                        dve.wait_ge(pool_done[s], PO[s]("x", i))
                        dve.wait_ge(sems.stored[s], 16 * i + 1)
                        nc.vector.scalar_tensor_tensor(b.xout[:], b.z[:], 0.0, b.x[:], ALU.max, ALU.add)\
                            .then_inc(dve_done[s], 1)

                todo = {f"hT_{l}": hT, f"soft_{l}": soft, f"att_{l}": att, f"aT_{l}": aT, f"agg_{l}": agg,
                        f"ln_{l}": ln}
                todo.update({f"w0_{l}": w(0), f"w2_{l}": w(2)} if directed else {f"mr_{l}": mr, f"lin_{l}": lin})
                return todo

            run_stages(dve, dve_order, {"stat": stat, **layer(0), **layer(1)})

        @block.tensor
        def _(pe):
            pe.wait_ge(g.hi_split[phase], 6)
            pe.wait_ge(g.lo_split[phase], 6)
            pe.wait_ge(g.const_in, g.const_count)

            def layer(l):
                def hT(s, i):
                    b = bufs[s]
                    if l == 0:
                        pe.wait_ge(act_done[s], AC[s]("h", i))
                        if later(i):
                            read_out = [("aT_1", 1), ("w2_1", 1)] if directed else [("aT_1", 1)]
                            pe.wait_ge(dve_done[s], DV[s].all(i, *read_out))
                    for t in range(T):
                        if l == 1:
                            pe.wait_ge(act_done[s], AC[s](f"h_next{t}_0", i))
                        for c in range(C):
                            mm = nc.tensor.transpose(b.ps_row[:, c, t * P:(t + 1) * P],
                                                     b.h[:, t, c * P:(c + 1) * P], g.ident[:])
                    mm.then_inc(pe_done[s], 1)

                left_23 = [("ctx_1" if directed else "cen_1", 1)] if l == 0 else []

                def project_T(b, out, m):
                    for o in range(C):
                        mm = exact_product(nc, out[:, o], [
                            (g.w_hi[:, 3 * l + m, c, o * P:(o + 1) * P], g.w_lo[:, 3 * l + m, c, o * P:(o + 1) * P],
                             b.t_hi[:, c], b.t_lo[:, c]) for c in range(C)])
                    return mm

                def project(b, t, bank, m):
                    return exact_product(nc, b.ps[:, bank, 0:FEAT], [
                        (b.t_hi[:, c, t * P:(t + 1) * P], b.t_lo[:, c, t * P:(t + 1) * P],
                         g.w_hi[:, 3 * l + m, c], g.w_lo[:, 3 * l + m, c]) for c in range(C)])

                def ml(s, i):
                    pe.wait_ge(dve_done[s], DV[s].all(i, (f"hT_lo_{l}", 0), *left_23))
                    project_T(bufs[s], bufs[s].ps_row2, LEFT).then_inc(pe_done[s], 1)

                def mr(s, i):
                    pe.wait_ge(act_done[s], AC[s](f"hT_{l}", i))
                    project_T(bufs[s], bufs[s].ps_row, RIGHT).then_inc(pe_done[s], 1)

                def lin(s, i):
                    pe.wait_ge(act_done[s], AC[s](f"ml_{l}", i))
                    for t in range(T):
                        mm = project(bufs[s], t, 2 + t, LIN)
                    mm.then_inc(pe_done[s], 1)

                def w0(s, i):
                    pe.wait_ge(dve_done[s], DV[s].all(i, (f"hT_lo_{l}", 0), *left_23))
                    for t in range(T):
                        mm = project(bufs[s], t, 2 + t, UPPER)
                    mm.then_inc(pe_done[s], 1)

                def w1(s, i):
                    pe.wait_ge(act_done[s], AC[s](f"hT_{l}", i))
                    project(bufs[s], 0, 1, ON)
                    pe.wait_ge(dve_done[s], DV[s](f"w0_{l}", i))
                    project(bufs[s], 1, 2, ON).then_inc(pe_done[s], 1)

                def w2(s, i):
                    project(bufs[s], 1, 3, LOWER)
                    pe.wait_ge(act_done[s], AC[s](f"w1_{l}", i))
                    project(bufs[s], 0, 1, LOWER).then_inc(pe_done[s], 1)

                def u(s, i):
                    b = bufs[s]
                    if directed:
                        pe.wait_ge(act_done[s], AC[s](f"hT_{l}", i))
                        for t in range(T):
                            at = slice(t * P, (t + 1) * P)
                            for c in range(C):
                                mm = nc.tensor.matmul(b.ps_tiles[:, t], b.hT[:, c, at],
                                                      b.hT[:, c, at], start=(c == 0), stop=(c == C - 1))
                        mm.then_inc(pe_done[s], 1)
                        return
                    pe.wait_ge(act_done[s], AC[s].all(i, (f"hT_{l}", 0), (f"ml_{l}", 0)))
                    pe.wait_ge(dve_done[s], DV[s](f"mr_{l}", i))
                    for t in range(T):
                        for gr in range(2):
                            at = t * P + gr * NODES
                            for c in range(C):
                                mm = nc.tensor.matmul(
                                    b.ps[gr * NODES:(gr + 1) * NODES, 0, t * P:(t + 1) * P],
                                    b.hT[:, c, at:at + NODES], b.mlr[:, c, :, at:at + NODES],
                                    start=(c == 0), stop=(c == C - 1))
                    mm.then_inc(pe_done[s], 1)

                def aT(s, i):
                    b = bufs[s]
                    pe.wait_ge(dve_done[s], DV[s](f"att_{l}", i))
                    for t in range(T):
                        out = b.ps[:, 0 if directed else 1, t * P:(t + 1) * P]
                        mm = nc.tensor.transpose(out, b.a_bd[:, t], g.ident[:])
                    mm.then_inc(pe_done[s], 1)

                def agg(s, i):
                    b = bufs[s]
                    pe.wait_ge(dve_done[s], DV[s].all(i, (f"aT_{l}", 0), (f"w2_{l}" if directed else f"lin_{l}", 0)))
                    if directed:
                        for t in range(T):
                            for k, m in enumerate((UPPER, LOWER)):
                                mm = nc.tensor.matmul(b.ps[:, 2 + t, 0:FEAT], b.aT[:, t, k], b.hw[:, t, m],
                                                      start=(k == 0), stop=(k == 1))
                    else:
                        for t in range(T):
                            mm = nc.tensor.matmul(b.ps[:, 2 + t, 0:FEAT], b.aT[:, t], b.hw[:, t],
                                                  start=True, stop=True)
                    mm.then_inc(pe_done[s], 1)

                both = {f"hT_{l}": hT, f"u_{l}": u, f"aT_{l}": aT, f"agg_{l}": agg}
                if directed:
                    return {**both, f"w0_{l}": w0, f"w1_{l}": w1, f"w2_{l}": w2}
                return {**both, f"ml_{l}": ml, f"mr_{l}": mr, f"lin_{l}": lin}

            run_stages(pe, pe_order, {**layer(0), **layer(1)})


def graph_stack(nc, x, adj, adj_t, w0, w1, w2, w3, rows0, rows1, rows2, rows3, ident, tri, eye,
                part_cols, out):
    with ExitStack() as ctx:
        def sb(name, shape, dt=F32):
            return ctx.enter_context(nc.sbuf_tensor(name, shape, dt))

        def sem(name):
            return ctx.enter_context(nc.semaphore(name))
        g = Shared()
        g.ident = sb("ident", [P, P])
        g.tri = sb("tri", [P, 2, NODES])
        g.eye = sb("eye", [P, NODES])
        g.part_cols = sb("part_cols", [P, 2, P])
        g.neg_half = sb("neg_half", [P, T])
        g.pos_half = sb("pos_half", [P, T])
        g.ones = sb("ones", [P, T, NODES])
        g.mark = sb("mark", [P, STREAMS])
        g.idle = sb("idle", [P, STREAMS])
        g.pad = sb("pad", [P, 1])
        g.w_hi = sb("w_hi", [P, MATS, C, FEAT], F32R)
        g.w_lo = sb("w_lo", [P, MATS, C, FEAT], F32R)
        g.w_raw = sb("w_raw", [P, MATS, C, FEAT])
        g.ps = [ctx.enter_context(nc.psum_tensor(f"ps{s}", [P, 4, BANK], F32)) for s in range(STREAMS)]
        g.weights = [w.rearrange("m (c p) o -> p m c o", p=P) for w in (w0, w1, w2, w3)]
        g.weights_in = [sem(f"weights_in{k}") for k in range(4)]
        g.hi_split = [sem(f"hi_split{k}") for k in range(4)]
        g.lo_split = [sem(f"lo_split{k}") for k in range(4)]
        g.powers = sem("powers")
        g.const_in = sem("const_in")
        g.const_loads = [(g.ident[:], ident), (g.tri[:], tri), (g.eye[:], eye),
                         (g.part_cols[:], part_cols)]
        g.const_count = 16 * len(g.const_loads)

        def groups(a):
            return a.rearrange("b s f -> (b s) f").rearrange("(n t p) f -> n p t f", t=T, p=P)
        between = [nc.dram_tensor(f"x_after_{k}", (GRAPHS, NODES, FEAT), F32, kind="Internal").ap()
                   for k in range(3)]
        xs = [groups(a) for a in [x] + between + [out]]
        a_n, a_t = groups(adj), groups(adj_t)
        gcn_phase(nc, g, 0, False, xs[0], xs[1], [a_n, a_t], [[r[l] for r in rows0] for l in range(2)])
        attention_phase(nc, g, 1, 2, xs[1], xs[2], a_n, *rows1)
        attention_phase(nc, g, 2, 1, xs[2], xs[3], a_n, *rows2)
        gcn_phase(nc, g, 3, True, xs[3], xs[4], [a_n], [[r[l] for r in rows3] for l in range(2)])


def kernel(**inputs):
    import concourse.bacc as bacc
    from concourse.bass_utils import run_bass_kernel_spmd

    def f(name):
        return np.asarray(inputs[name])

    def transposed(names, layers=None):
        if layers is None:
            return np.ascontiguousarray(np.stack([f(n).T for n in names]))
        return np.ascontiguousarray(np.stack([f(n)[l].T for l in range(layers) for n in names]))

    i, j = np.arange(NODES)[:, None], np.arange(NODES)[None, :]
    above, on, below = (j > i), (j == i), (j < i)
    tri = np.stack([above | on, below]).astype(np.float32) / np.float32(np.sqrt(FEAT))
    blocks = np.zeros((P, 2, P), np.float32)
    for k in range(P // NODES):
        at = slice(k * NODES, (k + 1) * NODES)
        blocks[at, :, at] = np.stack([above, below]).astype(np.float32).transpose(2, 0, 1)
    arrays = {
        "x": np.ascontiguousarray(f("x")),
        "adj": np.ascontiguousarray(f("adj")),
        "adj_t": np.ascontiguousarray(f("adj").transpose(0, 2, 1)),
        "w0": transposed(["L0_gnn_W_left", "L0_gnn_W_right", "L0_gnn_W_lin"], 2),
        "w1": transposed([f"L1_gnn_W{c}" for c in "qkvo"]),
        "w2": transposed([f"L2_gnn_W{c}" for c in "qkvo"]),
        "w3": transposed(["L3_gnn_Wl", "L3_gnn_Ws", "L3_gnn_Wr"], 2),
        "ident": np.eye(P, dtype=np.float32),
        "tri": np.ascontiguousarray(np.tile(tri.transpose(1, 0, 2), (P // NODES, 1, 1))),
        "eye": np.ascontiguousarray(np.tile(on.astype(np.float32), (P // NODES, 1))),
        "part_cols": blocks,
    }
    rows = [["L0_gnn_b_lin", "L0_gnn_ln_a", "L0_gnn_ln_b"], ["L1_gnn_bv", "L1_gnn_bo"],
            ["L2_gnn_bv", "L2_gnn_bo"], ["L3_gnn_bl", "L3_gnn_bs", "L3_gnn_br", "L3_gnn_ln_w", "L3_gnn_ln_b"]]
    for names in rows:
        for name in names:
            arrays[name] = np.ascontiguousarray(f(name))

    nc = bacc.Bacc("TRN2", target_bir_lowering=False, num_devices=1)
    at = {name: nc.dram_tensor(f"in_{name}", a.shape, mybir.dt.from_np(a.dtype), kind="ExternalInput").ap()
          for name, a in arrays.items()}
    out = nc.dram_tensor("out", (GRAPHS, NODES, FEAT), F32, kind="ExternalOutput").ap()
    graph_stack(nc, at["x"], at["adj"], at["adj_t"], at["w0"], at["w1"], at["w2"], at["w3"],
                *[[at[name] for name in names] for names in rows],
                at["ident"], at["tri"], at["eye"], at["part_cols"], out)
    got = run_bass_kernel_spmd(nc, [{f"in_{name}": a for name, a in arrays.items()}], core_ids=[0])
    return got.results[0]["out"]
```

```python
from contextlib import ExitStack

import numpy as np

from concourse import mybir

GRAPHS, NODES, FEAT = 128, 64, 384
P = 128
C = FEAT // P
T = 2
TOK = T * P
STREAMS = 2
GROUPS = GRAPHS * NODES // TOK
ITER = GROUPS // STREAMS
HEADS = 12
HD = FEAT // HEADS
HT = HEADS * T
HPC = P // HD
BANK = 512
MATS = 6
STAGED = 4
EARLY = range(2)
LN_EPS = 1e-5
BEHIND_GCN0, BEHIND_ATT, BEHIND_GCN3 = 0.308, 0.501, 0.497

ATT_STAGES = [
    ("stat", None, None, 0.2856, 0.4826), ("bias", None, None, None, 0.6245),
    ("norm", None, 0.4722, None, None), ("hT", 0.4466, 0.4904, 0.3931, None),
    ("q", 0.5205, 0.5583, None, None), ("k", 0.5207, 0.6068, None, None), ("v", 0.5863, None, 0.7424, None),
    ("scores", 0.7999, None, None, None), ("soft_a", None, None, 0.8466, None),
    ("soft_b", None, 1.0101, 0.9228, None), ("soft_c", None, None, 1.0288, 1.1245),
    ("pt0", 1.0894, 1.1557, None, None), ("pt1", 1.2180, None, 1.1343, None),
    ("pt2", 1.2337, 1.1808, None, None), ("pt3", 1.2437, None, 1.2083, None),
    ("pt4", 1.2530, 1.2006, None, None), ("pt5", 1.2595, None, 1.2403, None),
    ("pv", 1.2688, 1.3772, 1.3435, None), ("out", 1.4602, None, 1.4924, None),
    ("xb", None, None, None, 1.0292),
]
GCN0_STAGES = [
    ("stat", None, None, 0.3312, 0.2180), ("adj", None, None, None, 0.4964),
    ("norm", None, 0.5330, None, None), ("hT_0", 0.6020, 0.6083, 0.6348, None),
    ("ml_0", 0.6398, 0.6584, None, None), ("mr_0", 0.6542, None, 0.7104, None),
    ("lin_0", 0.7026, None, 0.7744, None), ("u_0", 0.7399, None, None, None),
    ("soft_0", None, 0.8521, 0.7816, None), ("att_0", None, None, 0.8848, None),
    ("aT_0", 0.8827, None, 0.8982, None), ("agg_0", 0.9243, None, 0.9476, 0.9093),
    ("ln_0", None, 1.0241, 0.9529, None), ("hT_1", 1.0030, 1.0699, 1.0277, None),
    ("ml_1", 1.1119, 1.2867, None, None), ("mr_1", 1.2516, None, 1.2643, None),
    ("lin_1", 1.2973, None, 1.4408, None), ("u_1", 1.3118, None, None, None),
    ("soft_1", None, 1.4346, 1.3852, None), ("att_1", None, None, 1.3927, None),
    ("aT_1", 1.5372, None, 1.5092, None), ("agg_1", 1.5727, None, 1.6004, 1.5147),
    ("ln_1", None, None, 1.6618, None), ("x", None, None, None, 0.9204),
]
GCN3_STAGES = [
    ("stat", None, None, 0.1383, 0.0183), ("adj", None, None, None, 0.2318),
    ("norm", None, 0.2314, None, None), ("hT_0", 0.4547, 0.4480, 0.4295, None),
    ("w0_0", 0.5220, 0.5323, None, 0.5423), ("u_0", 0.5895, None, None, None),
    ("w1_0", 0.6159, 0.7259, None, 0.5529), ("w2_0", 0.6627, None, 0.7088, None),
    ("soft_0", None, 0.5817, 0.5860, None), ("att_0", None, None, 0.6358, None),
    ("aT_0", 0.6801, None, 0.7089, None), ("agg_0", 0.7460, None, 0.7493, 0.6033),
    ("ln_0", None, 0.8547, 0.7597, None), ("hT_1", 0.9059, 0.9286, 0.8773, None),
    ("w0_1", 0.9975, 1.2198, None, 1.2298), ("u_1", 1.1963, None, None, None),
    ("w1_1", 1.2542, 1.3507, None, 1.2333), ("w2_1", 1.3215, None, 1.2930, None),
    ("soft_1", None, 1.2653, 1.2188, None), ("att_1", None, None, 1.2458, None),
    ("aT_1", 1.3724, None, 1.3560, None), ("agg_1", 1.4921, None, 1.4715, 1.3931),
    ("ln_1", None, None, 1.4741, None), ("x", None, None, None, 0.4462),
]

ALU = mybir.AluOpType
ACT = mybir.ActivationFunctionType
F32 = mybir.dt.float32
F32R = mybir.dt.float32r
AX = mybir.AxisListType


class Count:

    def __init__(self, order, s, stages):
        self.late = {}
        self.place = {}
        for stage, stream, late in order:
            if stream == s:
                for name in stages.get(stage, []):
                    self.place[name] = len(self.place) + 1
                    self.late[name] = late
        self.missing = sum(self.late.values())

    def all(self, i, *events):
        there = [(name, back) for name, back in events if not isinstance(i, int) or i >= back]
        name, back = max(there, key=lambda event: (self.late[event[0]] - event[1], self.place[event[0]]))
        return self(name, i - back)

    def __call__(self, name, i):
        turn = i + self.late[name]
        if isinstance(turn, int) and turn in (0, ITER):
            here = sum(self.late[n] == (turn > 0) for n in self.place if self.place[n] <= self.place[name])
            return here + (ITER * len(self.place) - self.missing if turn else 0)
        return turn * len(self.place) + (self.place[name] - self.missing)


def stage_orders(stages, behind):
    orders = []
    for engine in range(1, 5):
        order = []
        for s in range(STREAMS):
            for k, stage in enumerate(stages):
                if stage[engine] is not None:
                    at = stage[engine] + s * behind
                    assert 0 <= at < 2
                    order.append((at % 1, s, k, stage[0], int(at)))
        orders.append([(name, s, late) for _, s, _, name, late in sorted(order)])
    return orders


def counts(order, stages):
    return [Count(order, s, stages) for s in range(STREAMS)]


def run_stages(eng, order, todo):
    order = [(todo[stage], s, late) for stage, s, late in order if stage in todo]

    def round_of(r):
        for stage, s, late in order:
            if not isinstance(r, int) or 0 <= r - late < ITER:
                stage(s, r - late)
    round_of(0)
    round_of(1)
    with eng.Fori(2, ITER) as r:
        round_of(r)
    round_of(ITER)


def later(i):
    return not isinstance(i, int) or i > 0


def head_tile(t, h):
    return (h % HPC) * T * C + t * C + h // HPC


def exact_product(nc, out, terms):
    for k, (lhs_hi, lhs_lo, rhs_hi, rhs_lo) in enumerate(terms):
        nc.tensor.matmul(out, lhs_hi, rhs_hi, start=(k == 0), stop=False)
        nc.tensor.matmul(out, lhs_hi, rhs_lo, start=False, stop=False)
        last = nc.tensor.matmul(out, lhs_lo, rhs_hi, start=False, stop=(k == len(terms) - 1))
    return last


class Shared:
    pass


def first(s, i):
    return s == 0 and isinstance(i, int) and i == 0


def weight_split(nc, g, phase, mats, act, dve):
    if act is not None:
        for m in mats:
            weights_wait(act, g, phase, m)
            nc.scalar.activation(g.w_hi[:, m], g.w_raw[:, m], ACT.Copy).then_inc(g.hi_split[phase], 1)
    if dve is not None:
        for m in mats:
            weights_wait(dve, g, phase, m)
            dve.wait_ge(g.hi_split[phase], m + 1)
            nc.vector.tensor_tensor(g.w_lo[:, m], g.w_raw[:, m], g.w_hi[:, m].bitcast(F32),
                                    ALU.subtract).then_inc(g.lo_split[phase], 1)


def weights_made(pe, g, phase, m, i):
    if isinstance(i, int) and i == 0:
        pe.wait_ge(g.hi_split[phase], m + 1)
        pe.wait_ge(g.lo_split[phase], m + 1)


def weights_wait(eng, g, phase, m):
    if m in (0, len(EARLY)):
        eng.wait_ge(g.weights_in[phase], 16)
    if m == STAGED:
        eng.wait_ge(g.more_weights_in[phase], 16)


def move_program(nc, sp, g, phase, n_mats, rows, x_out, bufs, sems, x_free, x_new):
    def load(s, i, of=phase):
        group = i * STREAMS + s
        x_in, adj_list = g.sources[of]
        sp.dma_start(g.xin[s][:], x_in[group]).then_inc(g.x_in[of][s], 16)
        for k, a in enumerate(adj_list):
            sp.dma_start(g.adjin[s][:, k], a[group]).then_inc(g.adj_in[of][s], 16)

    def store(s, i):
        x_new(s, i)
        sp.dma_start(x_out[i * STREAMS + s], bufs[s].xout[:]).then_inc(sems.stored[s], 16)

    if phase == 0:
        for s in range(STREAMS):
            load(s, 0)
    for dst, src in rows:
        sp.dma_start(dst, src.partition_broadcast(P)).then_inc(sems.params_in, 16)
    if n_mats > STAGED:
        sp.dma_start(g.w_raw[:, STAGED:], g.weights[phase][:, STAGED:]).then_inc(g.more_weights_in[phase], 16)
    if phase + 1 < len(g.weights):
        sp.wait_ge(g.hi_split[phase], n_mats)
        sp.wait_ge(g.lo_split[phase], n_mats)
        nxt = g.weights[phase + 1]
        sp.dma_start(g.w_raw[:, :STAGED], nxt[:, :STAGED]).then_inc(g.weights_in[phase + 1], 16)

    def turn(i):
        for s in range(STREAMS):
            x_free(s, i - 1)
            load(s, i)
        for s in range(STREAMS):
            store(s, i - 1)
    turn(1)
    with sp.Fori(2, ITER) as i:
        turn(i)
    if phase + 1 < len(g.sources):
        for s in range(STREAMS):
            x_free(s, ITER - 1)
            sp.wait_ge(sems.stored[s], 16 * (ITER - 1) + 1)
            load(s, 0, of=phase + 1)
    for s in range(STREAMS):
        store(s, ITER - 1)
    for s in range(STREAMS):
        sp.wait_ge(sems.stored[s], 16 * ITER + 1)


class Sems:
    pass


class Buf:
    pass


def phase_sems(nc, g, ctx, phase):
    m = Sems()

    def sem(name):
        return ctx.enter_context(nc.semaphore(f"{name}_{phase}"))
    m.params_in = sem("params_in")
    m.start_zero = sem("start_zero")
    m.factor_set = sem("factor_set")
    m.x_in, m.adj_in = g.x_in[phase], g.adj_in[phase]
    m.stored, m.pe_done, m.act_done, m.dve_done, m.pool_done = (
        [sem(f"{name}{s}") for s in range(STREAMS)]
        for name in ("stored", "pe_done", "act_done", "dve_done", "pool_done"))
    return m


def attention_phase(nc, g, phase, bias_times, x_out, bv, bo):
    SCALE = float(FEAT) ** -0.5
    WQ, WK, WV, WO = range(4)
    pe_order, act_order, dve_order, pool_order = stage_orders(ATT_STAGES, BEHIND_ATT)
    PE = counts(pe_order, {n: [n] for n in ["hT", "q", "k", "v", "scores", "pt0", "pt1", "pt2", "pt3", "pt4",
                                         "pt5", "pv", "out"]})
    AC = counts(act_order, {"norm": ["h"], "hT": ["hT_hi"], "q": ["q"], "k": ["k"], "soft_b": ["e"], "pt0": ["pt0"],
                        "pt2": ["pt2"], "pt4": ["pt4"], "pv": ["oT_hi"]})
    DV = counts(dve_order, {"stat": ["stats", "aggr", "var", "shift"], "hT": ["hT_lo"], "v": ["v"],
                        "soft_a": ["s", "max"], "soft_b": ["diff", "absmax"],
                        "soft_c": ["sum", "rsum", "factor", "p"], "pt1": ["pt1"], "pt3": ["pt3"],
                        "pt5": ["pt5"], "pv": ["oT_lo"], "out": ["xout"]})
    PO = counts(pool_order, {"stat": ["rstd"], "bias": ["bias"], "xb": ["xb"], "soft_c": ["p"]})

    with ExitStack() as ctx:
        def sb(name, shape, dt=F32):
            return ctx.enter_context(nc.sbuf_tensor(f"{name}_{phase}", shape, dt))
        sems = phase_sems(nc, g, ctx, phase)
        pe_done, act_done, dve_done, pool_done = sems.pe_done, sems.act_done, sems.dve_done, sems.pool_done
        bv_row = sb("bv_row", [P, FEAT])
        bo_row = sb("bo_row", [P, FEAT])
        bias_factor = sb("bias_factor", [P, T, NODES])
        spare = [w[:, STAGED:].rearrange("p m c o -> p (m c o)") for w in (g.w_hi, g.w_lo, g.w_raw)]
        bufs = []
        for s in range(STREAMS):
            b = Buf()
            b.xin, b.adjin = g.xin[s], g.adjin[s]
            b.xout = sb(f"xout{s}", [P, T, FEAT])
            b.bias = sb(f"bias{s}", [P, T, NODES])
            b.x_st = sb(f"x_st{s}", [P, T, 6])
            b.x_mv = sb(f"x_mv{s}", [P, T, 2])
            b.x_rstd = sb(f"x_rstd{s}", [P, T])
            b.x_shift = sb(f"x_shift{s}", [P, T])
            b.h = sb(f"h{s}", [P, T, FEAT])
            b.t_hi = sb(f"t_hi{s}", [P, C, TOK], F32R)
            b.t_lo = sb(f"t_lo{s}", [P, C, TOK], F32R)
            b.q = sb(f"q{s}", [P, C, TOK])
            b.k = sb(f"k{s}", [P, C, TOK])
            b.v = sb(f"v{s}", [P, T, FEAT])
            b.s = sb(f"s{s}", [P, HT, NODES])
            if s == 0:
                b.e = spare[2][:, 0:HT * NODES].rearrange("p (h k) -> p h k", k=NODES)
            else:
                b.e = sb("e", [P, HT, NODES])
            b.o_hi, b.o_lo = (a[:, s * C * TOK:(s + 1) * C * TOK].rearrange("p (c t) -> p c t", c=C)
                              for a in spare[0:2])
            b.max = sb(f"max{s}", [P, HT])
            b.absmax = sb(f"absmax{s}", [P, HT])
            b.sum = sb(f"sum{s}", [P, HT])
            b.rsum = sb(f"rsum{s}", [P, HT])
            b.factor = sb(f"factor{s}", [P, HT])
            b.p = sb(f"p{s}", [P, HT, P])
            b.pT = sb(f"pT{s}", [P, HT, P])
            b.ps = g.ps[s]
            b.ps_row = b.ps[:, 0:2, :].rearrange("p a b -> p (a b)")[:, 0:C * TOK].rearrange(
                "p (c t) -> p c t", c=C)
            b.ps_row2 = b.ps[:, 2:4, :].rearrange("p a b -> p (a b)")[:, 0:C * TOK].rearrange(
                "p (c t) -> p c t", c=C)
            b.ps_s = b.ps[:, :, 0:T * C * NODES].rearrange("p r (t c k) -> p r t c k", t=T, c=C)
            bufs.append(b)

        block = ctx.enter_context(nc.Block())

        @block.sync
        def _(sp):
            def x_free(s, i):
                sp.wait_ge(pool_done[s], PO[s].all(i, ("xb", 0), ("bias", 0)))
                sp.wait_ge(act_done[s], AC[s]("h", i))

            def x_new(s, i):
                sp.wait_ge(dve_done[s], DV[s]("xout", i))
            move_program(nc, sp, g, phase, 4, [(bv_row[:], bv), (bo_row[:], bo)], x_out, bufs,
                         sems, x_free, x_new)

        @block.gpsimd
        def _(pool):
            nc.gpsimd.memset(bias_factor[:], bias_times / SCALE).then_inc(sems.factor_set, 1)
            pool.wait_ge(sems.factor_set, 1)

            def stat(s, i):
                b = bufs[s]
                pool.wait_ge(dve_done[s], DV[s]("var", i))
                nc.gpsimd.tensor_tensor(b.x_rstd[:], b.x_rstd[:], g.neg_half[:, 0:T],
                                        ALU.pow).then_inc(pool_done[s], 1)
                pool.wait_ge(pool_done[s], PO[s]("rstd", i))

            def bias(s, i):
                b = bufs[s]
                pool.wait_ge(sems.adj_in[s], 16 * (i + 1))
                if later(i):
                    pool.wait_ge(dve_done[s], DV[s]("s", i - 1))
                nc.gpsimd.tensor_tensor(b.bias[:], b.adjin[:, 0], bias_factor[:], ALU.mult)\
                    .then_inc(pool_done[s], 1)
                pool.wait_ge(pool_done[s], PO[s]("bias", i))
                if first(s, i):
                    for other in bufs:
                        nc.gpsimd.memset(other.p[:], 0.0).then_inc(sems.start_zero, 1)
                    pool.wait_ge(sems.start_zero, STREAMS)

            def xb(s, i):
                b = bufs[s]
                pool.wait_ge(sems.x_in[s], 16 * (i + 1))
                if isinstance(i, int) and i == 0:
                    pool.wait_ge(sems.params_in, 32)
                pool.wait_ge(sems.stored[s], 16 * i + 1)
                nc.gpsimd.tensor_tensor(b.xout[:], b.xin[:], bo_row[:].unsqueeze(1).broadcast_to([P, T, FEAT]),
                                        ALU.add).then_inc(pool_done[s], 1)
                pool.wait_ge(pool_done[s], PO[s]("xb", i))

            def soft_c(s, i):
                b = bufs[s]
                pool.wait_ge(dve_done[s], DV[s]("factor", i))
                nc.gpsimd.tensor_tensor(b.p[NODES:P, :, NODES:P], b.e[NODES:P],
                                        b.factor[NODES:P].unsqueeze(2).broadcast_to([NODES, HT, NODES]),
                                        ALU.mult).then_inc(pool_done[s], 1)
                pool.wait_ge(pool_done[s], PO[s]("p", i))

            run_stages(pool, pool_order, {"stat": stat, "bias": bias, "xb": xb, "soft_c": soft_c})

        @block.scalar
        def _(act):
            weight_split(nc, g, phase, EARLY, act, None)

            def norm(s, i):
                b = bufs[s]
                act.wait_ge(dve_done[s], DV[s]("shift", i))
                if later(i):
                    act.wait_ge(pe_done[s], PE[s]("hT", i - 1))
                for t in range(T):
                    ins = nc.scalar.activation(b.h[:, t], b.xin[:, t], ACT.Relu, bias=b.x_shift[:, t:t + 1],
                                               scale=b.x_rstd[:, t:t + 1])
                ins.then_inc(act_done[s], 1)

            def hT(s, i):
                b = bufs[s]
                act.wait_ge(pe_done[s], PE[s].all(i, ("hT", 0), ("v", 1)))
                nc.scalar.activation(b.t_hi[:], b.ps_row, ACT.Copy).then_inc(act_done[s], 1)
                if first(s, i):
                    weight_split(nc, g, phase, range(len(EARLY), 4), act, None)

            def q(s, i):
                b = bufs[s]
                act.wait_ge(pe_done[s], PE[s]("q", i))
                nc.scalar.activation(b.q[:], b.ps_row, ACT.Copy).then_inc(act_done[s], 1)

            def k(s, i):
                b = bufs[s]
                act.wait_ge(pe_done[s], PE[s]("k", i))
                nc.scalar.activation(b.k[:], b.ps_row2, ACT.Copy).then_inc(act_done[s], 1)

            def soft_b(s, i):
                b = bufs[s]
                act.wait_ge(dve_done[s], DV[s]("diff", i))
                nc.scalar.activation(b.e[:], b.e[:], ACT.Exp, scale=SCALE).then_inc(act_done[s], 1)

            def pt(u):
                def stage(s, i):
                    b = bufs[s]
                    act.wait_ge(pe_done[s], PE[s](f"pt{u}", i))
                    nc.scalar.activation(b.pT[:, 4 * u:4 * u + 4], b.ps[:, u % 4, :], ACT.Copy)\
                        .then_inc(act_done[s], 1)
                return stage

            def pv(s, i):
                b = bufs[s]
                act.wait_ge(pe_done[s], PE[s]("pv", i))
                nc.scalar.activation(b.o_hi[:], b.ps_row2, ACT.Copy).then_inc(act_done[s], 1)

            run_stages(act, act_order, {"norm": norm, "hT": hT, "q": q, "k": k, "soft_b": soft_b,
                                        "pt0": pt(0), "pt2": pt(2), "pt4": pt(4), "pv": pv})

        @block.vector
        def _(dve):
            for s in range(STREAMS):
                nc.vector.memset(g.mark[:, s:s + 1], 0.0).then_inc(sems.stored[s], 1)

            def stat(s, i):
                b = bufs[s]
                dve.wait_ge(sems.x_in[s], 16 * (i + 1))
                for t in range(T):
                    ins = nc.vector.bn_stats(b.x_st[:, t], b.xin[:, t])
                ins.then_inc(dve_done[s], 1)
                dve.wait_ge(dve_done[s], DV[s]("stats", i))
                nc.vector.memset(g.pad[:], 0.0)
                for t in range(T):
                    ins = nc.vector.bn_aggr(b.x_mv[:, t], b.x_st[:, t])
                ins.then_inc(dve_done[s], 1)
                dve.wait_ge(dve_done[s], DV[s]("aggr", i))
                nc.vector.tensor_scalar(b.x_rstd[:], b.x_mv[:, :, 1], LN_EPS, None, ALU.add)\
                    .then_inc(dve_done[s], 1)
                dve.wait_ge(pool_done[s], PO[s]("rstd", i))
                nc.vector.scalar_tensor_tensor(b.x_shift[:], b.x_mv[:, :, 0], -1.0, b.x_rstd[:], ALU.mult,
                                               ALU.mult).then_inc(dve_done[s], 1)
                if first(s, i):
                    weight_split(nc, g, phase, EARLY, None, dve)

            def hT(s, i):
                b = bufs[s]
                dve.wait_ge(act_done[s], AC[s]("hT_hi", i))
                nc.vector.tensor_tensor(b.t_lo[:], b.ps_row, b.t_hi[:].bitcast(F32), ALU.subtract)\
                    .then_inc(dve_done[s], 1)
                if first(s, i):
                    weight_split(nc, g, phase, range(len(EARLY), 4), None, dve)
                    dve.wait_ge(sems.params_in, 32)

            def v(s, i):
                b = bufs[s]
                dve.wait_ge(pe_done[s], PE[s]("v", i))
                nc.vector.tensor_tensor(b.v[:], b.ps[:, 0:2, 0:FEAT],
                                        bv_row[:].unsqueeze(1).broadcast_to([P, T, FEAT]),
                                        ALU.add).then_inc(dve_done[s], 1)

            def soft_a(s, i):
                b = bufs[s]
                dve.wait_ge(pe_done[s], PE[s]("scores", i))
                dve.wait_ge(pool_done[s], PO[s]("bias", i))
                for t in range(T):
                    ins = nc.vector.tensor_tensor(
                        b.s[:].rearrange("p (r t c) k -> p r t c k", r=HPC, t=T)[:, :, t], b.ps_s[:, :, t],
                        b.bias[:, t:t + 1].unsqueeze(1).broadcast_to([P, HPC, C, NODES]), ALU.add)
                ins.then_inc(dve_done[s], 1)
                dve.wait_ge(dve_done[s], DV[s]("s", i))
                nc.vector.tensor_reduce(b.max[:], b.s[:], AX.X, ALU.max).then_inc(dve_done[s], 1)

            def soft_b(s, i):
                b = bufs[s]
                dve.wait_ge(dve_done[s], DV[s]("max", i))
                nc.vector.tensor_tensor(b.e[:], b.s[:], b.max[:].unsqueeze(2).broadcast_to([P, HT, NODES]),
                                        ALU.subtract).then_inc(dve_done[s], 1)
                nc.vector.tensor_reduce(b.absmax[:], b.s[:], AX.X, ALU.max, apply_absolute_value=True)\
                    .then_inc(dve_done[s], 1)

            def soft_c(s, i):
                b = bufs[s]
                dve.wait_ge(act_done[s], AC[s]("e", i))
                nc.vector.tensor_reduce(b.sum[:], b.e[:], AX.X, ALU.add).then_inc(dve_done[s], 1)
                dve.wait_ge(dve_done[s], DV[s]("sum", i))
                nc.vector.reciprocal(b.rsum[:], b.sum[:]).then_inc(dve_done[s], 1)
                dve.wait_ge(dve_done[s], DV[s]("rsum", i))
                nc.vector.scalar_tensor_tensor(b.factor[:], b.absmax[:], 0.0, b.rsum[:], ALU.not_equal,
                                               ALU.mult).then_inc(dve_done[s], 1)
                dve.wait_ge(dve_done[s], DV[s]("factor", i))
                if isinstance(i, int) and i == 0:
                    dve.wait_ge(sems.start_zero, STREAMS)
                nc.vector.tensor_tensor(b.p[0:NODES, :, 0:NODES], b.e[0:NODES],
                                        b.factor[0:NODES].unsqueeze(2).broadcast_to([NODES, HT, NODES]),
                                        ALU.mult).then_inc(dve_done[s], 1)

            def pt(u):
                def stage(s, i):
                    b = bufs[s]
                    dve.wait_ge(pe_done[s], PE[s](f"pt{u}", i))
                    nc.vector.tensor_copy(b.pT[:, 4 * u:4 * u + 4],
                                          b.ps[:, u % 4, :].rearrange("p (h k) -> p h k", k=P))\
                        .then_inc(dve_done[s], 1)
                return stage

            def pv(s, i):
                b = bufs[s]
                dve.wait_ge(act_done[s], AC[s]("oT_hi", i))
                nc.vector.tensor_tensor(b.o_lo[:], b.ps_row2, b.o_hi[:].bitcast(F32), ALU.subtract)\
                    .then_inc(dve_done[s], 1)

            def out(s, i):
                b = bufs[s]
                dve.wait_ge(pe_done[s], PE[s]("out", i))
                dve.wait_ge(pool_done[s], PO[s]("xb", i))
                nc.vector.tensor_tensor(b.xout[:], b.ps[:, 2:4, 0:FEAT], b.xout[:], ALU.add)\
                    .then_inc(dve_done[s], 1)

            run_stages(dve, dve_order, {"stat": stat, "hT": hT, "v": v, "soft_a": soft_a,
                                    "soft_b": soft_b, "soft_c": soft_c, "pt1": pt(1), "pt3": pt(3),
                                    "pt5": pt(5), "pv": pv, "out": out})

        @block.tensor
        def _(pe):
            pe.wait_ge(g.const_in, g.const_count)

            def hT(s, i):
                b = bufs[s]
                pe.wait_ge(act_done[s], AC[s].all(i, ("h", 0), ("pt4", 1)))
                if later(i):
                    pe.wait_ge(dve_done[s], DV[s]("pt5", i - 1))
                for c in range(C):
                    for t in range(T):
                        mm = nc.tensor.transpose(b.ps_row[:, c, t * P:(t + 1) * P],
                                                 b.h[:, t, c * P:(c + 1) * P], g.ident[:])
                mm.then_inc(pe_done[s], 1)

            def project_T(b, out, m):
                for o in range(C):
                    mm = exact_product(nc, out[:, o], [
                        (g.w_hi[:, m, c, o * P:(o + 1) * P], g.w_lo[:, m, c, o * P:(o + 1) * P],
                         b.t_hi[:, c], b.t_lo[:, c]) for c in range(C)])
                return mm

            def project(b, hi, lo, banks, m):
                for t in range(T):
                    mm = exact_product(nc, b.ps[:, banks + t, 0:FEAT], [
                        (hi[:, c, t * P:(t + 1) * P], lo[:, c, t * P:(t + 1) * P],
                         g.w_hi[:, m, c], g.w_lo[:, m, c]) for c in range(C)])
                return mm

            def q(s, i):
                pe.wait_ge(act_done[s], AC[s]("hT_hi", i))
                pe.wait_ge(dve_done[s], DV[s]("hT_lo", i))
                weights_made(pe, g, phase, WQ, i)
                project_T(bufs[s], bufs[s].ps_row, WQ).then_inc(pe_done[s], 1)

            def k(s, i):
                if later(i):
                    pe.wait_ge(dve_done[s], DV[s]("xout", i - 1))
                weights_made(pe, g, phase, WK, i)
                project_T(bufs[s], bufs[s].ps_row2, WK).then_inc(pe_done[s], 1)

            def v(s, i):
                pe.wait_ge(act_done[s], AC[s]("q", i))
                weights_made(pe, g, phase, WV, i)
                project(bufs[s], bufs[s].t_hi, bufs[s].t_lo, 0, WV).then_inc(pe_done[s], 1)

            def scores(s, i):
                b = bufs[s]
                pe.wait_ge(act_done[s], AC[s].all(i, ("q", 0), ("k", 0)))
                pe.wait_ge(dve_done[s], DV[s]("v", i))
                for t in range(T):
                    for h in range(HEADS):
                        r = HD * (h % HPC)
                        for gr in range(2):
                            at = t * P + gr * NODES
                            mm = nc.tensor.matmul(b.ps_s[gr * NODES:(gr + 1) * NODES, h % HPC, t, h // HPC],
                                                  b.q[r:r + HD, h // HPC, at:at + NODES],
                                                  b.k[r:r + HD, h // HPC, at:at + NODES],
                                                  start=True, stop=True)
                mm.then_inc(pe_done[s], 1)

            def pt(u):
                def stage(s, i):
                    b = bufs[s]
                    if u == 0:
                        pe.wait_ge(dve_done[s], DV[s]("p", i))
                        pe.wait_ge(pool_done[s], PO[s]("p", i))
                    if u >= 4:
                        if u % 2 == 0:
                            pe.wait_ge(act_done[s], AC[s](f"pt{u - 4}", i))
                        else:
                            pe.wait_ge(dve_done[s], DV[s](f"pt{u - 4}", i))
                    for j in range(4):
                        mm = nc.tensor.transpose(b.ps[:, u % 4, j * P:(j + 1) * P], b.p[:, 4 * u + j],
                                                 g.ident[:])
                    mm.then_inc(pe_done[s], 1)
                return stage

            def pv(s, i):
                b = bufs[s]
                pe.wait_ge(act_done[s], AC[s]("pt4", i))
                pe.wait_ge(dve_done[s], DV[s]("pt5", i))
                for t in range(T):
                    for h in range(HEADS):
                        r = HD * (h % HPC)
                        mm = nc.tensor.matmul(b.ps_row2[r:r + HD, h // HPC, t * P:(t + 1) * P],
                                              b.v[:, t, h * HD:(h + 1) * HD], b.pT[:, head_tile(t, h)],
                                              start=True, stop=True, tile_position=(0, r))
                mm.then_inc(pe_done[s], 1)

            def out(s, i):
                pe.wait_ge(act_done[s], AC[s]("oT_hi", i))
                pe.wait_ge(dve_done[s], DV[s]("oT_lo", i))
                weights_made(pe, g, phase, WO, i)
                project(bufs[s], bufs[s].o_hi, bufs[s].o_lo, 2, WO).then_inc(pe_done[s], 1)

            todo = {"hT": hT, "q": q, "k": k, "v": v, "scores": scores, "pv": pv, "out": out}
            todo.update({f"pt{u}": pt(u) for u in range(6)})
            run_stages(pe, pe_order, todo)


def gcn_phase(nc, g, phase, directed, x_out, params):
    TEMPER = float(np.sqrt(FEAT))
    n_adj = len(g.sources[phase][1])
    LEFT, RIGHT, LIN = range(3)
    UPPER, ON, LOWER = range(3)
    pe_order, act_order, dve_order, pool_order = stage_orders(GCN3_STAGES, BEHIND_GCN3) if directed else \
        stage_orders(GCN0_STAGES, BEHIND_GCN0)

    def both(stages_):
        return {f"{st}_{l}": [f"{name}_{l}" for name in names if (name[:6], l) != ("h_next", 1)]
                for l in range(2) for st, names in stages_.items()}

    if directed:
        PE = counts(pe_order, both({n: [n] for n in ["hT", "w0", "w1", "w2", "u", "aT", "agg"]}))
        AC = counts(act_order, {"norm": ["h"], **both({"hT": ["hT_hi", "hT"], "w0": ["w0"], "w1": ["w1"], "soft": ["e"],
                                                   "ln": ["h_next0", "h_next1"]})})
        events = both({"hT": ["hT_lo"], "w2": ["w2"], "soft": ["max", "diff"],
                       "att": ["sum", "rsum", "ea", "a", "asum", "asum_eps", "rasum", "att", "on", "on_sum",
                               "diag"],
                       "aT": ["aT"], "agg": ["ctx", "lstats", "laggr", "lvar", "cen"],
                       "ln": ["z0", "z1"]})
        PO = counts(pool_order, {"stat": ["rstd"], "adj": ["adj"], "x": ["x"],
                            **both({"w0": ["w0"], "w1": ["w1"], "agg": ["lstd"]})})
    else:
        PE = counts(pe_order, both({n: [n] for n in ["hT", "ml", "mr", "lin", "u", "aT", "agg"]}))
        AC = counts(act_order, {"norm": ["h"], **both({"hT": ["hT_hi", "hT"], "ml": ["ml"], "soft": ["e"],
                                                   "ln": ["h_next0", "h_next1"]})})
        events = both({"hT": ["hT_lo"], "mr": ["mr"], "lin": ["lin"], "soft": ["w", "u"],
                       "att": ["ea", "asum", "asum_eps", "rasum", "att"], "aT": ["aT"],
                       "agg": ["lstats", "laggr", "lvar", "cen"], "ln": ["lsig", "lrstd", "z0", "z1"]})
        PO = counts(pool_order, {"stat": ["rstd"], "adj": ["adj", "clr"], "x": ["x"], **both({"agg": ["lstd"]})})
    events["ln_1"].append("xout")
    DV = counts(dve_order, {"stat": ["stats", "aggr", "var", "shift"], **events})

    with ExitStack() as ctx:
        def sb(name, shape, dt=F32):
            return ctx.enter_context(nc.sbuf_tensor(f"{name}_{phase}", shape, dt))
        sems = phase_sems(nc, g, ctx, phase)
        pe_done, act_done, dve_done, pool_done = sems.pe_done, sems.act_done, sems.dve_done, sems.pool_done
        rows = [[sb(f"row{l}_{k}", [P, FEAT]) for k in range(len(params[l]))] for l in range(2)]
        bufs = []
        for s in range(STREAMS):
            b = Buf()
            b.xin, b.adjin = g.xin[s], g.adjin[s]
            b.x = sb(f"x{s}", [P, T, FEAT])
            b.adj = sb(f"adj{s}", [P, T, NODES])
            b.st = sb(f"st{s}", [P, T, 6])
            b.mv = sb(f"mv{s}", [P, T, 2])
            b.rstd = sb(f"rstd{s}", [P, T])
            b.x_st = sb(f"x_st{s}", [P, T, 6])
            b.x_mv = sb(f"x_mv{s}", [P, T, 2])
            b.x_rstd = sb(f"x_rstd{s}", [P, T])
            b.x_shift = sb(f"x_shift{s}", [P, T])
            b.h = sb(f"h{s}", [P, T, FEAT])
            b.t_hi = sb(f"t_hi{s}", [P, C, TOK], F32R)
            b.t_lo = sb(f"t_lo{s}", [P, C, TOK], F32R)
            b.hT = sb(f"hT{s}", [P, C, TOK])
            b.e = sb(f"e{s}", [P, T, NODES])
            b.asum = sb(f"asum{s}", [P, T])
            b.rasum = sb(f"rasum{s}", [P, T])
            b.a_bd = sb(f"a_bd{s}", [P, T, P])
            b.z = sb(f"z{s}", [P, T, FEAT])
            b.xout = sb(f"xout{s}", [P, T, FEAT])
            if directed:
                b.max = sb(f"max{s}", [P, T])
                b.sum = sb(f"sum{s}", [P, T])
                b.rsum = sb(f"rsum{s}", [P, T])
                b.on = sb(f"on{s}", [P, T, NODES])
                b.diag = sb(f"diag{s}", [P, T])
                b.aT = sb(f"aT{s}", [P, T, 2, P])
                b.hw = sb(f"hw{s}", [P, T, 3, FEAT])
            else:
                b.clr = sb(f"clr{s}", [P, T, 2, NODES])
                b.mlr = sb(f"mlr{s}", [P, C, 2, TOK])
                b.w = sb(f"w{s}", [P, T, 2, NODES])
                b.aT = sb(f"aT{s}", [P, T, P])
                b.hw = sb(f"hw{s}", [P, T, FEAT])
            b.ps = g.ps[s]
            b.ps_row = b.ps[:, 0:2, :].rearrange("p a b -> p (a b)")[:, 0:C * TOK].rearrange(
                "p (c t) -> p c t", c=C)
            b.ps_row2 = b.ps[:, 2:4, :].rearrange("p a b -> p (a b)")[:, 0:C * TOK].rearrange(
                "p (c t) -> p c t", c=C)
            b.ps_tiles = b.ps[:, 0, 0:T * P].rearrange("p (t i) -> p t i", t=T)
            if directed:
                b.ps_w = [b.ps[:, 2:4, 0:FEAT], b.ps[:, 1:3, 0:FEAT], b.ps[:, 1:4:2, 0:FEAT]]
            bufs.append(b)

        block = ctx.enter_context(nc.Block())

        @block.sync
        def _(sp):
            def x_free(s, i):
                sp.wait_ge(pool_done[s], PO[s].all(i, ("x", 0), ("adj" if directed else "clr", 0)))
                sp.wait_ge(act_done[s], AC[s]("h", i))

            def x_new(s, i):
                sp.wait_ge(dve_done[s], DV[s]("xout", i))
            if phase == 0:
                sp.dma_start(g.w_raw[:, :STAGED], g.weights[0][:, :STAGED]).then_inc(g.weights_in[0], 16)
                for dst, src in g.const_loads:
                    sp.dma_start(dst, src).then_inc(g.const_in, 16)
            pairs = [(rows[l][k][:], params[l][k]) for l in range(2) for k in range(len(params[l]))]
            move_program(nc, sp, g, phase, 6, pairs, x_out, bufs, sems, x_free, x_new)

        n_rows = sum(len(p) for p in params)

        @block.gpsimd
        def _(pool):
            if phase == 0:
                nc.gpsimd.memset(g.neg_half[:], -0.5).then_inc(g.powers, 1)
                nc.gpsimd.memset(g.ones[:], 1.0).then_inc(g.powers, 1)
                nc.gpsimd.memset(g.pos_half[:], 0.5).then_inc(g.powers, 1)
            pool.wait_ge(g.powers, 3)
            pool.wait_ge(g.const_in, g.const_count)

            def stat(s, i):
                b = bufs[s]
                pool.wait_ge(dve_done[s], DV[s]("var", i))
                nc.gpsimd.tensor_tensor(b.x_rstd[:], b.x_rstd[:], g.neg_half[:, 0:T],
                                        ALU.pow).then_inc(pool_done[s], 1)

            def adj(s, i):
                b = bufs[s]
                pool.wait_ge(sems.adj_in[s], 16 * n_adj * (i + 1))
                if later(i):
                    pool.wait_ge(dve_done[s], DV[s]("att_1", i - 1))
                nc.gpsimd.tensor_tensor(b.adj[:], b.adjin[:, 0], g.ones[:], ALU.mult)\
                    .then_inc(pool_done[s], 1)
                if not directed:
                    for k in range(2):
                        ins = nc.gpsimd.tensor_tensor(b.clr[:, :, k], b.adjin[:, k],
                                                      g.tri[:, k:k + 1].broadcast_to([P, T, NODES]), ALU.mult)
                    ins.then_inc(pool_done[s], 1)

            def x(s, i):
                b = bufs[s]
                if later(i):
                    pool.wait_ge(dve_done[s], DV[s]("xout", i - 1))
                pool.wait_ge(sems.x_in[s], 16 * (i + 1))
                nc.gpsimd.tensor_tensor(g.idle[:, s:s + 1], g.pos_half[:, 0:1], g.pos_half[:, 0:1], ALU.mult)
                nc.gpsimd.tensor_scalar(b.x[:], b.xin[:], 1.0, 0.0, ALU.mult, ALU.add)\
                    .then_inc(pool_done[s], 1)

            def layer(l):
                def w(m):
                    def stage(s, i):
                        b = bufs[s]
                        pool.wait_ge(act_done[s], AC[s](f"w{m}_{l}", i))
                        if first(s, i):
                            pool.wait_ge(sems.params_in, 16 * n_rows)
                        nc.gpsimd.tensor_tensor(b.hw[:, :, m], b.hw[:, :, m],
                                                rows[l][m][:].unsqueeze(1).broadcast_to([P, T, FEAT]),
                                                ALU.add).then_inc(pool_done[s], 1)
                    return stage

                def agg(s, i):
                    b = bufs[s]
                    pool.wait_ge(dve_done[s], DV[s](f"lvar_{l}", i))
                    nc.gpsimd.tensor_tensor(b.rstd[:], b.rstd[:], (g.neg_half if directed else g.pos_half)[:, 0:T],
                                            ALU.pow).then_inc(pool_done[s], 1)
                return {f"agg_{l}": agg, **({f"w0_{l}": w(0), f"w1_{l}": w(1)} if directed else {})}

            run_stages(pool, pool_order, {"stat": stat, "adj": adj, "x": x, **layer(0), **layer(1)})

        @block.scalar
        def _(act):
            weight_split(nc, g, phase, EARLY, act, None)

            def norm(s, i):
                b = bufs[s]
                act.wait_ge(dve_done[s], DV[s]("shift", i))
                if later(i):
                    act.wait_ge(pe_done[s], PE[s]("hT_1", i - 1))
                for t in range(T):
                    ins = nc.scalar.activation(b.h[:, t], b.xin[:, t], ACT.Relu, bias=b.x_shift[:, t:t + 1],
                                               scale=b.x_rstd[:, t:t + 1])
                ins.then_inc(act_done[s], 1)

            def layer(l):
                def hT(s, i):
                    b = bufs[s]
                    used = [("u_1", 1), ("w2_1" if directed else "lin_1", 1)] if l == 0 else []
                    act.wait_ge(pe_done[s], PE[s].all(i, (f"hT_{l}", 0), *used))
                    nc.scalar.activation(b.t_hi[:], b.ps_row, ACT.Copy).then_inc(act_done[s], 1)
                    act.wait_ge(dve_done[s], DV[s](f"hT_lo_{l}", i))
                    nc.scalar.activation(b.hT[:], b.ps_row, ACT.Copy).then_inc(act_done[s], 1)
                    if first(s, i) and l == 0:
                        weight_split(nc, g, phase, range(len(EARLY), 6), act, None)

                def ml(s, i):
                    b = bufs[s]
                    act.wait_ge(pe_done[s], PE[s](f"ml_{l}", i))
                    nc.scalar.activation(b.mlr[:, :, 0], b.ps_row2, ACT.Copy).then_inc(act_done[s], 1)

                def w(m):
                    def stage(s, i):
                        b = bufs[s]
                        act.wait_ge(pe_done[s], PE[s](f"w{m}_{l}", i))
                        if l == 0 and later(i):
                            act.wait_ge(dve_done[s], DV[s]("ctx_1", i - 1))
                        nc.scalar.activation(b.hw[:, :, m], b.ps_w[m], ACT.Copy).then_inc(act_done[s], 1)
                    return stage

                def soft(s, i):
                    b = bufs[s]
                    act.wait_ge(dve_done[s], DV[s](f"diff_{l}" if directed else f"u_{l}", i))
                    nc.scalar.activation(b.e[:], b.e[:], ACT.Exp, scale=1.0 / TEMPER if directed else 1.0)\
                        .then_inc(act_done[s], 1)

                def ln(s, i):
                    b = bufs[s]
                    for t in range(T):
                        act.wait_ge(dve_done[s], DV[s](f"z{t}_{l}", i))
                        nc.scalar.activation(b.h[:, t], b.z[:, t], ACT.Relu).then_inc(act_done[s], 1)

                todo = {f"hT_{l}": hT, f"soft_{l}": soft}
                todo.update({f"w0_{l}": w(0), f"w1_{l}": w(1)} if directed else {f"ml_{l}": ml})
                todo.update({f"ln_{l}": ln} if l == 0 else {})
                return todo

            run_stages(act, act_order, {"norm": norm, **layer(0), **layer(1)})

        @block.vector
        def _(dve):
            for s in range(STREAMS):
                nc.vector.memset(g.mark[:, s:s + 1], 0.0).then_inc(sems.stored[s], 1)
            dve.wait_ge(g.const_in, g.const_count)

            def wait_own(s, name, i):
                dve.wait_ge(dve_done[s], DV[s](name, i))

            def stat(s, i):
                b = bufs[s]
                dve.wait_ge(sems.x_in[s], 16 * (i + 1))
                for t in range(T):
                    ins = nc.vector.bn_stats(b.x_st[:, t], b.xin[:, t])
                ins.then_inc(dve_done[s], 1)
                wait_own(s, "stats", i)
                nc.vector.memset(g.pad[:], 0.0)
                for t in range(T):
                    ins = nc.vector.bn_aggr(b.x_mv[:, t], b.x_st[:, t])
                ins.then_inc(dve_done[s], 1)
                wait_own(s, "aggr", i)
                nc.vector.tensor_scalar(b.x_rstd[:], b.x_mv[:, :, 1], LN_EPS, None, ALU.add)\
                    .then_inc(dve_done[s], 1)
                dve.wait_ge(pool_done[s], PO[s]("rstd", i))
                nc.vector.scalar_tensor_tensor(b.x_shift[:], b.x_mv[:, :, 0], -1.0, b.x_rstd[:], ALU.mult,
                                               ALU.mult).then_inc(dve_done[s], 1)
                if first(s, i):
                    weight_split(nc, g, phase, EARLY, None, dve)

            def layer(l):
                def hT(s, i):
                    b = bufs[s]
                    dve.wait_ge(act_done[s], AC[s](f"hT_hi_{l}", i))
                    nc.vector.tensor_tensor(b.t_lo[:], b.ps_row, b.t_hi[:].bitcast(F32), ALU.subtract)\
                        .then_inc(dve_done[s], 1)
                    if first(s, i) and l == 0:
                        weight_split(nc, g, phase, range(len(EARLY), 6), None, dve)
                        for other in bufs:
                            nc.vector.memset(other.a_bd[:], 0.0).then_inc(sems.start_zero, 1)
                        dve.wait_ge(sems.start_zero, STREAMS)
                        dve.wait_ge(sems.params_in, 16 * n_rows)

                def mr(s, i):
                    b = bufs[s]
                    dve.wait_ge(pe_done[s], PE[s](f"mr_{l}", i))
                    nc.vector.tensor_copy(b.mlr[:, :, 1], b.ps_row).then_inc(dve_done[s], 1)

                def lin(s, i):
                    b = bufs[s]
                    dve.wait_ge(pe_done[s], PE[s](f"lin_{l}", i))
                    nc.vector.tensor_tensor(b.hw[:], b.ps[:, 2:4, 0:FEAT],
                                            rows[l][0][:].unsqueeze(1).broadcast_to([P, T, FEAT]),
                                            ALU.add).then_inc(dve_done[s], 1)

                def w2(s, i):
                    b = bufs[s]
                    dve.wait_ge(pe_done[s], PE[s](f"w2_{l}", i))
                    nc.vector.tensor_tensor(b.hw[:, :, LOWER], b.ps_w[LOWER],
                                            rows[l][LOWER][:].unsqueeze(1).broadcast_to([P, T, FEAT]),
                                            ALU.add).then_inc(dve_done[s], 1)

                def soft(s, i):
                    b = bufs[s]
                    dve.wait_ge(pe_done[s], PE[s](f"u_{l}", i))
                    if directed:
                        own = [(slice(q, q + NODES), b.ps_tiles[q:q + NODES, :, q:q + NODES])
                               for q in (0, NODES)]
                        for at, scores in own:
                            ins = nc.vector.tensor_reduce(b.max[at], scores, AX.X, ALU.max)
                        ins.then_inc(dve_done[s], 1)
                        wait_own(s, f"max_{l}", i)
                        for at, scores in own:
                            ins = nc.vector.tensor_tensor(b.e[at], scores,
                                                          b.max[at].unsqueeze(2).broadcast_to([NODES, T, NODES]),
                                                          ALU.subtract)
                        ins.then_inc(dve_done[s], 1)
                    else:
                        dve.wait_ge(pool_done[s], PO[s]("clr", i))
                        nc.vector.tensor_tensor(
                            b.w[:], b.ps[:, 0, 0:T * P].rearrange("p (t k j) -> p t k j", t=T, k=2),
                            b.clr[:], ALU.mult).then_inc(dve_done[s], 1)
                        wait_own(s, f"w_{l}", i)
                        nc.vector.tensor_tensor(b.e[:], b.w[:, :, 0], b.w[:, :, 1], ALU.add)\
                            .then_inc(dve_done[s], 1)

                def att(s, i):
                    b = bufs[s]
                    dve.wait_ge(act_done[s], AC[s](f"e_{l}", i))
                    if directed:
                        nc.vector.tensor_reduce(b.sum[:], b.e[:], AX.X, ALU.add).then_inc(dve_done[s], 1)
                        wait_own(s, f"sum_{l}", i)
                        nc.vector.reciprocal(b.rsum[:], b.sum[:]).then_inc(dve_done[s], 1)
                        dve.wait_ge(pool_done[s], PO[s]("adj", i))
                        nc.vector.tensor_tensor(b.e[:], b.e[:], b.adj[:], ALU.mult).then_inc(dve_done[s], 1)
                        wait_own(s, f"ea_{l}", i)
                        nc.vector.tensor_tensor(b.e[:], b.e[:],
                                                b.rsum[:].unsqueeze(2).broadcast_to([P, T, NODES]),
                                                ALU.mult).then_inc(dve_done[s], 1)
                        wait_own(s, f"a_{l}", i)
                    else:
                        nc.vector.tensor_tensor(b.e[:], b.e[:], b.adj[:], ALU.mult).then_inc(dve_done[s], 1)
                        wait_own(s, f"ea_{l}", i)
                    nc.vector.tensor_reduce(b.asum[:], b.e[:], AX.X, ALU.add).then_inc(dve_done[s], 1)
                    wait_own(s, f"asum_{l}", i)
                    nc.vector.tensor_scalar(b.asum[:], b.asum[:], 1e-10, None, ALU.add)\
                        .then_inc(dve_done[s], 1)
                    wait_own(s, f"asum_eps_{l}", i)
                    nc.vector.reciprocal(b.rasum[:], b.asum[:]).then_inc(dve_done[s], 1)
                    wait_own(s, f"rasum_{l}", i)
                    for q in (0, NODES):
                        ins = nc.vector.tensor_tensor(
                            b.a_bd[q:q + NODES, :, q:q + NODES], b.e[q:q + NODES],
                            b.rasum[q:q + NODES].unsqueeze(2).broadcast_to([NODES, T, NODES]), ALU.mult)
                    ins.then_inc(dve_done[s], 1)
                    if directed:
                        nc.vector.tensor_tensor(b.on[:], b.e[:],
                                                g.eye[:].unsqueeze(1).broadcast_to([P, T, NODES]),
                                                ALU.mult).then_inc(dve_done[s], 1)
                        wait_own(s, f"on_{l}", i)
                        nc.vector.tensor_reduce(b.diag[:], b.on[:], AX.X, ALU.add).then_inc(dve_done[s], 1)
                        wait_own(s, f"on_sum_{l}", i)
                        nc.vector.tensor_tensor(b.diag[:], b.diag[:], b.rasum[:], ALU.mult)\
                            .then_inc(dve_done[s], 1)

                def aT(s, i):
                    b = bufs[s]
                    dve.wait_ge(pe_done[s], PE[s](f"aT_{l}", i))
                    if directed:
                        nc.vector.tensor_tensor(
                            b.aT[:], b.ps_tiles.unsqueeze(2).broadcast_to([P, T, 2, P]),
                            g.part_cols[:].unsqueeze(1).broadcast_to([P, T, 2, P]),
                            ALU.mult).then_inc(dve_done[s], 1)
                    else:
                        nc.vector.tensor_copy(b.aT[:], b.ps[:, 1, 0:T * P].rearrange("p (t i) -> p t i", t=T))\
                            .then_inc(dve_done[s], 1)

                def agg(s, i):
                    b = bufs[s]
                    dve.wait_ge(pe_done[s], PE[s](f"agg_{l}", i))
                    if directed:
                        wait_own(s, f"diag_{l}", i)
                        dve.wait_ge(pool_done[s], PO[s](f"w1_{l}", i))
                        for t in range(T):
                            ins = nc.vector.scalar_tensor_tensor(
                                b.z[:, t], b.hw[:, t, ON], b.diag[:, t:t + 1], b.ps[:, 2 + t, 0:FEAT],
                                ALU.mult, ALU.add)
                        ins.then_inc(dve_done[s], 1)
                        wait_own(s, f"ctx_{l}", i)
                    got = [b.z[:, t] if directed else b.ps[:, 2 + t, 0:FEAT] for t in range(T)]
                    for t in range(T):
                        ins = nc.vector.bn_stats(b.st[:, t], got[t])
                    ins.then_inc(dve_done[s], 1)
                    wait_own(s, f"lstats_{l}", i)
                    nc.vector.memset(g.pad[:], 0.0)
                    for t in range(T):
                        ins = nc.vector.bn_aggr(b.mv[:, t], b.st[:, t])
                    ins.then_inc(dve_done[s], 1)
                    wait_own(s, f"laggr_{l}", i)
                    if directed:
                        nc.vector.tensor_scalar(b.rstd[:], b.mv[:, :, 1], 1e-12, None, ALU.add)\
                            .then_inc(dve_done[s], 1)
                    else:
                        nc.vector.tensor_scalar(b.rstd[:], b.mv[:, :, 1], FEAT / (FEAT - 1.0), None, ALU.mult)\
                            .then_inc(dve_done[s], 1)
                    for t in range(T):
                        ins = nc.vector.scalar_tensor_tensor(b.z[:, t], got[t], b.mv[:, t, 0:1], rows[l][-2][:],
                                                             ALU.subtract, ALU.mult)
                    ins.then_inc(dve_done[s], 1)

                def ln(s, i):
                    b = bufs[s]
                    dve.wait_ge(pool_done[s], PO[s](f"lstd_{l}", i))
                    if not directed:
                        nc.vector.tensor_scalar(b.rstd[:], b.rstd[:], 1e-3, None, ALU.add)\
                            .then_inc(dve_done[s], 1)
                        wait_own(s, f"lsig_{l}", i)
                        nc.vector.reciprocal(b.rstd[:], b.rstd[:]).then_inc(dve_done[s], 1)
                        wait_own(s, f"lrstd_{l}", i)
                    wait_own(s, f"cen_{l}", i)
                    for t in range(T):
                        nc.vector.scalar_tensor_tensor(b.z[:, t], b.z[:, t], b.rstd[:, t:t + 1], rows[l][-1][:],
                                                       ALU.mult, ALU.add).then_inc(dve_done[s], 1)
                    if l == 1:
                        wait_own(s, "z1_1", i)
                        dve.wait_ge(pool_done[s], PO[s]("x", i))
                        dve.wait_ge(sems.stored[s], 16 * i + 1)
                        nc.vector.scalar_tensor_tensor(b.xout[:], b.z[:], 0.0, b.x[:], ALU.max, ALU.add)\
                            .then_inc(dve_done[s], 1)

                todo = {f"hT_{l}": hT, f"soft_{l}": soft, f"att_{l}": att, f"aT_{l}": aT, f"agg_{l}": agg,
                        f"ln_{l}": ln}
                todo.update({f"w2_{l}": w2} if directed else {f"mr_{l}": mr, f"lin_{l}": lin})
                return todo

            run_stages(dve, dve_order, {"stat": stat, **layer(0), **layer(1)})

        @block.tensor
        def _(pe):
            pe.wait_ge(g.const_in, g.const_count)

            def layer(l):
                def hT(s, i):
                    b = bufs[s]
                    if l == 0:
                        pe.wait_ge(act_done[s], AC[s]("h", i))
                        if later(i):
                            read_out = [("aT_1", 1), ("w2_1", 1)] if directed else [("aT_1", 1)]
                            pe.wait_ge(dve_done[s], DV[s].all(i, *read_out))
                    for t in range(T):
                        if l == 1:
                            pe.wait_ge(act_done[s], AC[s](f"h_next{t}_0", i))
                        for c in range(C):
                            mm = nc.tensor.transpose(b.ps_row[:, c, t * P:(t + 1) * P],
                                                     b.h[:, t, c * P:(c + 1) * P], g.ident[:])
                    mm.then_inc(pe_done[s], 1)

                left_23 = [("ctx_1" if directed else "cen_1", 1)] if l == 0 else []

                def project_T(b, out, m):
                    for o in range(C):
                        mm = exact_product(nc, out[:, o], [
                            (g.w_hi[:, 3 * l + m, c, o * P:(o + 1) * P], g.w_lo[:, 3 * l + m, c, o * P:(o + 1) * P],
                             b.t_hi[:, c], b.t_lo[:, c]) for c in range(C)])
                    return mm

                def project(b, t, bank, m):
                    return exact_product(nc, b.ps[:, bank, 0:FEAT], [
                        (b.t_hi[:, c, t * P:(t + 1) * P], b.t_lo[:, c, t * P:(t + 1) * P],
                         g.w_hi[:, 3 * l + m, c], g.w_lo[:, 3 * l + m, c]) for c in range(C)])

                def ml(s, i):
                    weights_made(pe, g, phase, 3 * l + LEFT, i)
                    pe.wait_ge(dve_done[s], DV[s].all(i, (f"hT_lo_{l}", 0), *left_23))
                    project_T(bufs[s], bufs[s].ps_row2, LEFT).then_inc(pe_done[s], 1)

                def mr(s, i):
                    weights_made(pe, g, phase, 3 * l + RIGHT, i)
                    pe.wait_ge(act_done[s], AC[s](f"hT_{l}", i))
                    project_T(bufs[s], bufs[s].ps_row, RIGHT).then_inc(pe_done[s], 1)

                def lin(s, i):
                    weights_made(pe, g, phase, 3 * l + LIN, i)
                    pe.wait_ge(act_done[s], AC[s](f"ml_{l}", i))
                    for t in range(T):
                        mm = project(bufs[s], t, 2 + t, LIN)
                    mm.then_inc(pe_done[s], 1)

                def w0(s, i):
                    weights_made(pe, g, phase, 3 * l + UPPER, i)
                    pe.wait_ge(dve_done[s], DV[s].all(i, (f"hT_lo_{l}", 0), *left_23))
                    for t in range(T):
                        mm = project(bufs[s], t, 2 + t, UPPER)
                    mm.then_inc(pe_done[s], 1)

                def w1(s, i):
                    weights_made(pe, g, phase, 3 * l + ON, i)
                    pe.wait_ge(act_done[s], AC[s](f"hT_{l}", i))
                    project(bufs[s], 0, 1, ON)
                    pe.wait_ge(act_done[s], AC[s](f"w0_{l}", i))
                    project(bufs[s], 1, 2, ON).then_inc(pe_done[s], 1)

                def w2(s, i):
                    weights_made(pe, g, phase, 3 * l + LOWER, i)
                    project(bufs[s], 1, 3, LOWER)
                    pe.wait_ge(act_done[s], AC[s](f"w1_{l}", i))
                    project(bufs[s], 0, 1, LOWER).then_inc(pe_done[s], 1)

                def u(s, i):
                    b = bufs[s]
                    if directed:
                        pe.wait_ge(act_done[s], AC[s](f"hT_{l}", i))
                        for t in range(T):
                            at = slice(t * P, (t + 1) * P)
                            for c in range(C):
                                mm = nc.tensor.matmul(b.ps_tiles[:, t], b.hT[:, c, at],
                                                      b.hT[:, c, at], start=(c == 0), stop=(c == C - 1))
                        mm.then_inc(pe_done[s], 1)
                        return
                    pe.wait_ge(act_done[s], AC[s].all(i, (f"hT_{l}", 0), (f"ml_{l}", 0)))
                    pe.wait_ge(dve_done[s], DV[s](f"mr_{l}", i))
                    for t in range(T):
                        for gr in range(2):
                            at = t * P + gr * NODES
                            for c in range(C):
                                mm = nc.tensor.matmul(
                                    b.ps[gr * NODES:(gr + 1) * NODES, 0, t * P:(t + 1) * P],
                                    b.hT[:, c, at:at + NODES], b.mlr[:, c, :, at:at + NODES],
                                    start=(c == 0), stop=(c == C - 1))
                    mm.then_inc(pe_done[s], 1)

                def aT(s, i):
                    b = bufs[s]
                    pe.wait_ge(dve_done[s], DV[s](f"att_{l}", i))
                    for t in range(T):
                        out = b.ps[:, 0 if directed else 1, t * P:(t + 1) * P]
                        mm = nc.tensor.transpose(out, b.a_bd[:, t], g.ident[:])
                    mm.then_inc(pe_done[s], 1)

                def agg(s, i):
                    b = bufs[s]
                    pe.wait_ge(dve_done[s], DV[s].all(i, (f"aT_{l}", 0), (f"w2_{l}" if directed else f"lin_{l}", 0)))
                    if directed:
                        pe.wait_ge(pool_done[s], PO[s](f"w0_{l}", i))
                        for t in range(T):
                            for k, m in enumerate((UPPER, LOWER)):
                                mm = nc.tensor.matmul(b.ps[:, 2 + t, 0:FEAT], b.aT[:, t, k], b.hw[:, t, m],
                                                      start=(k == 0), stop=(k == 1))
                    else:
                        for t in range(T):
                            mm = nc.tensor.matmul(b.ps[:, 2 + t, 0:FEAT], b.aT[:, t], b.hw[:, t],
                                                  start=True, stop=True)
                    mm.then_inc(pe_done[s], 1)

                both = {f"hT_{l}": hT, f"u_{l}": u, f"aT_{l}": aT, f"agg_{l}": agg}
                if directed:
                    return {**both, f"w0_{l}": w0, f"w1_{l}": w1, f"w2_{l}": w2}
                return {**both, f"ml_{l}": ml, f"mr_{l}": mr, f"lin_{l}": lin}

            run_stages(pe, pe_order, {**layer(0), **layer(1)})


def graph_stack(nc, x, adj, adj_t, w0, w1, w2, w3, rows0, rows1, rows2, rows3, ident, tri, eye,
                part_cols, out):
    with ExitStack() as ctx:
        def sb(name, shape, dt=F32):
            return ctx.enter_context(nc.sbuf_tensor(name, shape, dt))

        def sem(name):
            return ctx.enter_context(nc.semaphore(name))
        g = Shared()
        g.ident = sb("ident", [P, P])
        g.tri = sb("tri", [P, 2, NODES])
        g.eye = sb("eye", [P, NODES])
        g.part_cols = sb("part_cols", [P, 2, P])
        g.neg_half = sb("neg_half", [P, T])
        g.pos_half = sb("pos_half", [P, T])
        g.ones = sb("ones", [P, T, NODES])
        g.mark = sb("mark", [P, STREAMS])
        g.idle = sb("idle", [P, STREAMS])
        g.pad = sb("pad", [P, 1])
        g.w_hi = sb("w_hi", [P, MATS, C, FEAT], F32R)
        g.w_lo = sb("w_lo", [P, MATS, C, FEAT], F32R)
        g.w_raw = sb("w_raw", [P, MATS, C, FEAT])
        g.ps = [ctx.enter_context(nc.psum_tensor(f"ps{s}", [P, 4, BANK], F32)) for s in range(STREAMS)]
        g.weights = [w.rearrange("m (c p) o -> p m c o", p=P) for w in (w0, w1, w2, w3)]
        g.xin = [sb(f"xin{s}", [P, T, FEAT]) for s in range(STREAMS)]
        g.adjin = [sb(f"adjin{s}", [P, 2, T, NODES]) for s in range(STREAMS)]
        g.x_in = [[sem(f"x_in{s}_{k}") for s in range(STREAMS)] for k in range(4)]
        g.adj_in = [[sem(f"adj_in{s}_{k}") for s in range(STREAMS)] for k in range(4)]
        g.weights_in = [sem(f"weights_in{k}") for k in range(4)]
        g.more_weights_in = [sem(f"more_weights_in{k}") for k in range(4)]
        g.hi_split = [sem(f"hi_split{k}") for k in range(4)]
        g.lo_split = [sem(f"lo_split{k}") for k in range(4)]
        g.powers = sem("powers")
        g.const_in = sem("const_in")
        g.const_loads = [(g.ident[:], ident), (g.tri[:], tri), (g.eye[:], eye),
                         (g.part_cols[:], part_cols)]
        g.const_count = 16 * len(g.const_loads)

        def groups(a):
            return a.rearrange("b s f -> (b s) f").rearrange("(n t p) f -> n p t f", t=T, p=P)
        between = [nc.dram_tensor(f"x_after_{k}", (GRAPHS, NODES, FEAT), F32, kind="Internal").ap()
                   for k in range(3)]
        xs = [groups(a) for a in [x] + between + [out]]
        a_n, a_t = groups(adj), groups(adj_t)
        g.sources = [(xs[0], [a_n, a_t])] + [(xs[k], [a_n]) for k in (1, 2, 3)]
        gcn_phase(nc, g, 0, False, xs[1], [[r[l] for r in rows0] for l in range(2)])
        attention_phase(nc, g, 1, 2, xs[2], *rows1)
        attention_phase(nc, g, 2, 1, xs[3], *rows2)
        gcn_phase(nc, g, 3, True, xs[4], [[r[l] for r in rows3] for l in range(2)])


def kernel(**inputs):
    import concourse.bacc as bacc
    from concourse.bass_utils import run_bass_kernel_spmd

    def f(name):
        return np.asarray(inputs[name])

    def transposed(names, layers=None):
        if layers is None:
            return np.ascontiguousarray(np.stack([f(n).T for n in names]))
        return np.ascontiguousarray(np.stack([f(n)[l].T for l in range(layers) for n in names]))

    i, j = np.arange(NODES)[:, None], np.arange(NODES)[None, :]
    above, on, below = (j > i), (j == i), (j < i)
    tri = np.stack([above | on, below]).astype(np.float32) / np.float32(np.sqrt(FEAT))
    blocks = np.zeros((P, 2, P), np.float32)
    for k in range(P // NODES):
        at = slice(k * NODES, (k + 1) * NODES)
        blocks[at, :, at] = np.stack([above, below]).astype(np.float32).transpose(2, 0, 1)
    arrays = {
        "x": np.ascontiguousarray(f("x")),
        "adj": np.ascontiguousarray(f("adj")),
        "adj_t": np.ascontiguousarray(f("adj").transpose(0, 2, 1)),
        "w0": transposed(["L0_gnn_W_left", "L0_gnn_W_right", "L0_gnn_W_lin"], 2),
        "w1": transposed([f"L1_gnn_W{c}" for c in "qkvo"]),
        "w2": transposed([f"L2_gnn_W{c}" for c in "qkvo"]),
        "w3": transposed(["L3_gnn_Wl", "L3_gnn_Ws", "L3_gnn_Wr"], 2),
        "ident": np.eye(P, dtype=np.float32),
        "tri": np.ascontiguousarray(np.tile(tri.transpose(1, 0, 2), (P // NODES, 1, 1))),
        "eye": np.ascontiguousarray(np.tile(on.astype(np.float32), (P // NODES, 1))),
        "part_cols": blocks,
    }
    rows = [["L0_gnn_b_lin", "L0_gnn_ln_a", "L0_gnn_ln_b"], ["L1_gnn_bv", "L1_gnn_bo"],
            ["L2_gnn_bv", "L2_gnn_bo"], ["L3_gnn_bl", "L3_gnn_bs", "L3_gnn_br", "L3_gnn_ln_w", "L3_gnn_ln_b"]]
    for names in rows:
        for name in names:
            arrays[name] = np.ascontiguousarray(f(name))

    nc = bacc.Bacc("TRN2", target_bir_lowering=False, num_devices=1)
    at = {name: nc.dram_tensor(f"in_{name}", a.shape, mybir.dt.from_np(a.dtype), kind="ExternalInput").ap()
          for name, a in arrays.items()}
    out = nc.dram_tensor("out", (GRAPHS, NODES, FEAT), F32, kind="ExternalOutput").ap()
    graph_stack(nc, at["x"], at["adj"], at["adj_t"], at["w0"], at["w1"], at["w2"], at["w3"],
                *[[at[name] for name in names] for names in rows],
                at["ident"], at["tri"], at["eye"], at["part_cols"], out)
    got = run_bass_kernel_spmd(nc, [{f"in_{name}": a for name, a in arrays.items()}], core_ids=[0])
    return got.results[0]["out"]
```
